# Optimizing a Trainium2 kernel written in Bass

```python
import numpy as np
import jax
import jax.numpy as jnp

def _softmax(x, axis=-1):
    return jax.nn.softmax(x, axis=axis)

def _gelu(x):
    return jax.nn.gelu(x, approximate=True)

def _silu(x):
    return jax.nn.silu(x)

def _sigmoid(x):
    return jax.nn.sigmoid(x)

def _layernorm(x, axis=-1, eps=1e-05):
    m = jnp.mean(x, axis=axis, keepdims=True)
    v = jnp.var(x, axis=axis, keepdims=True)
    return (x - m) / jnp.sqrt(v + eps)

def _scatter_add(tgt, idx, src, axis=0):
    return tgt.at[idx].add(src)

def _segment_sum(src, seg, n):
    return jax.ops.segment_sum(src, seg, n)
kernel_name = 'mk_flamingo_gated_d2_seqx_r8_999826'

def setup_inputs(seed: int=0):
    np.random.seed(seed)
    _w = jnp.asarray

    def _rec_inputs():
        import jax
        import jax.numpy as jnp
        _rk = jax.random.key(seed)
        x = -0.0002928 + 1 * jax.random.normal(jax.random.fold_in(_rk, 1), (8, 256, 128), jnp.float32)
        _lenS = 256 - jax.random.randint(jax.random.fold_in(_rk, 7), (8,), 0, max(1, 256 // 4) + 1, jnp.int32)
        _lenS2 = 256 - jax.random.randint(jax.random.fold_in(_rk, 8), (8,), 0, max(1, 256 // 4) + 1, jnp.int32)
        _ctx_1024P = jax.random.normal(jax.random.fold_in(_rk, 11), (8, 16, 128), jnp.float32)
        _ctx_1024c = jax.random.dirichlet(jax.random.fold_in(_rk, 511), 0.3 * jnp.ones((16,), jnp.float32), (8, 256))
        _ctx_1024t = jnp.einsum('bsk,bkd->bsd', _ctx_1024c, _ctx_1024P)
        _ctx_1024t = _ctx_1024t * jax.lax.rsqrt(jnp.mean(jnp.square(_ctx_1024t)) + 1e-12) * 0.953939
        ctx_1024 = -1.39393e-06 + 0.999914 * (_ctx_1024t + 0.3 * jax.random.normal(jax.random.fold_in(_rk, 611), (8, 256, 128), jnp.float32))
        _validS = jnp.arange(256)[None, :] < _lenS[:, None]
        _validS2 = jnp.arange(256)[None, :] < _lenS2[:, None]
        _causal = jnp.tril(jnp.ones((256, 256), dtype=bool))
        mask_BxS2_bf0 = jnp.logical_not(jnp.ones((8, 256), dtype=bool))
        _g = jax.random.normal(jax.random.fold_in(_rk, 9001), (2, 2), jnp.float32)
        _g = jnp.sign(_g) * jnp.maximum(jnp.abs(_g), 1.0) + (_g == 0) * 1.0
        g_xattn = _g[0]
        g_ffn = _g[1]
        return (x, ctx_1024, mask_BxS2_bf0, g_xattn, g_ffn)
    x, ctx_1024, mask_BxS2_bf0, g_xattn, g_ffn = _rec_inputs()

    def _L0_xattn_setup():
        import jax, jax.numpy as jnp
        import numpy as np
        DIM = 128
        HEADS = 16
        DIM_HEAD = 64
        INNER = HEADS * DIM_HEAD
        B, N = (2, 256)
        SCALE = DIM_HEAD ** (-0.5)
        key = jax.random.key(seed)
        ks = jax.random.split(key, 9)
        s_in = 1.0 / np.sqrt(DIM)
        s_inner = 1.0 / np.sqrt(INNER)
        return {'q': jax.random.normal(ks[0], (B, N, DIM), jnp.float32), 'k': jax.random.normal(ks[1], (B, N, DIM), jnp.float32), 'v': jax.random.normal(ks[2], (B, N, DIM), jnp.float32), 'Wq': jax.random.normal(ks[3], (DIM, INNER), jnp.float32) * s_in, 'Wk': jax.random.normal(ks[4], (DIM, INNER), jnp.float32) * s_in, 'Wv': jax.random.normal(ks[5], (DIM, INNER), jnp.float32) * s_in, 'Wo': jax.random.normal(ks[6], (INNER, DIM), jnp.float32) * s_inner, 'bo': jax.random.normal(ks[7], (DIM,), jnp.float32) * s_inner, 'mask': jnp.zeros((B, N), dtype=bool)}
    _L0_xattn_all = _L0_xattn_setup()
    _L0_xattn_in = {k: v for k, v in _L0_xattn_all.items() if k in ('Wq', 'Wk', 'Wv', 'Wo', 'bo')}
    del _L0_xattn_all

    def _L0_ffn_setup():
        import jax, jax.numpy as jnp
        import numpy as np
        D = 128
        H = 256
        E = 8
        K = 2
        B, T = (4, 256)
        key = jax.random.key(seed)
        ks = jax.random.split(key, 7)
        s = 0.02
        return {'x': jax.random.normal(ks[0], (B, T, D), dtype=jnp.float32), 'W1': jax.random.normal(ks[1], (E, D, 2 * H), dtype=jnp.float32) * s, 'b1': jnp.zeros((E, 2 * H), dtype=jnp.float32), 'W2': jax.random.normal(ks[2], (E, H, D), dtype=jnp.float32) * s, 'b2': jnp.zeros((E, D), dtype=jnp.float32), 'Wr': jax.random.normal(ks[3], (D, E), dtype=jnp.float32) * s, 'br': jnp.zeros((E,), dtype=jnp.float32)}
    _L0_ffn_all = _L0_ffn_setup()
    _L0_ffn_in = {k: v for k, v in _L0_ffn_all.items() if k in ('W1', 'b1', 'W2', 'b2', 'Wr', 'br')}
    del _L0_ffn_all

    def _L1_xattn_setup():
        import jax, jax.numpy as jnp
        import numpy as np
        B, S, D, DFF = (4, 256, 128, 512)
        EPS = 1e-05

        def layernorm(x, gamma, beta):
            mu = jnp.mean(x, axis=-1, keepdims=True)
            var = jnp.var(x, axis=-1, keepdims=True)
            return (x - mu) * jax.lax.rsqrt(var + EPS) * gamma + beta

        def attention(Q, K, V, causal):
            d_k = Q.shape[-1]
            scores = jnp.einsum('bqd,bkd->bqk', Q, K) / jnp.sqrt(jnp.asarray(d_k, Q.dtype))
            if causal:
                q_len, k_len = (scores.shape[-2], scores.shape[-1])
                mask = jnp.tril(jnp.ones((q_len, k_len), dtype=bool))
                scores = jnp.where(mask[None], scores, jnp.asarray(-jnp.inf, scores.dtype))
            w = jax.nn.softmax(scores, axis=-1)
            return jnp.einsum('bqk,bkd->bqd', w, V)
        key = jax.random.key(seed)
        ks = jax.random.split(key, 12)
        sd = 0.02
        return {'y': jax.random.normal(ks[0], (B, S, D), jnp.float32), 'Z': jax.random.normal(ks[1], (B, S, D), jnp.float32), 'w1': jax.random.normal(ks[2], (D, DFF), jnp.float32) * sd, 'b1': jnp.zeros((DFF,), jnp.float32), 'w2': jax.random.normal(ks[3], (DFF, D), jnp.float32) * sd, 'b2': jnp.zeros((D,), jnp.float32), 'g1': jnp.ones((D,), jnp.float32), 'beta1': jnp.zeros((D,), jnp.float32), 'g2': jnp.ones((D,), jnp.float32), 'beta2': jnp.zeros((D,), jnp.float32), 'g3': jnp.ones((D,), jnp.float32), 'beta3': jnp.zeros((D,), jnp.float32)}
    _L1_xattn_all = _L1_xattn_setup()
    _L1_xattn_in = {k: v for k, v in _L1_xattn_all.items() if k in ('w1', 'b1', 'w2', 'b2', 'g1', 'beta1', 'g2', 'beta2', 'g3', 'beta3')}
    del _L1_xattn_all

    def _L1_ffn_setup():
        import jax, jax.numpy as jnp
        import numpy as np
        B, S, D = (2, 256, 128)
        E, F, TOP_K = (8, 256, 2)
        key = jax.random.key(seed)
        ks = jax.random.split(key, 5)
        scale = 0.02
        return {'x': jax.random.normal(ks[0], (B, S, D), dtype=jnp.float32), 'gate_w': jax.random.normal(ks[1], (E, D), dtype=jnp.float32) * scale, 'w_gate': jax.random.normal(ks[2], (E, D, F), dtype=jnp.float32) * scale, 'w_up': jax.random.normal(ks[3], (E, D, F), dtype=jnp.float32) * scale, 'w_down': jax.random.normal(ks[4], (E, F, D), dtype=jnp.float32) * scale}
    _L1_ffn_all = _L1_ffn_setup()
    _L1_ffn_in = {k: v for k, v in _L1_ffn_all.items() if k in ('gate_w', 'w_gate', 'w_up', 'w_down')}
    del _L1_ffn_all
    return {'x': x, 'ctx_1024': ctx_1024, 'mask_BxS2_bf0': mask_BxS2_bf0, 'g_xattn': g_xattn, 'g_ffn': g_ffn, 'L0_xattn_Wq': _L0_xattn_in['Wq'], 'L0_xattn_Wk': _L0_xattn_in['Wk'], 'L0_xattn_Wv': _L0_xattn_in['Wv'], 'L0_xattn_Wo': _L0_xattn_in['Wo'], 'L0_xattn_bo': _L0_xattn_in['bo'], 'L0_ffn_W1': _L0_ffn_in['W1'], 'L0_ffn_b1': _L0_ffn_in['b1'], 'L0_ffn_W2': _L0_ffn_in['W2'], 'L0_ffn_b2': _L0_ffn_in['b2'], 'L0_ffn_Wr': _L0_ffn_in['Wr'], 'L0_ffn_br': _L0_ffn_in['br'], 'L1_xattn_w1': _L1_xattn_in['w1'], 'L1_xattn_b1': _L1_xattn_in['b1'], 'L1_xattn_w2': _L1_xattn_in['w2'], 'L1_xattn_b2': _L1_xattn_in['b2'], 'L1_xattn_g1': _L1_xattn_in['g1'], 'L1_xattn_beta1': _L1_xattn_in['beta1'], 'L1_xattn_g2': _L1_xattn_in['g2'], 'L1_xattn_beta2': _L1_xattn_in['beta2'], 'L1_xattn_g3': _L1_xattn_in['g3'], 'L1_xattn_beta3': _L1_xattn_in['beta3'], 'L1_ffn_gate_w': _L1_ffn_in['gate_w'], 'L1_ffn_w_gate': _L1_ffn_in['w_gate'], 'L1_ffn_w_up': _L1_ffn_in['w_up'], 'L1_ffn_w_down': _L1_ffn_in['w_down']}

def reference(x, ctx_1024, mask_BxS2_bf0, g_xattn, g_ffn, L0_xattn_Wq, L0_xattn_Wk, L0_xattn_Wv, L0_xattn_Wo, L0_xattn_bo, L0_ffn_W1, L0_ffn_b1, L0_ffn_W2, L0_ffn_b2, L0_ffn_Wr, L0_ffn_br, L1_xattn_w1, L1_xattn_b1, L1_xattn_w2, L1_xattn_b2, L1_xattn_g1, L1_xattn_beta1, L1_xattn_g2, L1_xattn_beta2, L1_xattn_g3, L1_xattn_beta3, L1_ffn_gate_w, L1_ffn_w_gate, L1_ffn_w_up, L1_ffn_w_down):
    import jax
    import jax.numpy as jnp

    def _L0_xattn_ref(q, k, v, Wq, Wk, Wv, Wo, bo, mask):
        import jax, jax.numpy as jnp
        import numpy as np
        DIM = 128
        HEADS = 16
        DIM_HEAD = 64
        INNER = HEADS * DIM_HEAD
        B, N = (2, 256)
        SCALE = DIM_HEAD ** (-0.5)
        b, n, _ = q.shape
        h, d = (HEADS, DIM_HEAD)

        def split_heads(x):
            return x.reshape(b, n, h, d).transpose(0, 2, 1, 3)
        qh = split_heads(q @ Wq)
        kh = split_heads(k @ Wk)
        vh = split_heads(v @ Wv)
        dots = jnp.einsum('bhid,bhjd->bhij', qh, kh) * SCALE
        mask_value = -jnp.finfo(dots.dtype).max
        dots = jnp.where(mask[:, None, None, :], mask_value, dots)
        causal = jnp.triu(jnp.ones((n, n), dtype=bool), k=1)
        dots = jnp.where(causal[None, None, :, :], mask_value, dots)
        attn = jax.nn.softmax(dots, axis=-1)
        out = jnp.einsum('bhij,bhjd->bhid', attn, vh)
        out = out.transpose(0, 2, 1, 3).reshape(b, n, h * d)
        return out @ Wo + bo

    def _L0_ffn_ref(x, W1, b1, W2, b2, Wr, br):
        import jax, jax.numpy as jnp
        import numpy as np
        D = 128
        H = 256
        E = 8
        K = 2
        B, T = (4, 256)
        Bb, Tt, Dd = x.shape
        xf = x.reshape(-1, Dd)
        logits = xf @ Wr + br
        topk_val, topk_idx = jax.lax.top_k(logits, K)
        scores = jax.nn.softmax(topk_val, axis=-1)
        h = jnp.einsum('nd,edh->enh', xf, W1) + b1[:, None, :]
        a, g = jnp.split(h, 2, axis=-1)
        act = jax.nn.silu(a) * g
        out_e = jnp.einsum('enh,ehd->end', act, W2) + b2[:, None, :]
        out_ne = out_e.transpose(1, 0, 2)
        gathered = jnp.take_along_axis(out_ne, topk_idx[:, :, None], axis=1)
        out = jnp.sum(gathered * scores[:, :, None], axis=1)
        return out.reshape(Bb, Tt, Dd)

    def _L1_xattn_ref(y, Z, w1, b1, w2, b2, g1, beta1, g2, beta2, g3, beta3):
        import jax, jax.numpy as jnp
        import numpy as np
        B, S, D, DFF = (4, 256, 128, 512)
        EPS = 1e-05

        def layernorm(x, gamma, beta):
            mu = jnp.mean(x, axis=-1, keepdims=True)
            var = jnp.var(x, axis=-1, keepdims=True)
            return (x - mu) * jax.lax.rsqrt(var + EPS) * gamma + beta

        def attention(Q, K, V, causal):
            d_k = Q.shape[-1]
            scores = jnp.einsum('bqd,bkd->bqk', Q, K) / jnp.sqrt(jnp.asarray(d_k, Q.dtype))
            if causal:
                q_len, k_len = (scores.shape[-2], scores.shape[-1])
                mask = jnp.tril(jnp.ones((q_len, k_len), dtype=bool))
                scores = jnp.where(mask[None], scores, jnp.asarray(-jnp.inf, scores.dtype))
            w = jax.nn.softmax(scores, axis=-1)
            return jnp.einsum('bqk,bkd->bqd', w, V)
        sa = attention(y, y, y, causal=True)
        y = layernorm(y + sa, g1, beta1)
        ca = attention(y, Z, Z, causal=False)
        y = layernorm(y + ca, g2, beta2)
        h = jax.nn.relu(jnp.einsum('bsd,df->bsf', y, w1) + b1)
        ff = jnp.einsum('bsf,fd->bsd', h, w2) + b2
        y = layernorm(y + ff, g3, beta3)
        return y

    def _L1_ffn_ref(x, gate_w, w_gate, w_up, w_down):
        import jax, jax.numpy as jnp
        import numpy as np
        B, S, D = (2, 256, 128)
        E, F, TOP_K = (8, 256, 2)
        b, s, d = x.shape
        xt = x.reshape(-1, d)
        T = xt.shape[0]
        logits = xt @ gate_w.T
        top_v, top_i = jax.lax.top_k(logits, TOP_K)
        top_w = jax.nn.softmax(top_v, axis=-1)
        w_dense = jnp.zeros_like(logits).at[jnp.arange(T)[:, None], top_i].add(top_w)
        g = jnp.einsum('td,edf->tef', xt, w_gate)
        u = jnp.einsum('td,edf->tef', xt, w_up)
        h = jax.nn.silu(g) * u
        y = jnp.einsum('tef,efd,te->td', h, w_down, w_dense)
        return y.reshape(b, s, d)
    x = x + jnp.tanh(g_xattn[0]) * _L0_xattn_ref(_layernorm(x, axis=-1), ctx_1024, ctx_1024, L0_xattn_Wq, L0_xattn_Wk, L0_xattn_Wv, L0_xattn_Wo, L0_xattn_bo, mask_BxS2_bf0)
    x = x + jnp.tanh(g_ffn[0]) * _L0_ffn_ref(_layernorm(x, axis=-1), L0_ffn_W1, L0_ffn_b1, L0_ffn_W2, L0_ffn_b2, L0_ffn_Wr, L0_ffn_br)
    x = x + jnp.tanh(g_xattn[1]) * _L1_xattn_ref(_layernorm(x, axis=-1), ctx_1024, L1_xattn_w1, L1_xattn_b1, L1_xattn_w2, L1_xattn_b2, L1_xattn_g1, L1_xattn_beta1, L1_xattn_g2, L1_xattn_beta2, L1_xattn_g3, L1_xattn_beta3)
    x = x + jnp.tanh(g_ffn[1]) * _L1_ffn_ref(_layernorm(x, axis=-1), L1_ffn_gate_w, L1_ffn_w_gate, L1_ffn_w_up, L1_ffn_w_down)
    return x

_drawn_inputs = setup_inputs


def setup_inputs(seed=0):
    import zlib

    import numpy as np

    out = dict(_drawn_inputs(seed))
    spreads = {'g_ffn': (-1.0, 0.6),
     'L0_ffn_b1': (0.0, 0.8),
     'L0_ffn_b2': (0.0, 0.1),
     'L0_ffn_br': (0.0, 0.1),
     'L1_xattn_b1': (0.0, 0.1),
     'L1_xattn_b2': (0.0, 0.1),
     'L1_xattn_g1': (1.0, 0.2),
     'L1_xattn_beta1': (0.0, 0.1),
     'L1_xattn_g2': (1.0, 0.2),
     'L1_xattn_beta2': (0.0, 0.1),
     'L1_xattn_g3': (1.0, 0.2),
     'L1_xattn_beta3': (0.0, 0.1)}
    factors = {'L0_xattn_bo': 3.42,
     'L0_ffn_W1': 8.0,
     'L0_ffn_W2': 8.0,
     'L1_ffn_gate_w': 8.0,
     'L1_ffn_w_gate': 7.249,
     'L1_ffn_w_up': 7.284,
     'L1_ffn_w_down': 7.191}
    for name, (base, spread) in spreads.items():
        noise = np.random.default_rng([zlib.crc32(name.encode()), seed]).standard_normal(out[name].shape)
        drawn = base * np.exp(spread * noise) if base else spread * noise
        out[name] = jnp.asarray(drawn.astype(out[name].dtype))
    for name, factor in factors.items():
        out[name] = (out[name] * factor).astype(out[name].dtype)
    return out
```

```python
import concourse.bass as bass
from concourse import mybir
from contextlib import ExitStack

f32 = mybir.dt.float32
f32r = mybir.dt.float32r
u8 = mybir.dt.uint8
ALU = mybir.AluOpType
ACT = mybir.ActivationFunctionType
AX = mybir.AxisListType

B, N, D = 8, 256, 128
HEADS, DH = 16, 64
PAIRS = HEADS // 2
INNER = HEADS * DH
E, H = 8, 256
DFF = 512
T = 128
QB = N // T
TILES = B * QB
CH = 4
CHUNKS = TILES // CH
W = CH * T
U = 4
ONE = 1
EPS = 1e-5
BIG = 1e30
HUGE = 3e38


def ds(start, size):
    return bass.ds(start, size)


def at_least(eng, sem, value):
    if isinstance(value, int) and value <= 0:
        return
    eng.wait_ge(sem, value)


def waits_alone(eng, const, *waits):
    held = [(sem, value if isinstance(value, int) else eng.to_reg(value)) for sem, value in waits]
    eng.wait_ge(const, 1)
    for sem, value in held:
        at_least(eng, sem, value)


def build(nc, x, ctx_in, mask, g_xattn, g_ffn, Wq, Wk, Wv, Wo, bo, m0_W1, m0_b1, m0_W2, m0_b2, m0_Wr, m0_br,
          w1, b1, w2, b2, g1, beta1, g2, beta2, g3, beta3, m1_gate, m1_wg, m1_wu, m1_wd, out):
    stack = ExitStack()
    with stack:
        def sb(name, shape, dt=f32):
            return stack.enter_context(nc.sbuf_tensor(name, shape, dt))

        def sem(name):
            return stack.enter_context(nc.semaphore(name))

        P = [stack.enter_context(nc.psum_tensor(f"bank{i}", [128, 512], f32)) for i in range(8)]

        X = sb("X", [128, TILES * D])
        MV = sb("MV", [128, TILES, 2])
        RSTD = sb("RSTD", [128, TILES])
        HALF = sb("HALF", [128, TILES])
        STAT = sb("STAT", [128, 8 * 6])
        AGGR = sb("AGGR", [128, 8, 2])
        ident = sb("ident", [128, 128])
        TRI = sb("TRI", [128, 3 * T])
        ZERO = sb("ZERO", [128, N])
        GATE = sb("GATE", [128, 4])
        BC = sb("BC", [128, 8, D])
        ROWS = sb("ROWS", [128, 128])
        COLS = sb("COLS", [128, 128])
        RAW = sb("RAW", [128, 3 * INNER])
        WT = sb("WT", [128, 3 * INNER])
        GHI = sb("GHI", [128, HEADS * D], f32r)
        GLO = sb("GLO", [128, HEADS * D], f32r)
        WVHI = sb("WVHI", [128, INNER], f32r)
        WVLO = sb("WVLO", [128, INNER], f32r)
        WOS = sb("WOS", [128, PAIRS, D])
        WVO = sb("WVO", [128, D])
        MASK = sb("MASK", [128, B * N], u8)
        MB = sb("MB", [128, 3 * T])
        XN = sb("XN", [128, N])
        CS = sb("CS", [128, QB, D])
        XCHI = sb("XCHI", [128, 2 * N], f32r)
        XCLO = sb("XCLO", [128, 2 * N], f32r)
        CBAR = sb("CBAR", [128, 1])
        CBARB = sb("CBARB", [128, 128])
        KHI = [sb(f"KHI{i}", [128, 2 * N], f32r) for i in range(2)]
        KLO = [sb(f"KLO{i}", [128, 2 * N], f32r) for i in range(2)]
        ARENA = sb("ARENA", [128, 6144])
        VB = ARENA[:, 0:2048].rearrange("p (q c) -> p q c", q=QB)
        SP = [ARENA[:, 2048 + 768 * i:2816 + 768 * i] for i in range(2)]
        NEGM = [sb(f"NEGM{i}", [128, 4]) for i in range(2)]
        RSUM = [sb(f"RSUM{i}", [128, 4]) for i in range(2)]
        RCP = [sb(f"RCP{i}", [128, 4]) for i in range(2)]
        PT = [ARENA[:, 3584 + 384 * i:3968 + 384 * i] for i in range(2)]
        OT = ARENA[:, 4352:4608]
        TGBO = sb("TGBO", [128, D])
        FCOL = sb("FCOL", [128, 2])
        GCOL = sb("GCOL", [128, 2])
        XTHI = sb("XTHI", [128, TILES * T], f32r)
        XTLO = sb("XTLO", [128, TILES * T], f32r)
        W1RAW = sb("W1RAW", [128, 2 * H])
        W1HI = sb("W1HI", [128, E * 2 * H], f32r)
        W1LO = sb("W1LO", [128, E * 2 * H], f32r)
        W2S = [sb(f"W2S{m}", [128, E * 2 * D]) for m in range(2)]
        B2S = sb("B2S", [E, D])
        WRF = sb("WRF", [128, 2 * 128])
        WRHI = sb("WRHI", [128, 2 * 128], f32r)
        WRLO = sb("WRLO", [128, 2 * 128], f32r)
        BRB = sb("BRB", [128, E])
        HT = [ARENA[:, 1024 * k:1024 * (k + 1)].rearrange("p (j t) -> p j t", j=2) for k in range(2)]
        SIL = [ARENA[:, 2048 + W * j:2048 + W * (j + 1)] for j in range(2)]
        ACC = ARENA[:, 3072:3584]
        XNS = [ARENA[:, 3584 + W * k:3584 + W * (k + 1)] for k in range(2)]
        LTS = [ARENA[:, 4608 + W * k:4608 + W * (k + 1)] for k in range(2)]
        LG = sb("LG", [128, TILES * E])
        RANK = sb("RANK", [128, TILES, E])
        RT = [sb(f"RT{k}", [128, TILES, E]) for k in range(4)]
        RV = [sb(f"RV{k}", [128, TILES]) for k in range(6)]
        WGT = sb("WGT", [128, TILES * E])
        WSL = sb("WSL", [128, CH * E])
        WTS = sb("WTS", [E, W])
        L1W1 = sb("L1W1", [128, DFF])
        L1W2 = sb("L1W2", [128, DFF // 128, D])
        UP = ARENA[:, 0:2048]
        YS = ARENA[:, 2048:3072]
        CU = ARENA[:, 3072:4096].rearrange("p (u q d) -> p u q d", u=U, q=QB)
        YR = ARENA[:, 4096:6144]
        UNEG = sb("UNEG", [128, U * QB])
        USUM = sb("USUM", [128, U * QB])
        URCP = sb("URCP", [128, U * QB])
        YT = RAW[:, 0:U * 512]
        UPT = WT[:, 0:U * 512]
        HL = WT

        block = stack.enter_context(nc.Block())
        S = {}

        def s(name):
            if name not in S:
                S[name] = sem(name)
            return S[name]

        TICK = sb("TICK", [128, 32])
        COUNTED = ["stat_done", "aggr_done", "mv_done", "dav_ready", "dres_done", "dfin", "dff_ready", "w1lo_split1"]
        COUNTED += [f"m{m}_{name}" for m in range(2)
                    for name in ("xt_ready", "xtlo_done", "lt_done", "lg_done", "chunk_done", "acc_chain")]

        def open_counts(eng):
            for k, name in enumerate(COUNTED):
                eng.memset(TICK[:, k:k + 1], 0.0).then_inc(s(name), ONE)

        for name in ("x_loaded proj_loaded wo_loaded rows_loaded bcast_loaded mask_loaded gates_loaded wr_loaded "
                     "w2_loaded l1w_loaded out_stored pool_const ident_ready rows_zero wrf_zero "
                     "stat_done aggr_done mv_done veps_ready rstd_ready gate_ready cbar_sum "
                     "wt_ready wt_act wt_dve cols_ready cols_done g_ready ghi_done glo_done wvo_ready wvo_done wr_split wr_act wv_act wv_dve "
                     "xn_ready c_loaded xct_ready xchi_done xclo_done mb_ready cbar_done "
                     "kp_ready khi_done klo_done v_ready v_done s0_ready s1_ready neg_done exp_done recip_done norm_done "
                     "ta_ready tb_ready pta_done ptb_done ot_ready ot_done acc_ready tail_chain tail_done "
                     "w1raw_loaded w1hi_split w1lo_split w1raw_loaded1 w1hi_split1 w1lo_split1").split():
            s(name)

        W1_LOADS = {0: 1, 1: 2}

        xt = x.rearrange("b (q p) d -> p (b q) d", p=T)
        outt = out.rearrange("b (q p) d -> p (b q) d", p=T)
        ctxt = ctx_in.rearrange("b (q p) d -> p (b q) d", p=T)

        def row(v):
            return v.rearrange("(a n) -> a n", a=1)

        def act_loads(act):
            act.dma_start(GATE[:, 0:2], row(g_xattn).partition_broadcast(128)).then_inc(s("gates_loaded"), 16)
            act.dma_start(GATE[:, 2:4], row(g_ffn).partition_broadcast(128)).then_inc(s("gates_loaded"), 16)
            act.dma_start(MASK[:, :], mask.rearrange("(a b) n -> a (b n)", a=1).partition_broadcast(128)
                          ).then_inc(s("mask_loaded"), 16)
            for k, v in enumerate((bo, g1, beta1, g2, beta2, g3, beta3, b2)):
                act.dma_start(BC[:, k, :], row(v).partition_broadcast(128)).then_inc(s("bcast_loaded"), 16)
            act.dma_start(BRB[:, :], row(m0_br).partition_broadcast(128)).then_inc(s("bcast_loaded"), 16)
            act.dma_start(B2S[:, :], m0_b2).then_inc(s("bcast_loaded"), 16)
            act.wait_ge(s("rows_zero"), 1)
            act.dma_start(ROWS[0:32, :], m0_b1.rearrange("e (c p) -> (e c) p", p=128)).then_inc(s("rows_loaded"), 16)
            act.dma_start(ROWS[32:36, :], b1.rearrange("(c p) -> c p", p=128)).then_inc(s("rows_loaded"), 16)
            act.dma_start(ROWS[64:72, :], m1_gate).then_inc(s("rows_loaded"), 16)
            act.wait_ge(s("wrf_zero"), 1)
            act.dma_start(WRF[:, 0:E], m0_Wr).then_inc(s("wr_loaded"), 16)

        BCASTS = 10 * 16

        bK, bV, bS0, bS1, bO, bA = P[0], P[1], P[2], P[3], P[6], P[7]
        bT = (P[4], P[5])

        def pe_proj(pe, b, hp):
            n = b * PAIRS + hp
            if hp == 0:
                pe.wait_ge(s("xclo_done"), b + 1)
            at_least(pe, s("klo_done"), n)
            for h in range(2):
                g = ds((2 * hp + h) * D, D)
                for k, (l, r) in enumerate(((GHI, XCHI), (GHI, XCLO), (GLO, XCHI))):
                    last = pe.matmul(bK[:, h * N:(h + 1) * N], l[:, g], r[:, 0:N], start=k == 0, stop=k == 2)
            last.then_inc(s("kp_ready"), 1)
            if hp % 2 == 0:
                at_least(pe, s("v_done"), b * (PAIRS // 2) + hp // 2)
                cols = ds(hp * 128, 256)
                for q in range(QB):
                    t = ds(q * T, T)
                    for k, (l, r) in enumerate(((XCHI, WVHI), (XCHI, WVLO), (XCLO, WVHI))):
                        last = pe.matmul(bV[:, q * 256:(q + 1) * 256], l[:, t], r[:, cols], start=k == 0, stop=k == 2)
                last.then_inc(s("v_ready"), 1)

        def pe_scores(pe, b, hp):
            n = b * PAIRS + hp
            pe.wait_ge(s("klo_done"), n + 1)
            at_least(pe, s("neg_done"), 4 * n)
            kh, kl = KHI[hp % 2], KLO[hp % 2]

            def first_keys(t):
                return t[:, :].rearrange("p (h k) -> p h k", h=2)[:, :, 0:T]

            q0, q1 = ds(N, T), ds(N + T, T)
            o0 = bS0[:, 0:2 * T].rearrange("p (h k) -> p h k", h=2)
            for k, (l, r) in enumerate(((XCHI, kh), (XCHI, kl), (XCLO, kh))):
                last = pe.matmul(o0, l[:, q0], first_keys(r), start=k == 0, stop=k == 2)
            last.then_inc(s("s0_ready"), 1)
            for k, (l, r) in enumerate(((XCHI, kh), (XCHI, kl), (XCLO, kh))):
                last = pe.matmul(bS1[:, :], l[:, q1], r[:, :], start=k == 0, stop=k == 2)
            last.then_inc(s("s1_ready"), 1)

        def pe_transpose_probs(pe, b, hp):
            n = b * PAIRS + hp
            pe.wait_ge(s("norm_done"), n + 1)
            p = SP[hp % 2]
            for h, ready, done in ((0, "ta_ready", "pta_done"), (1, "tb_ready", "ptb_done")):
                at_least(pe, s(done), n)
                for k, c in enumerate((h * T, 2 * T + h * N, 2 * T + h * N + T)):
                    last = pe.transpose(bT[h][:, k * T:(k + 1) * T], p[:, c:c + T], ident[:, :])
                last.then_inc(s(ready), 1)

        def pe_values(pe, b, hp):
            n = b * PAIRS + hp
            if hp % 2 == 0:
                pe.wait_ge(s("v_done"), b * (PAIRS // 2) + hp // 2 + 1)
            pe.wait_ge(s("pta_done"), n + 1)
            pe.wait_ge(s("ptb_done"), n + 1)
            at_least(pe, s("ot_done"), n)
            for k in range(QB):
                for h in range(2):
                    v = VB[:, k, (2 * hp + h) * DH:(2 * hp + h + 1) * DH]
                    probs = PT[h][:, 0:N] if k == 0 else PT[h][:, N:N + T]
                    last = pe.matmul(bO[h * DH:(h + 1) * DH, k * T:N], v, probs, start=k == 0, stop=k == 1,
                                     skip_group_check=True)
            last.then_inc(s("ot_ready"), 1)

        def pe_uniform(pe, b):
            at_least(pe, s("tail_done"), b)
            pe.wait_ge(s("cbar_done"), b + 1)
            pe.matmul(bA[:, N:N + D], CBARB[:, :], WVO[:, :], start=True, stop=True, skip_group_check=True)

        def pe_project(pe, b, hp):
            n = b * PAIRS + hp
            pe.wait_ge(s("ot_done"), n + 1)
            for q in range(QB):
                last = pe.matmul(bA[:, q * D:(q + 1) * D], OT[:, q * T:(q + 1) * T], WOS[:, hp, :], start=False,
                                 stop=hp == PAIRS - 1, skip_group_check=True)
            if hp == PAIRS - 1:
                last.then_inc(s("acc_ready"), 1)

        def pe_attention(pe, b, first):
            pe.wait_ge(s("xn_ready"), b + 1)
            pe.wait_ge(s("c_loaded"), 16 * (b + 1))
            at_least(pe, s("klo_done"), b * PAIRS)
            for k in range(QB):
                pe.transpose(bK[:, k * T:(k + 1) * T], CS[:, k, :], ident[:, :])
            for k in range(QB):
                last = pe.transpose(bK[:, N + k * T:N + (k + 1) * T], XN[:, k * T:(k + 1) * T], ident[:, :])
            last.then_inc(s("xct_ready"), 1)
            if not first:
                pe_transpose_probs(pe, b - 1, PAIRS - 1)
                pe_project(pe, b - 1, PAIRS - 2)
            pe_proj(pe, b, 0)
            if not first:
                pe_values(pe, b - 1, PAIRS - 1)
            for hp in range(PAIRS):
                pe_scores(pe, b, hp)
                if hp == 0 and not first:
                    pe_project(pe, b - 1, PAIRS - 1)
                if hp == 2:
                    pe_uniform(pe, b)
                if hp >= 2:
                    pe_project(pe, b, hp - 2)
                if hp >= 1:
                    pe_transpose_probs(pe, b, hp - 1)
                if hp < PAIRS - 1:
                    pe_proj(pe, b, hp + 1)
                if hp >= 1:
                    pe_values(pe, b, hp - 1)

        def act_k_hi(act, b, hp):
            n = b * PAIRS + hp
            act.wait_ge(s("kp_ready"), n + 1)
            act.activation(KHI[hp % 2][:, :], bK[:, :], ACT.Copy).then_inc(s("khi_done"), 1)

        def act_v(act, b, hp):
            act.wait_ge(s("v_ready"), b * (PAIRS // 2) + hp // 2 + 1)
            act.activation(VB[:, :, hp * 128:hp * 128 + 256], bV[:, :].rearrange("p (q c) -> p q c", q=QB),
                           ACT.Copy).then_inc(s("v_done"), 1)

        def act_out(act, b, hp):
            act.wait_ge(s("ot_ready"), b * PAIRS + hp + 1)
            act.activation(OT[:, :], bO[:, 0:N], ACT.Copy).then_inc(s("ot_done"), 1)

        BLOCKS = ((0, T, 0), (T, T, 1), (2 * T, N, 2), (2 * T + N, N, 3))

        def act_attention(act, b, first):
            act.wait_ge(s("xct_ready"), b + 1)
            act.activation(XCHI[:, :], bK[:, :], ACT.Copy).then_inc(s("xchi_done"), 1)
            act_k_hi(act, b, 0)
            act_v(act, b, 0)
            if not first:
                act_out(act, b - 1, PAIRS - 1)
            for hp in range(PAIRS):
                n = b * PAIRS + hp
                k = hp % 2
                for c, w, i in BLOCKS:
                    act.wait_ge(s("neg_done"), 4 * n + i + 1)
                    act.activation(SP[k][:, c:c + w], SP[k][:, c:c + w], ACT.Exp, bias=NEGM[k][:, i:i + 1],
                                   scale=-1.0, accum_out=RSUM[k][:, i:i + 1]).then_inc(s("exp_done"), 1)
                if hp < PAIRS - 1:
                    act_k_hi(act, b, hp + 1)
                    if hp % 2 == 1:
                        act_v(act, b, hp + 1)
                if hp >= 1:
                    act_out(act, b, hp - 1)

        def dve_k_lo(dve, b, hp):
            n = b * PAIRS + hp
            dve.wait_ge(s("khi_done"), n + 1)
            dve.tensor_tensor(KLO[hp % 2][:, :], bK[:, :], KHI[hp % 2][:, :].bitcast(f32), ALU.subtract
                              ).then_inc(s("klo_done"), 1)

        def dve_probs(dve, b, hp):
            n = b * PAIRS + hp
            for h, ready, done in ((0, "ta_ready", "pta_done"), (1, "tb_ready", "ptb_done")):
                dve.wait_ge(s(ready), n + 1)
                dve.tensor_copy(PT[h][:, :], bT[h][:, 0:3 * T]).then_inc(s(done), 1)

        def dve_tail(dve, b):
            c = s("tail_chain")
            base = b * 4 + 2
            tok = ds(b * N, N)
            dve.tensor_tensor(X[:, tok].rearrange("p (q d) -> p q d", q=QB), X[:, tok].rearrange("p (q d) -> p q d", q=QB),
                              TGBO[:, :].unsqueeze(1).to_broadcast([128, QB, D]), ALU.add).then_inc(c, 1)
            dve.wait_ge(s("acc_ready"), b + 1)
            dve.wait_ge(c, base + 1)
            for q in range(QB):
                xq = X[:, ds(b * N + q * D, D)]
                i = dve.scalar_tensor_tensor(out=xq, in0=bA[:, q * D:(q + 1) * D], scalar=GCOL[:, q:q + 1], in1=xq,
                                             op0=ALU.mult, op1=ALU.add)
            i.then_inc(c, 1)
            dve.wait_ge(c, base + 2)
            for q in range(QB):
                xq = X[:, ds(b * N + q * D, D)]
                i = dve.scalar_tensor_tensor(out=xq, in0=bA[:, N:N + D], scalar=FCOL[:, q:q + 1], in1=xq,
                                             op0=ALU.mult, op1=ALU.add)
            i.then_inc(s("tail_done"), 1)

        def dve_flags(dve, b):
            c = s("tail_chain")
            at_least(dve, s("tail_done"), b)
            dve.wait_ge(s("neg_done"), 4 * (b * PAIRS) + 4)
            dve.tensor_scalar(FCOL[:, :], NEGM[0][:, 0:4:2], BIG / 10, GATE[:, 0:1], ALU.is_ge, ALU.mult).then_inc(c, 1)
            dve.wait_ge(c, b * 4 + 1)
            dve.tensor_scalar(GCOL[:, :], FCOL[:, :], -1.0, GATE[:, 0:1], ALU.mult, ALU.add).then_inc(c, 1)

        def dve_attention(dve, b, first):
            at_least(dve, s("xct_ready"), b)
            for q in range(QB):
                i = dve.tensor_scalar(XN[:, q * D:(q + 1) * D], X[:, ds(b * N + q * D, D)],
                                      MV[:, ds(b * QB + q, 1), 0:1].rearrange("p a c -> p (a c)"),
                                      RSTD[:, ds(b * QB + q, 1)], ALU.subtract, ALU.mult)
            i.then_inc(s("xn_ready"), 1)
            at_least(dve, s("neg_done"), 4 * b * PAIRS)
            for lo, n, k in ((0, T, 0), (T, N, 0)):
                i = dve.scalar_tensor_tensor(out=MB[:, lo:lo + n], in0=MASK[:, ds(b * N, n)], scalar=-BIG,
                                             in1=TRI[:, lo:lo + n], op0=ALU.mult, op1=ALU.add)
            i.then_inc(s("mb_ready"), 1)
            dve.wait_ge(s("xchi_done"), b + 1)
            at_least(dve, s("cbar_done"), b)
            dve.reduce_sum(CBAR[:, :], bK[:, 0:N], AX.X).then_inc(s("cbar_sum"), 1)
            dve.tensor_tensor(XCLO[:, :], bK[:, :], XCHI[:, :].bitcast(f32), ALU.subtract).then_inc(s("xclo_done"), 1)
            if not first:
                dve_probs(dve, b - 1, PAIRS - 1)
            dve_k_lo(dve, b, 0)
            for hp in range(PAIRS):
                n = b * PAIRS + hp
                k = hp % 2
                waits_alone(dve, s("ident_ready"), (s("tb_ready"), n - 1), (s("mb_ready"), b + 1), (s("s0_ready"), n + 1))
                for c, w, i in BLOCKS:
                    if i == 2:
                        waits_alone(dve, s("ident_ready"), (s("s1_ready"), n + 1))
                    bank, bc = (bS0, c) if i < 2 else (bS1, c - 2 * T)
                    m = MB[:, 0:T] if i < 2 else MB[:, T:3 * T]
                    dve.tensor_tensor_reduce(out=SP[k][:, c:c + w], in0=bank[:, bc:bc + w], in1=m, scale=-1.0, scalar=HUGE,
                                             op0=ALU.add, op1=ALU.min, accum_out=NEGM[k][:, i:i + 1]
                                             ).then_inc(s("neg_done"), 1)
                if hp == 0:
                    if not first:
                        dve_tail(dve, b - 1)
                    dve_flags(dve, b)
                if hp == 1:
                    dve.wait_ge(s("cbar_sum"), b + 1)
                    dve.tensor_scalar(CBARB[:, :], ZERO[:, 0:128], 1.0, CBAR[:, 0:1], ALU.mult, ALU.add
                                      ).then_inc(s("cbar_done"), 1)
                if hp >= 1:
                    dve_probs(dve, b, hp - 1)
                dve.wait_ge(s("exp_done"), 4 * (n + 1))
                dve.reciprocal(RCP[k][:, :], RSUM[k][:, :]).then_inc(s("recip_done"), 1)
                if hp < PAIRS - 1:
                    dve_k_lo(dve, b, hp + 1)

        def pool_attention(pool, b):
            for hp in range(PAIRS):
                n = b * PAIRS + hp
                k = hp % 2
                waits_alone(pool, s("ident_ready"), (s("recip_done"), n + 1))
                for c, w, i in BLOCKS:
                    last = pool.tensor_scalar(SP[k][:, c:c + w], SP[k][:, c:c + w], RCP[k][:, i:i + 1], 1.0,
                                              ALU.mult, ALU.mult)
                last.then_inc(s("norm_done"), 1)
                w1e = ds(b * 2 * H, 2 * H)
                if hp == 2:
                    pool.wait_ge(s("w1raw_loaded"), 16 * (b + 1))
                    pool.tensor_copy(W1HI[:, w1e], W1RAW[:, :]).then_inc(s("w1hi_split"), 1)
                if hp == 5:
                    pool.wait_ge(s("w1hi_split"), b + 1)
                    pool.tensor_tensor(W1LO[:, w1e], W1RAW[:, :], W1HI[:, w1e].bitcast(f32), ALU.subtract
                                       ).then_inc(s("w1lo_split"), 1)

        STATS = [0]

        def dve_stats(dve, src):
            base = STATS[0]
            STATS[0] += TILES // 4
            with dve.Fori(0, TILES // 4) as i:
                waits_alone(dve, s("ident_ready"), (s("aggr_done"), ONE + base + i))
                for j in range(4):
                    l = dve.bn_stats(STAT[:, j * 6:(j + 1) * 6], src[:, ds(i * 4 * D + j * D, D)])
                l.then_inc(s("stat_done"), 1)
                waits_alone(dve, s("ident_ready"), (s("stat_done"), ONE + base + i + 1), (s("mv_done"), ONE + base + i))
                for j in range(4):
                    l = dve.bn_aggr(AGGR[:, j, :], STAT[:, j * 6:(j + 1) * 6])
                l.then_inc(s("aggr_done"), 1)
                waits_alone(dve, s("ident_ready"), (s("aggr_done"), ONE + base + i + 1))
                dve.tensor_copy(MV[:, ds(i * 4, 4), :], AGGR[:, 0:4, :]).then_inc(s("mv_done"), 1)
            dve_veps(dve)

        VEPS = [0]

        def dve_veps(dve):
            dve.wait_ge(s("mv_done"), ONE + STATS[0])
            dve.tensor_scalar(RSTD[:, :], MV[:, :, 1], EPS, None, ALU.add).then_inc(s("veps_ready"), 1)
            VEPS[0] += 1
            dve.wait_ge(s("rstd_ready"), VEPS[0])

        RST = [0]

        def pool_rstd(pool):
            RST[0] += 1
            pool.wait_ge(s("veps_ready"), RST[0])
            pool.tensor_tensor(RSTD[:, :], RSTD[:, :], HALF[:, :], ALU.pow).then_inc(s("rstd_ready"), 1)

        for m in range(2):
            for name in ("n_ready xt_ready xthi_done xtlo_done lt_ready lt_done lg_ready lg_done route exp_ready "
                         "w_ready wsl_done wt_ready wt_done b2_ready up_a up_g sil_done h_done y_ready acc_chain "
                         "chunk_done").split():
                s(f"m{m}_{name}")

        def dve_route(dve, m):
            c = s(f"m{m}_route")
            step = [0]

            def then(i):
                i.then_inc(c, 1)
                step[0] += 1
                dve.wait_ge(c, step[0])

            lg = LG[:, :].rearrange("p (t e) -> p t e", e=E)
            full = [128, TILES, E]

            def over(v):
                return v[:, :].unsqueeze(2).to_broadcast(full)

            dve.wait_ge(s(f"m{m}_lg_done"), ONE + CHUNKS)
            then(dve.tensor_reduce(RV[0][:, :], lg, AX.X, ALU.max))
            then(dve.tensor_tensor(RT[0][:, :, :], lg, over(RV[0]), ALU.is_equal))
            then(dve.tensor_tensor(RT[0][:, :, :], RT[0][:, :, :], RANK[:, :, :], ALU.mult))
            then(dve.tensor_reduce(RV[1][:, :], RT[0][:, :, :], AX.X, ALU.max))
            then(dve.tensor_tensor(RT[0][:, :, :], RT[0][:, :, :], over(RV[1]), ALU.is_equal))
            then(dve.scalar_tensor_tensor(out=RT[1][:, :, :], in0=RT[0][:, :, :], scalar=-BIG, in1=lg,
                                          op0=ALU.mult, op1=ALU.add))
            then(dve.tensor_reduce(RV[2][:, :], RT[1][:, :, :], AX.X, ALU.max))
            then(dve.tensor_tensor(RT[1][:, :, :], RT[1][:, :, :], over(RV[2]), ALU.is_equal))
            then(dve.tensor_tensor(RT[1][:, :, :], RT[1][:, :, :], RANK[:, :, :], ALU.mult))
            then(dve.tensor_reduce(RV[1][:, :], RT[1][:, :, :], AX.X, ALU.max))
            then(dve.tensor_tensor(RT[1][:, :, :], RT[1][:, :, :], over(RV[1]), ALU.is_equal))
            then(dve.tensor_tensor(RV[3][:, :], RV[2][:, :], RV[0][:, :], ALU.subtract))
            dve.wait_ge(s(f"m{m}_exp_ready"), 1)
            then(dve.tensor_scalar(RV[5][:, :], RV[4][:, :], 1.0, None, ALU.add))
            then(dve.reciprocal(RV[5][:, :], RV[5][:, :]))
            then(dve.tensor_tensor(RV[4][:, :], RV[4][:, :], RV[5][:, :], ALU.mult))
            then(dve.tensor_tensor(RT[0][:, :, :], RT[0][:, :, :], over(RV[5]), ALU.mult))
            then(dve.tensor_tensor(RT[1][:, :, :], RT[1][:, :, :], over(RV[4]), ALU.mult))
            dve.tensor_tensor(WGT[:, :].rearrange("p (t e) -> p t e", e=E), RT[0][:, :, :], RT[1][:, :, :], ALU.add
                              ).then_inc(s(f"m{m}_w_ready"), 1)
            dve.wait_ge(s(f"m{m}_w_ready"), 1)

        DIFF_STEP = 12

        def dve_mixture(dve, m):
            q = lambda name: s(f"m{m}_{name}")
            dve_stats(dve, X)
            with dve.Fori(0, CHUNKS // 2) as i:
                dve.wait_ge(q("xt_ready"), ONE + 2 * i)
                for k in range(2):
                    for t in range(CH):
                        tile = i * 2 * CH + k * CH + t
                        l = dve.tensor_scalar(XNS[k][:, t * D:(t + 1) * D], X[:, ds(tile * D, D)],
                                              MV[:, ds(tile, 1), 0:1].rearrange("p a c -> p (a c)"),
                                              RSTD[:, ds(tile, 1)], ALU.subtract, ALU.mult)
                    l.then_inc(q("n_ready"), 1)
                for k in range(2):
                    c = ds((i * 2 + k) * W, W)
                    dve.wait_ge(q("xthi_done"), 2 * i + k + 1)
                    dve.tensor_tensor(XTLO[:, c], P[k][:, :], XTHI[:, c].bitcast(f32), ALU.subtract
                                      ).then_inc(q("xtlo_done"), 1)
                for k in range(2):
                    dve.wait_ge(q("lg_ready"), 2 * i + k + 1)
                    src = P[4 + k][:, :].rearrange("p (t c) -> p t c", c=128)[:, :, 0:E]
                    dst = LG[:, ds((i * 2 + k) * CH * E, CH * E)].rearrange("p (t e) -> p t e", e=E)
                    if m == 0:
                        l = dve.tensor_tensor(dst, src, BRB[:, :].unsqueeze(1).to_broadcast([128, CH, E]), ALU.add)
                    else:
                        l = dve.tensor_copy(dst, src)
                    l.then_inc(q("lg_done"), 1)
            dve_route(dve, m)
            combs = E + 1 if m == 0 else E
            with dve.Fori(0, CHUNKS) as c:
                steps = c * E
                dve.wait_ge(q("chunk_done"), ONE + c)
                dve.tensor_copy(WSL[:, :], WGT[:, ds(c * CH * E, CH * E)]).then_inc(q("wsl_done"), 1)
                dve.wait_ge(q("wsl_done"), c + 1)

                def comb(e):
                    dve.wait_ge(q("y_ready"), steps + e + 1)
                    done = c * combs + e + (combs - E)
                    dve.wait_ge(q("acc_chain"), ONE + done)
                    y = P[4 + e % 2]
                    for t in range(CH):
                        tok = slice(t * D, (t + 1) * D)
                        w = WSL[:, t * E + e:t * E + e + 1]
                        if m == 1 and e == 0:
                            l = dve.tensor_scalar(ACC[:, tok], y[:, tok], w, None, ALU.mult)
                        else:
                            l = dve.scalar_tensor_tensor(out=ACC[:, tok], in0=y[:, tok], scalar=w, in1=ACC[:, tok],
                                                         op0=ALU.mult, op1=ALU.add)
                    l.then_inc(q("acc_chain"), 1)

                if m == 0:
                    dve.wait_ge(q("b2_ready"), c + 1)
                    dve.tensor_copy(ACC[:, :], P[7][:, :]).then_inc(q("acc_chain"), 1)
                for e in range(E):
                    for j in range(2):
                        n = 2 * (steps + e) + j + 1
                        dve.wait_ge(q("sil_done"), n)
                        dve.wait_ge(q("up_g"), n)
                        if m == 0:
                            l = dve.scalar_tensor_tensor(out=HT[e % 2][:, j, :], in0=P[2 * j + 1][:, :],
                                                         scalar=COLS[:, e * 4 + 2 + j:e * 4 + 3 + j], in1=SIL[j][:, :],
                                                         op0=ALU.add, op1=ALU.mult)
                        else:
                            l = dve.tensor_tensor(HT[e % 2][:, j, :], P[2 * j + 1][:, :], SIL[j][:, :], ALU.mult)
                        l.then_inc(q("h_done"), 1)
                    if e >= 1:
                        comb(e - 1)
                comb(E - 1)
                dve.wait_ge(q("acc_chain"), ONE + (c + 1) * combs)
                xc = X[:, ds(c * W, W)]
                dve.scalar_tensor_tensor(out=xc, in0=ACC[:, :], scalar=GATE[:, 2 + m:3 + m], in1=xc,
                                         op0=ALU.mult, op1=ALU.add).then_inc(q("chunk_done"), 1)
            dve.wait_ge(q("chunk_done"), ONE + CHUNKS)

        def pe_mixture(pe, m):
            q = lambda name: s(f"m{m}_{name}")
            wr = ds(m * 128, 128)
            with pe.Fori(0, CHUNKS // 2) as i:
                for k in range(2):
                    pe.wait_ge(q("n_ready"), 2 * i + k + 1)
                    pe.wait_ge(q("xtlo_done"), ONE + 2 * i)
                    for t in range(CH):
                        l = pe.transpose(P[k][:, t * T:(t + 1) * T], XNS[k][:, t * D:(t + 1) * D], ident[:, :])
                    l.then_inc(q("xt_ready"), 1)
                for k in range(2):
                    c = ds((i * 2 + k) * W, W)
                    pe.wait_ge(q("xtlo_done"), ONE + 2 * i + k + 1)
                    pe.wait_ge(q("lt_done"), ONE + 2 * i)
                    for n, (l_, r_) in enumerate(((WRHI, XTHI), (WRHI, XTLO), (WRLO, XTHI))):
                        l = pe.matmul(P[2 + k][:, :], l_[:, wr], r_[:, c], start=n == 0, stop=n == 2)
                    l.then_inc(q("lt_ready"), 1)
                for k in range(2):
                    pe.wait_ge(q("lt_done"), ONE + 2 * i + k + 1)
                    pe.wait_ge(q("lg_done"), ONE + 2 * i)
                    for t in range(CH):
                        l = pe.transpose(P[4 + k][:, t * T:(t + 1) * T], LTS[k][:, t * T:(t + 1) * T], ident[:, :])
                    l.then_inc(q("lg_ready"), 1)
            pe.wait_ge(q("lg_done"), ONE + CHUNKS)
            with pe.Fori(0, CHUNKS) as c:
                steps = c * E
                tok = ds(c * W, W)
                if m == 0:
                    pe.wait_ge(q("wsl_done"), c + 1)
                    for t in range(CH):
                        l = pe.transpose(P[6][0:E, t * T:(t + 1) * T], WSL[:, t * E:(t + 1) * E], ident[:, :])
                    l.then_inc(q("wt_ready"), 1)
                    pe.wait_ge(q("wt_done"), c + 1)
                    for t in range(CH):
                        l = pe.matmul(P[7][:, t * D:(t + 1) * D], WTS[:, t * T:(t + 1) * T], B2S[:, :], start=True, stop=True)
                    l.then_inc(q("b2_ready"), 1)

                def down(e):
                    pe.wait_ge(q("h_done"), 2 * (steps + e) + 2)
                    done = c * (E + 1 - m) + e - 1 + (1 - m)
                    if e >= 2:
                        pe.wait_ge(q("acc_chain"), ONE + done)
                    for t in range(CH):
                        for j in range(2):
                            l = pe.matmul(P[4 + e % 2][:, t * D:(t + 1) * D], HT[e % 2][:, j, t * T:(t + 1) * T],
                                          W2S[m][:, (2 * e + j) * D:(2 * e + j + 1) * D], start=j == 0, stop=j == 1)
                    l.then_inc(q("y_ready"), 1)

                for e in range(E):
                    for j in range(2):
                        pe.wait_ge(q("h_done"), 2 * (steps + e - 1) + j + 1) if e else \
                            pe.wait_ge(q("chunk_done"), ONE + c)
                        for bank, col, ready in ((P[2 * j], j, "up_a"), (P[2 * j + 1], 2 + j, "up_g")):
                            wc = ds(e * 2 * H + col * 128, 128)
                            for n, (l_, r_) in enumerate(((W1HI, XTHI), (W1HI, XTLO), (W1LO, XTHI))):
                                l = pe.matmul(bank[:, :], l_[:, wc], r_[:, tok], start=n == 0, stop=n == 2)
                            l.then_inc(q(ready), 1)
                    if e >= 1:
                        down(e - 1)
                down(E - 1)
            pe.wait_ge(q("chunk_done"), ONE + CHUNKS)

        def act_mixture(act, m):
            q = lambda name: s(f"m{m}_{name}")
            with act.Fori(0, CHUNKS // 2) as i:
                for k in range(2):
                    act.wait_ge(q("xt_ready"), ONE + 2 * i + k + 1)
                    act.activation(XTHI[:, ds((i * 2 + k) * W, W)], P[k][:, :], ACT.Copy).then_inc(q("xthi_done"), 1)
                for k in range(2):
                    act.wait_ge(q("lt_ready"), 2 * i + k + 1)
                    act.activation(LTS[k][:, :], P[2 + k][:, :], ACT.Copy).then_inc(q("lt_done"), 1)
            act.wait_ge(q("route"), DIFF_STEP)
            act.activation(RV[4][:, :], RV[3][:, :], ACT.Exp).then_inc(q("exp_ready"), 1)
            with act.Fori(0, CHUNKS) as c:
                steps = c * E
                if m == 0:
                    act.wait_ge(q("wt_ready"), c + 1)
                    act.activation(WTS[:, :], P[6][0:E, :], ACT.Copy).then_inc(q("wt_done"), 1)
                for e in range(E):
                    for j in range(2):
                        n = 2 * (steps + e) + j
                        act.wait_ge(q("up_a"), n + 1)
                        if e:
                            act.wait_ge(q("h_done"), n - 1)
                        else:
                            act.wait_ge(q("chunk_done"), ONE + c)
                        bias = COLS[:, e * 4 + j:e * 4 + j + 1] if m == 0 else 0.0
                        act.activation(SIL[j][:, :], P[2 * j][:, :], ACT.Silu, bias=bias).then_inc(q("sil_done"), 1)

        for name in ("d_loaded dy_ready dyt_ready dyt_done ds_ready dneg_done dexp_done dt_ready dpt_done dav_ready "
                     "dres_done dchain dcnt dh_ready dh_done dff_ready dfin").split():
            s(name)
        TURNS = B // U

        def decoder_loads(sp):
            with sp.Fori(0, TURNS) as i:
                sp.wait_ge(s("dres_done"), ONE + (TURNS + i) * U)
                sp.dma_start(CU[:, :, :, :].rearrange("p u q d -> p (u q) d"), ctxt[:, ds(i * U * QB, U * QB), :]
                             ).then_inc(s("d_loaded"), 16)

        def final_store(sp):
            for c in range(CHUNKS):
                sp.wait_ge(s("m1_chunk_done"), ONE + c + 1)
                sp.dma_start(outt[:, c * CH:(c + 1) * CH, :], X[:, c * W:(c + 1) * W].rearrange("p (t d) -> p t d", d=D)
                             ).then_inc(s("out_stored"), 16)
            sp.wait_ge(s("out_stored"), 16 * CHUNKS)

        SC = float(D) ** -0.5

        def dve_apply(dve, src, i, gamma, beta):
            c = s("dchain")
            for t in range(U * QB):
                tile = i * U * QB + t
                l = dve.tensor_scalar(YS[:, t * D:(t + 1) * D], src[:, ds(tile * D, D)],
                                      MV[:, ds(tile, 1), 0:1].rearrange("p a c -> p (a c)"),
                                      RSTD[:, ds(tile, 1)], ALU.subtract, ALU.mult)
                if gamma is None and t % QB == QB - 1:
                    l.then_inc(s("dy_ready"), 1)
            if gamma is not None:
                l.then_inc(c, 1)
                for u in range(U):
                    y = YS[:, u * N:(u + 1) * N].rearrange("p (q d) -> p q d", d=D)
                    if u == 0:
                        dve_linked(dve, i)
                    l = dve.tensor_tensor(y, y, BC[:, gamma, :].unsqueeze(1).to_broadcast([128, QB, D]), ALU.mult)
                l.then_inc(c, 1)
                dve_linked(dve, i)
                for u in range(U):
                    y = YS[:, u * N:(u + 1) * N].rearrange("p (q d) -> p q d", d=D)
                    dve.tensor_tensor(y, y, BC[:, beta, :].unsqueeze(1).to_broadcast([128, QB, D]), ALU.add
                                      ).then_inc(s("dy_ready"), 1)

        LINK = [0, 0, 0]

        def dve_linked(dve, i):
            LINK[1] += 1
            dve.wait_ge(s("dchain"), LINK[0] + i * LINK[2] + LINK[1])

        def dve_decoder(dve):
            dve_stats(dve, X)
            for stage in range(2):
                cross = stage == 1
                LINK[1], LINK[2] = 0, (3 if cross else 1)
                keys = N if cross else T
                base = stage * B
                if cross:
                    dve_veps(dve)
                with dve.Fori(0, TURNS) as i:
                    n0 = base + i * U
                    dve.wait_ge(s("dav_ready"), ONE + n0)
                    if cross:
                        dve_apply(dve, YR, i, 1, 2)
                    else:
                        dve_apply(dve, X, i, None, None)
                    for u in range(U):
                        waits_alone(dve, s("ident_ready"), (s("ds_ready"), n0 + u + 1))
                        for q in range(QB):
                            lo, n = (q * N, N) if cross else ((0, T) if q == 0 else (T, N))
                            m = ZERO[:, :] if cross else TRI[:, lo:lo + n]
                            k = u * QB + q
                            dve.tensor_tensor_reduce(out=UP[:, u * 512 + lo:u * 512 + lo + n], in0=P[u][:, lo:lo + n],
                                                     in1=m, scale=-SC, scalar=HUGE, op0=ALU.add, op1=ALU.min,
                                                     accum_out=UNEG[:, k:k + 1]).then_inc(s("dneg_done"), 1)
                    for u in range(U):
                        w = 512 if cross else 3 * T
                        dve.wait_ge(s("dt_ready"), n0 + u + 1)
                        dve.tensor_copy(UPT[:, u * 512:u * 512 + w], P[4 + u][:, 0:w]).then_inc(s("dpt_done"), 1)
                    dve.wait_ge(s("dexp_done"), 2 * (n0 + U))
                    dve.reciprocal(URCP[:, :], USUM[:, :]).then_inc(s("dchain"), 1)
                    dve_linked(dve, i)
                    for u in range(U):
                        dve.wait_ge(s("dav_ready"), ONE + n0 + u + 1)
                        for q in range(QB):
                            k = u * QB + q
                            tile = i * U * QB + k
                            l = dve.scalar_tensor_tensor(out=YR[:, ds(tile * D, D)], in0=P[u][:, q * D:(q + 1) * D],
                                                         scalar=URCP[:, k:k + 1], in1=YS[:, k * D:(k + 1) * D],
                                                         op0=ALU.mult, op1=ALU.add)
                        l.then_inc(s("dres_done"), 1)
                    dve_turn_stats(dve, i, (s("dres_done"), ONE + n0 + U))
                    assert LINK[1] == LINK[2], LINK
                LINK[0] += TURNS * LINK[2]
            dve_veps(dve)
            LINK[1], LINK[2] = 0, 3
            with dve.Fori(0, TURNS) as i:
                dve.wait_ge(s("dfin"), ONE + i * U)
                dve_apply(dve, YR, i, 3, 4)
                dve.wait_ge(s("dy_ready"), 2 * B + (i + 1) * U)
                for u in range(U):
                    y = YS[:, u * N:(u + 1) * N].rearrange("p (q d) -> p q d", d=D)
                    dve.wait_ge(s("dyt_ready"), 2 * B + i * U + u + 1)
                    l = dve.tensor_tensor(y, y, BC[:, 7, :].unsqueeze(1).to_broadcast([128, QB, D]), ALU.add)
                l.then_inc(s("dchain"), 1)
                dve_linked(dve, i)
                for u in range(U):
                    dve.wait_ge(s("dff_ready"), ONE + i * U + u + 1)
                    dve.tensor_tensor(YR[:, ds((i * U + u) * N, N)], P[4 + u][:, 0:N], YS[:, u * N:(u + 1) * N], ALU.add
                                      ).then_inc(s("dfin"), 1)
                dve_turn_stats(dve, i, (s("dfin"), ONE + (i + 1) * U))
                assert LINK[1] == LINK[2], LINK
            dve_veps(dve)
            fc = s("dcnt")
            dve.tensor_scalar(BC[:, 5, :], BC[:, 5, :], GATE[:, 1:2], None, ALU.mult)
            dve.tensor_scalar(BC[:, 6, :], BC[:, 6, :], GATE[:, 1:2], None, ALU.mult).then_inc(fc, 1)
            dve.wait_ge(fc, 1)
            with dve.Fori(0, TURNS) as i:
                for t in range(U * QB):
                    tile = i * U * QB + t
                    l = dve.tensor_scalar(YS[:, t * D:(t + 1) * D], YR[:, ds(tile * D, D)],
                                          MV[:, ds(tile, 1), 0:1].rearrange("p a c -> p (a c)"),
                                          RSTD[:, ds(tile, 1)], ALU.subtract, ALU.mult)
                l.then_inc(fc, 1)
                dve.wait_ge(fc, i * 4 + 2)
                full = [128, U * QB, D]
                y = YS[:, :].rearrange("p (t d) -> p t d", d=D)
                xs = X[:, ds(i * U * N, U * N)]
                dve.tensor_tensor(y, y, BC[:, 5, :].unsqueeze(1).to_broadcast(full), ALU.mult).then_inc(fc, 1)
                dve.wait_ge(fc, i * 4 + 3)
                dve.tensor_tensor(y, y, BC[:, 6, :].unsqueeze(1).to_broadcast(full), ALU.add).then_inc(fc, 1)
                dve.wait_ge(fc, i * 4 + 4)
                dve.tensor_tensor(xs, xs, YS[:, :], ALU.add).then_inc(fc, 1)
                dve.wait_ge(fc, i * 4 + 5)

        def dve_turn_stats(dve, i, written):
            base = STATS[0]
            waits_alone(dve, s("ident_ready"), written)
            for t in range(U * QB):
                l = dve.bn_stats(STAT[:, t * 6:(t + 1) * 6], YR[:, ds((i * U * QB + t) * D, D)])
            l.then_inc(s("stat_done"), 1)
            waits_alone(dve, s("ident_ready"), (s("stat_done"), ONE + base + i + 1))
            for t in range(U * QB):
                l = dve.bn_aggr(AGGR[:, t, :], STAT[:, t * 6:(t + 1) * 6])
            l.then_inc(s("aggr_done"), 1)
            waits_alone(dve, s("ident_ready"), (s("aggr_done"), ONE + base + i + 1))
            dve.tensor_copy(MV[:, ds(i * U * QB, U * QB), :], AGGR[:, :, :]).then_inc(s("mv_done"), 1)
            dve.wait_ge(s("mv_done"), ONE + base + i + 1)
            STATS[0] = base + TURNS

        def pe_decoder(pe):
            for stage in range(2):
                cross = stage == 1
                base = stage * B
                with pe.Fori(0, TURNS) as i:
                    n0 = base + i * U
                    if cross:
                        pe.wait_ge(s("d_loaded"), 16 * (i + 1))
                    pe.wait_ge(s("dres_done"), ONE + n0)
                    for u in range(U):
                        pe.wait_ge(s("dy_ready"), n0 + u + 1)
                        for k in range(QB):
                            l = pe.transpose(P[u][:, k * T:(k + 1) * T], YS[:, u * N + k * D:u * N + (k + 1) * D], ident[:, :])
                        if cross:
                            for k in range(QB):
                                l = pe.transpose(P[u][:, N + k * T:N + (k + 1) * T], CU[:, u, k, :], ident[:, :])
                        l.then_inc(s("dyt_ready"), 1)
                    for u in range(U):
                        pe.wait_ge(s("dyt_done"), n0 + u + 1)
                        yt = YT[:, u * 512:(u + 1) * 512]
                        for q in range(QB):
                            lo, n = (q * N, N) if cross else ((0, T) if q == 0 else (T, N))
                            keys = yt[:, N:2 * N] if cross else yt[:, 0:n]
                            l = pe.matmul(P[u][:, lo:lo + n], yt[:, q * T:(q + 1) * T], keys, start=True, stop=True)
                        l.then_inc(s("ds_ready"), 1)
                    for u in range(U):
                        pe.wait_ge(s("dexp_done"), 2 * (n0 + u + 1))
                        blocks = 4 if cross else 3
                        for k in range(blocks):
                            l = pe.transpose(P[4 + u][:, k * T:(k + 1) * T], UP[:, u * 512 + k * T:u * 512 + (k + 1) * T],
                                             ident[:, :])
                        l.then_inc(s("dt_ready"), 1)
                    for u in range(U):
                        pe.wait_ge(s("dpt_done"), n0 + u + 1)
                        for q in range(QB):
                            ks = range(QB) if cross else range(q + 1)
                            for k in ks:
                                blk = 2 * q + k if cross else q + k
                                v = CU[:, u, k, :] if cross else YS[:, u * N + k * D:u * N + (k + 1) * D]
                                l = pe.matmul(P[u][:, q * D:(q + 1) * D],
                                              UPT[:, u * 512 + blk * T:u * 512 + (blk + 1) * T], v,
                                              start=k == 0, stop=k == ks[-1])
                        l.then_inc(s("dav_ready"), 1)
            hc = DFF // 128
            with pe.Fori(0, TURNS) as i:
                pe.wait_ge(s("dres_done"), ONE + 2 * B)
                pe.wait_ge(s("dfin"), ONE + i * U)
                for u in range(U):
                    pe.wait_ge(s("dy_ready"), 2 * B + i * U + u + 1)
                    for k in range(QB):
                        l = pe.transpose(P[u][:, k * T:(k + 1) * T], YS[:, u * N + k * D:u * N + (k + 1) * D], ident[:, :])
                    l.then_inc(s("dyt_ready"), 1)
                pe.wait_ge(s("dyt_done"), 2 * B + (i + 1) * U)
                for k in range(2):
                    for m in range(hc):
                        g = k * hc + m
                        if g >= 4:
                            pe.wait_ge(s("dh_done"), i * 2 * hc + g - 3)
                        l = pe.matmul(P[g % 4][:, :], L1W1[:, m * 128:(m + 1) * 128], YT[:, k * W:(k + 1) * W],
                                      start=True, stop=True)
                        l.then_inc(s("dh_ready"), 1)
                for u in range(U):
                    half = u // 2
                    pe.wait_ge(s("dh_done"), i * 2 * hc + (half + 1) * hc)
                    for k in range(QB):
                        t = (u % 2) * QB + k
                        for m in range(hc):
                            c = (half * hc + m) * W + t * T
                            src = HL[:, c:c + T] if half == 0 else UP_HL(c)
                            l = pe.matmul(P[4 + u][:, k * D:(k + 1) * D], src, L1W2[:, m, :],
                                          start=m == 0, stop=m == hc - 1)
                    l.then_inc(s("dff_ready"), 1)

        def UP_HL(c):
            return UP[:, c - 4 * W:c - 4 * W + T]

        def act_decoder(act):
            for stage in range(2):
                cross = stage == 1
                base = stage * B
                with act.Fori(0, TURNS) as i:
                    n0 = base + i * U
                    w = 512 if cross else N
                    for u in range(U):
                        act.wait_ge(s("dyt_ready"), n0 + u + 1)
                        act.activation(YT[:, u * 512:u * 512 + w], P[u][:, 0:w], ACT.Copy).then_inc(s("dyt_done"), 1)
                    for u in range(U):
                        for q in range(QB):
                            k = u * QB + q
                            lo, n = (q * N, N) if cross else ((0, T) if q == 0 else (T, N))
                            act.wait_ge(s("dneg_done"), 2 * n0 + k + 1)
                            p = UP[:, u * 512 + lo:u * 512 + lo + n]
                            act.activation(p, p, ACT.Exp, bias=UNEG[:, k:k + 1], scale=-1.0,
                                           accum_out=USUM[:, k:k + 1]).then_inc(s("dexp_done"), 1)
            hc = DFF // 128
            with act.Fori(0, TURNS) as i:
                for u in range(U):
                    act.wait_ge(s("dyt_ready"), 2 * B + i * U + u + 1)
                    act.activation(YT[:, u * N:(u + 1) * N], P[u][:, 0:N], ACT.Copy).then_inc(s("dyt_done"), 1)
                for g in range(2 * hc):
                    act.wait_ge(s("dh_ready"), i * 2 * hc + g + 1)
                    if g == 0:
                        act.wait_ge(s("dff_ready"), ONE + i * U)
                    dst = HL[:, g * W:(g + 1) * W] if g < hc else UP[:, (g - hc) * W:(g - hc + 1) * W]
                    act.activation(dst, P[g % 4][:, :], ACT.Relu, bias=COLS[:, 32 + g % hc:33 + g % hc]
                                   ).then_inc(s("dh_done"), 1)

        def pool_split1(pool):
            pool.wait_ge(s("m0_chunk_done"), ONE + CHUNKS)
            with pool.Fori(0, E) as e:
                w1e = ds(e * 2 * H, 2 * H)
                pool.wait_ge(s("w1lo_split1"), ONE + e)
                pool.dma_start(W1RAW[:, 0:H], m1_wg.rearrange("e d h -> d e h")[:, ds(e, 1), :].rearrange("d e h -> d (e h)")
                               ).then_inc(s("w1raw_loaded1"), 16)
                pool.dma_start(W1RAW[:, H:2 * H], m1_wu.rearrange("e d h -> d e h")[:, ds(e, 1), :].rearrange("d e h -> d (e h)")
                               ).then_inc(s("w1raw_loaded1"), 16)
                pool.wait_ge(s("w1raw_loaded1"), 32 * (e + 1))
                pool.tensor_copy(W1HI[:, w1e], W1RAW[:, :]).then_inc(s("w1hi_split1"), 1)
                pool.wait_ge(s("w1hi_split1"), e + 1)
                pool.tensor_tensor(W1LO[:, w1e], W1RAW[:, :], W1HI[:, w1e].bitcast(f32), ALU.subtract
                                   ).then_inc(s("w1lo_split1"), 1)

        @block.sync
        def _(sp):
            for c in range(CHUNKS):
                sp.dma_start(X[:, c * W:(c + 1) * W].rearrange("p (t d) -> p t d", d=D),
                             xt[:, c * CH:(c + 1) * CH, :]).then_inc(s("x_loaded"), 16)
            for k, w in enumerate((Wq, Wk, Wv)):
                sp.dma_start(RAW[:, k * INNER:(k + 1) * INNER], w).then_inc(s("proj_loaded"), 16)
            sp.dma_start(WOS[:, :, :], Wo.rearrange("(c p) d -> p c d", p=128)).then_inc(s("wo_loaded"), 16)
            sp.dma_start(L1W1[:, :], w1).then_inc(s("l1w_loaded"), 16)
            sp.dma_start(L1W2[:, :, :], w2.rearrange("(c p) d -> p c d", p=128)).then_inc(s("l1w_loaded"), 16)
            sp.dma_start(W2S[0][:, :].rearrange("p (g d) -> p g d", d=D),
                         m0_W2.rearrange("e (j p) d -> p (e j) d", p=128)).then_inc(s("w2_loaded"), 16)
            sp.dma_start(W2S[1][:, :].rearrange("p (g d) -> p g d", d=D),
                         m1_wd.rearrange("e (j p) d -> p (e j) d", p=128)).then_inc(s("w2_loaded"), 16)

            def attention_loads(b):
                at_least(sp, s("xct_ready"), b)
                sp.dma_start(CS[:, :, :], ctxt[:, ds(b * QB, QB), :]).then_inc(s("c_loaded"), 16)
                at_least(sp, s("w1lo_split"), b)
                sp.dma_start(W1RAW[:, :], m0_W1.rearrange("e d h -> d e h")[:, ds(b, 1), :].rearrange("d e h -> d (e h)")
                             ).then_inc(s("w1raw_loaded"), 16)

            attention_loads(0)
            with sp.Fori(1, B) as b:
                attention_loads(b)
            decoder_loads(sp)
            final_store(sp)

        @block.gpsimd
        def _(pool):
            pool.memset(ident[:, :], 0.0).then_inc(s("pool_const"), 1)
            pool.memset(TRI[:, :], 0.0).then_inc(s("pool_const"), 1)
            pool.memset(ROWS[:, :], 0.0).then_inc(s("rows_zero"), 1)
            pool.memset(WRF[:, :], 0.0).then_inc(s("wrf_zero"), 1)
            pool.memset(HALF[:, :], -0.5)
            pool.memset(ZERO[:, :], 0.0)
            for e in range(E):
                l = pool.memset(RANK[:, :, e:e + 1], float(E - e))
            l.then_inc(s("pool_const"), 1)
            pool.wait_ge(s("pool_const"), 2)
            pool.affine_select(out=ident[:, :], in_=ident[:, :], compare_op=ALU.not_equal, fill=1.0, base=0,
                               pattern=[[-1, 128]], channel_multiplier=1).then_inc(s("ident_ready"), 1)
            pool.affine_select(out=TRI[:, 0:T], in_=TRI[:, 0:T], compare_op=ALU.is_ge, fill=-BIG, base=0,
                               pattern=[[-1, T]], channel_multiplier=1)
            pool.affine_select(out=TRI[:, T:3 * T], in_=TRI[:, T:3 * T], compare_op=ALU.is_ge, fill=-BIG, base=T,
                               pattern=[[-1, N]], channel_multiplier=1).then_inc(s("ident_ready"), 1)
            pool_rstd(pool)
            pool_attention(pool, 0)
            with pool.Fori(1, B) as b:
                pool_attention(pool, b)
            pool_rstd(pool)
            pool_rstd(pool)
            pool_split1(pool)
            pool_rstd(pool)
            pool_rstd(pool)
            pool_rstd(pool)
            pool_rstd(pool)

        @block.scalar
        def _(act):
            act_loads(act)
            act.wait_ge(s("gates_loaded"), 32)
            act.activation(GATE[:, :], GATE[:, :], ACT.Tanh).then_inc(s("gate_ready"), 1)
            for g in (0, 2, 4):
                act.wait_ge(s("wt_ready"), g + 1)
                act.activation(WT[:, g * 512:(g + 1) * 512], P[g][:, :], ACT.Copy).then_inc(s("wt_act"), 1)
            act.activation(WVHI[:, :], RAW[:, 2 * INNER:3 * INNER], ACT.Copy).then_inc(s("wv_act"), 1)
            for k in range(4):
                act.wait_ge(s("g_ready"), k + 1)
                dst = GHI[:, :].rearrange("p (h d) -> p h d", d=D)[:, 8 * (k // 2) + k % 2:8 * (k // 2) + 8:2, :]
                act.activation(dst, P[k][:, :].rearrange("p (h d) -> p h d", d=D), ACT.Copy, scale=DH ** -0.5
                               ).then_inc(s("ghi_done"), 1)
            act.wait_ge(s("cols_done"), 2)
            act.activation(WRHI[:, :], WRF[:, :], ACT.Copy).then_inc(s("wr_act"), 1)
            act_attention(act, 0, True)
            with act.Fori(1, B) as b:
                act_attention(act, b, False)
            act_out(act, B - 1, PAIRS - 1)
            act_mixture(act, 0)
            act_decoder(act)
            act_mixture(act, 1)

        @block.vector
        def _(dve):
            open_counts(dve)
            dve.wait_ge(s("x_loaded"), 16 * CHUNKS)
            dve.wait_ge(s("pool_const"), 3)
            dve_stats(dve, X)
            dve.wait_ge(s("ident_ready"), 2)
            for g in (1, 3, 5):
                dve.wait_ge(s("wt_ready"), g + 1)
                dve.tensor_copy(WT[:, g * 512:(g + 1) * 512], P[g][:, :]).then_inc(s("wt_dve"), 1)
            dve.wait_ge(s("wv_act"), 1)
            dve.tensor_tensor(WVLO[:, :], RAW[:, 2 * INNER:3 * INNER], WVHI[:, :].bitcast(f32), ALU.subtract
                              ).then_inc(s("wv_dve"), 1)
            for k in range(4):
                dve.wait_ge(s("ghi_done"), k + 1)
                sel = (slice(None), slice(8 * (k // 2) + k % 2, 8 * (k // 2) + 8, 2), slice(None))
                dve.scalar_tensor_tensor(out=GLO[:, :].rearrange("p (h d) -> p h d", d=D)[sel],
                                         in0=P[k][:, :].rearrange("p (h d) -> p h d", d=D), scalar=DH ** -0.5,
                                         in1=GHI[:, :].bitcast(f32).rearrange("p (h d) -> p h d", d=D)[sel],
                                         op0=ALU.mult, op1=ALU.subtract).then_inc(s("glo_done"), 1)
            dve.wait_ge(s("wvo_ready"), 1)
            dve.tensor_scalar(WVO[:, :], P[4][:, 0:D], 1.0 / N, None, ALU.mult).then_inc(s("wvo_done"), 1)
            dve.wait_ge(s("cols_ready"), 1)
            dve.tensor_copy(COLS[:, :], P[6][:, 0:128]).then_inc(s("cols_done"), 1)
            dve.wait_ge(s("cols_done"), 1)
            dve.wait_ge(s("wr_loaded"), 16)
            dve.tensor_copy(WRF[:, 128:128 + E], COLS[:, 64:64 + E]).then_inc(s("cols_done"), 1)
            dve.wait_ge(s("wr_act"), 1)
            dve.tensor_tensor(WRLO[:, :], WRF[:, :], WRHI[:, :].bitcast(f32), ALU.subtract).then_inc(s("wr_split"), 1)
            dve.wait_ge(s("bcast_loaded"), BCASTS)
            dve.wait_ge(s("gate_ready"), 1)
            dve.tensor_scalar(TGBO[:, :], BC[:, 0, :], GATE[:, 0:1], None, ALU.mult).then_inc(s("wr_split"), 1)
            dve.wait_ge(s("wr_split"), 2)
            dve.wait_ge(s("mask_loaded"), 16)
            dve_attention(dve, 0, True)
            with dve.Fori(1, B) as b:
                dve_attention(dve, b, False)
            dve_probs(dve, B - 1, PAIRS - 1)
            dve_tail(dve, B - 1)
            dve.wait_ge(s("tail_done"), B)
            dve_mixture(dve, 0)
            dve_decoder(dve)
            dve_mixture(dve, 1)

        @block.tensor
        def _(pe):
            pe.wait_ge(s("ident_ready"), 1)
            pe.wait_ge(s("proj_loaded"), 48)
            for g in range(6):
                for k in range(4):
                    c = g * 512 + k * 128
                    l = pe.transpose(P[g][:, k * 128:(k + 1) * 128], RAW[:, c:c + 128], ident[:, :])
                l.then_inc(s("wt_ready"), 1)
            pe.wait_ge(s("rows_loaded"), 48)
            pe.transpose(P[6][:, 0:128], ROWS[:, :], ident[:, :]).then_inc(s("cols_ready"), 1)
            pe.wait_ge(s("wt_act"), 3)
            pe.wait_ge(s("wt_dve"), 3)
            for k in range(4):
                r = (k % 2) * DH
                for j in range(4):
                    c = (4 * (k // 2) + j) * 128
                    l = pe.matmul(P[k][:, j * D:(j + 1) * D], WT[r:r + DH, INNER + c:INNER + c + 128],
                                  WT[r:r + DH, c:c + 128], start=True, stop=True)
                l.then_inc(s("g_ready"), 1)
            pe.wait_ge(s("wo_loaded"), 16)
            for c in range(PAIRS):
                l = pe.matmul(P[4][:, 0:D], WT[:, 2 * INNER + c * 128:2 * INNER + (c + 1) * 128], WOS[:, c, :],
                              start=c == 0, stop=c == PAIRS - 1)
            l.then_inc(s("wvo_ready"), 1)
            pe.wait_ge(s("glo_done"), 4)
            pe.wait_ge(s("wv_dve"), 1)
            pe.wait_ge(s("wvo_done"), 1)
            pe.wait_ge(s("cols_done"), 1)
            pe_attention(pe, 0, True)
            with pe.Fori(1, B) as b:
                pe_attention(pe, b, False)
            pe_transpose_probs(pe, B - 1, PAIRS - 1)
            pe_project(pe, B - 1, PAIRS - 2)
            pe_values(pe, B - 1, PAIRS - 1)
            pe_project(pe, B - 1, PAIRS - 1)
            pe.wait_ge(s("tail_done"), B)
            pe.wait_ge(s("wr_split"), 2)
            pe.wait_ge(s("w1lo_split"), E)
            pe.wait_ge(s("w2_loaded"), 32)
            pe.wait_ge(s("bcast_loaded"), BCASTS)
            pe_mixture(pe, 0)
            pe.wait_ge(s("l1w_loaded"), 32)
            pe_decoder(pe)
            pe.wait_ge(s("dfin"), ONE + B)
            pe.wait_ge(s("w1lo_split1"), ONE + E)
            pe_mixture(pe, 1)


_ARGS = ['x', 'ctx_1024', 'mask_BxS2_bf0', 'g_xattn', 'g_ffn', 'L0_xattn_Wq', 'L0_xattn_Wk', 'L0_xattn_Wv',
         'L0_xattn_Wo', 'L0_xattn_bo', 'L0_ffn_W1', 'L0_ffn_b1', 'L0_ffn_W2', 'L0_ffn_b2', 'L0_ffn_Wr', 'L0_ffn_br',
         'L1_xattn_w1', 'L1_xattn_b1', 'L1_xattn_w2', 'L1_xattn_b2', 'L1_xattn_g1', 'L1_xattn_beta1', 'L1_xattn_g2',
         'L1_xattn_beta2', 'L1_xattn_g3', 'L1_xattn_beta3', 'L1_ffn_gate_w', 'L1_ffn_w_gate', 'L1_ffn_w_up',
         'L1_ffn_w_down']


def kernel(**inputs):
    import numpy as np
    import concourse.bacc as bacc
    from concourse import mybir as mb
    from concourse.bass_utils import run_bass_kernel_spmd

    nc = bacc.Bacc("TRN2", target_bir_lowering=False, num_devices=1)
    arrays, args = {}, []
    for name in _ARGS:
        a = np.ascontiguousarray(inputs[name])
        arrays[f"in_{name}"] = a
        args.append(nc.dram_tensor(f"in_{name}", a.shape, mb.dt.from_np(a.dtype), kind="ExternalInput").ap())
    out = nc.dram_tensor("out_x", (B, N, D), f32, kind="ExternalOutput").ap()
    build(nc, *args, out)
    r = run_bass_kernel_spmd(nc, [arrays], core_ids=[0])
    return r.results[0]["out_x"]
```

```python
import math

import concourse.bass as bass
from concourse import mybir
from contextlib import ExitStack

f32 = mybir.dt.float32
f32r = mybir.dt.float32r
u8 = mybir.dt.uint8
ALU = mybir.AluOpType
ACT = mybir.ActivationFunctionType
AX = mybir.AxisListType

B, N, D = 8, 256, 128
HEADS, DH = 16, 64
PAIRS = HEADS // 2
INNER = HEADS * DH
E, H = 8, 256
DFF = 512
T = 128
QB = N // T
TILES = B * QB
CH = 4
CHUNKS = TILES // CH
W = CH * T
U = 4
ONE = 1
H0 = 2
EPS = 1e-5
BIG = 1e30
HUGE = 3e38


def ds(start, size):
    return bass.ds(start, size)


def at_least(eng, sem, value):
    if isinstance(value, int) and value <= 0:
        return
    eng.wait_ge(sem, value)


def waits_alone(eng, const, *waits):
    held = [(sem, value if isinstance(value, int) else eng.to_reg(value)) for sem, value in waits]
    eng.wait_ge(const, 1)
    for sem, value in held:
        at_least(eng, sem, value)


def build(nc, x, ctx_in, mask, g_xattn, g_ffn, Wq, Wk, Wv, Wo, bo, m0_W1, m0_b1, m0_W2, m0_b2, m0_Wr, m0_br,
          w1, b1, w2, b2, g1, beta1, g2, beta2, g3, beta3, m1_gate, m1_wg, m1_wu, m1_wd, out):
    stack = ExitStack()
    with stack:
        def sb(name, shape, dt=f32):
            return stack.enter_context(nc.sbuf_tensor(name, shape, dt))

        def sem(name):
            return stack.enter_context(nc.semaphore(name))

        P = [stack.enter_context(nc.psum_tensor(f"bank{i}", [128, 512], f32)) for i in range(8)]

        X = sb("X", [128, TILES * D])
        MV = sb("MV", [128, TILES, 2])
        RSTD = sb("RSTD", [128, TILES])
        HALF = sb("HALF", [128, 8])
        EULER = sb("EULER", [128, CH])
        EPS2 = sb("EPS2", [128, 8, 2])
        STAT = sb("STAT", [128, 8 * 6])
        AGGR = sb("AGGR", [128, 8, 2])
        ident = sb("ident", [128, 128])
        TRI = sb("TRI", [128, 3 * T])
        ZERO = sb("ZERO", [128, N])
        GATE = sb("GATE", [128, 4])
        BC = sb("BC", [128, 8, D])
        ROWS = sb("ROWS", [128, 128])
        COLS = sb("COLS", [128, 128])
        RAW = sb("RAW", [128, 3 * INNER])
        WT = sb("WT", [128, 3 * INNER])
        SPLITS = sb("SPLITS", [128, 9216], f32r)
        GHI = SPLITS[:, 0:2048]
        GLO = SPLITS[:, 2048:4096]
        WVHI = SPLITS[:, 4096:5120]
        WVLO = SPLITS[:, 5120:6144]
        WOS = sb("WOS", [128, PAIRS, D])
        WVO = sb("WVO", [128, D])
        MASK = sb("MASK", [128, B * N], u8)
        MB = sb("MB", [128, 3 * T])
        XN = sb("XN", [128, N])
        CS = sb("CS", [128, QB, D])
        XCHI = SPLITS[:, 6144:6656]
        XCLO = SPLITS[:, 6656:7168]
        CBAR = sb("CBAR", [128, 1])
        CBARB = sb("CBARB", [128, 128])
        KHI = [SPLITS[:, 7168 + 512 * i:7680 + 512 * i] for i in range(2)]
        KLO = [SPLITS[:, 8192 + 512 * i:8704 + 512 * i] for i in range(2)]
        ARENA = sb("ARENA", [128, 6144])
        VB = ARENA[:, 0:2048].rearrange("p (q c) -> p q c", q=QB)
        SP = [ARENA[:, 2048 + 768 * i:2816 + 768 * i] for i in range(2)]
        NEGM = [sb(f"NEGM{i}", [128, 4]) for i in range(2)]
        RSUM = [sb(f"RSUM{i}", [128, 4]) for i in range(2)]
        RCP = [sb(f"RCP{i}", [128, 4]) for i in range(2)]
        PT = [ARENA[:, 3584 + 384 * i:3968 + 384 * i] for i in range(2)]
        OT = ARENA[:, 4352:4608]
        TGBO = sb("TGBO", [128, D])
        NKEEP = sb("NKEEP", [128, 2])
        FCOL = sb("FCOL", [128, 2])
        GCOL = sb("GCOL", [128, 2])
        XTHI = sb("XTHI", [128, TILES * T], f32r)
        XTLO = sb("XTLO", [128, TILES * T], f32r)
        W1RAW = sb("W1RAW", [128, 2 * H])
        W1HI = [sb("W1HI", [128, E * 2 * H], f32r), SPLITS[:, 0:E * 2 * H]]
        W1LO = [sb("W1LO", [128, E * 2 * H], f32r), SPLITS[:, E * 2 * H:2 * E * 2 * H]]
        W2S = [sb(f"W2S{m}", [128, E * 2 * D]) for m in range(2)]
        B2S = sb("B2S", [E, D])
        WRF = sb("WRF", [128, 2 * 128])
        WRHI = sb("WRHI", [128, 2 * 128], f32r)
        WRLO = sb("WRLO", [128, 2 * 128], f32r)
        BRB = sb("BRB", [128, E])
        HT = [ARENA[:, 1024 * k:1024 * (k + 1)].rearrange("p (j t) -> p j t", j=2) for k in range(2)]
        SIL = [ARENA[:, 2048 + W * j:2048 + W * (j + 1)] for j in range(2)]
        ACC = ARENA[:, 3072:3584]
        XNS = ARENA[:, 3584:3584 + W]
        LTS = ARENA[:, 4608:4608 + W]
        LG = sb("LG", [128, CH, E])
        RANK = sb("RANK", [128, CH, E])
        RT = [sb(f"RT{k}", [128, CH, E]) for k in range(2)]
        RV = [sb(f"RV{k}", [128, CH]) for k in range(6)]
        WGT = sb("WGT", [128, CH, E])
        WSL = sb("WSL", [128, CH * E])
        WTS = sb("WTS", [E, W])
        L1W1 = sb("L1W1", [128, DFF])
        L1W2 = sb("L1W2", [128, DFF // 128, D])
        UP = ARENA[:, 0:2048]
        YS = ARENA[:, 2048:3072]
        CU = ARENA[:, 3072:4096].rearrange("p (u q d) -> p u q d", u=U, q=QB)
        YR = ARENA[:, 4096:6144]
        UNEG = sb("UNEG", [128, U * QB])
        USUM = sb("USUM", [128, U * QB])
        URCP = sb("URCP", [128, U * QB])
        YT = RAW[:, 0:U * 512]
        UPT = WT[:, 0:U * 512]
        HL = WT

        block = stack.enter_context(nc.Block())
        S = {}

        def s(name):
            if name not in S:
                S[name] = sem(name)
            return S[name]

        TICK = sb("TICK", [128, 32])
        COUNTED = ["stat_done", "aggr_done", "mv_done", "dav_ready", "dres_done", "dfin", "dff_ready"]
        COUNTED += [f"m{m}_{name}" for m in range(2) for name in ("chunk_done", "acc_chain")]

        def open_counts(eng):
            for k, name in enumerate(COUNTED):
                eng.memset(TICK[:, k:k + 1], 0.0).then_inc(s(name), ONE)
            for m in range(2):
                eng.memset(TICK[:, 16 + m:17 + m], 0.0).then_inc(s(f"m{m}_h_done"), H0)

        for name in ("x_loaded proj_loaded wo_loaded rows_loaded bcast_loaded mask_loaded gates_loaded wr_loaded "
                     "w2_loaded l1w_loaded out_stored pool_const ident_ready rows_zero wrf_zero "
                     "stat_done aggr_done mv_done rstd_ready gate_ready cbar_sum "
                     "wt_ready wt_act wt_dve cols_ready cols_done g_ready ghi_done glo_done wvo_ready wvo_done wr_split wr_act wv_act wv_dve "
                     "xn_ready c_loaded xct_ready xchi_done xclo_done mb_ready cbar_done "
                     "neg_kept kp_ready khi_done klo_done v_ready v_done s0_ready s1_ready neg_done exp_done recip_done norm_done "
                     "ta_ready tb_ready pta_done ptb_done ot_ready ot_done acc_ready tail_chain tail_done "
                     "w1raw_loaded w1hi_split w1lo_split w1raw_loaded1 w1hi_split1 w1lo_split1").split():
            s(name)

        xt = x.rearrange("b (q p) d -> p (b q) d", p=T)
        outt = out.rearrange("b (q p) d -> p (b q) d", p=T)
        ctxt = ctx_in.rearrange("b (q p) d -> p (b q) d", p=T)

        def row(v):
            return v.rearrange("(a n) -> a n", a=1)

        def act_loads(act):
            act.dma_start(GATE[:, 0:2], row(g_xattn).partition_broadcast(128)).then_inc(s("gates_loaded"), 16)
            act.dma_start(GATE[:, 2:4], row(g_ffn).partition_broadcast(128)).then_inc(s("gates_loaded"), 16)
            act.dma_start(MASK[:, :], mask.rearrange("(a b) n -> a (b n)", a=1).partition_broadcast(128)
                          ).then_inc(s("mask_loaded"), 16)
            for k, v in enumerate((bo, g1, beta1, g2, beta2, g3, beta3, b2)):
                act.dma_start(BC[:, k, :], row(v).partition_broadcast(128)).then_inc(s("bcast_loaded"), 16)
            act.dma_start(BRB[:, :], row(m0_br).partition_broadcast(128)).then_inc(s("bcast_loaded"), 16)
            act.dma_start(B2S[:, :], m0_b2).then_inc(s("bcast_loaded"), 16)
            act.wait_ge(s("rows_zero"), 1)
            act.dma_start(ROWS[0:32, :], m0_b1.rearrange("e (c p) -> (e c) p", p=128)).then_inc(s("rows_loaded"), 16)
            act.dma_start(ROWS[32:36, :], b1.rearrange("(c p) -> c p", p=128)).then_inc(s("rows_loaded"), 16)
            act.dma_start(ROWS[64:72, :], m1_gate).then_inc(s("rows_loaded"), 16)
            act.wait_ge(s("wrf_zero"), 1)
            act.dma_start(WRF[:, 0:E], m0_Wr).then_inc(s("wr_loaded"), 16)

        BCASTS = 10 * 16

        bK, bV, bS0, bS1, bO, bA = P[0], P[1], P[2], P[3], P[6], P[7]
        bT = (P[4], P[5])

        def pe_proj(pe, b, hp):
            n = b * PAIRS + hp
            if hp == 0:
                pe.wait_ge(s("xclo_done"), b + 1)
            at_least(pe, s("klo_done"), n)
            for h in range(2):
                g = ds((2 * hp + h) * D, D)
                for k, (l, r) in enumerate(((GHI, XCHI), (GHI, XCLO), (GLO, XCHI))):
                    last = pe.matmul(bK[:, h * N:(h + 1) * N], l[:, g], r[:, 0:N], start=k == 0, stop=k == 2)
            last.then_inc(s("kp_ready"), 1)
            if hp % 2 == 0:
                at_least(pe, s("v_done"), b * (PAIRS // 2) + hp // 2)
                cols = ds(hp * 128, 256)
                for q in range(QB):
                    t = ds(q * T, T)
                    for k, (l, r) in enumerate(((XCHI, WVHI), (XCHI, WVLO), (XCLO, WVHI))):
                        last = pe.matmul(bV[:, q * 256:(q + 1) * 256], l[:, t], r[:, cols], start=k == 0, stop=k == 2)
                last.then_inc(s("v_ready"), 1)

        def pe_scores(pe, b, hp):
            n = b * PAIRS + hp
            pe.wait_ge(s("klo_done"), n + 1)
            at_least(pe, s("neg_done"), 4 * n)
            kh, kl = KHI[hp % 2], KLO[hp % 2]

            def first_keys(t):
                return t[:, :].rearrange("p (h k) -> p h k", h=2)[:, :, 0:T]

            q0, q1 = ds(N, T), ds(N + T, T)
            o0 = bS0[:, 0:2 * T].rearrange("p (h k) -> p h k", h=2)
            for k, (l, r) in enumerate(((XCHI, kh), (XCHI, kl), (XCLO, kh))):
                last = pe.matmul(o0, l[:, q0], first_keys(r), start=k == 0, stop=k == 2)
            last.then_inc(s("s0_ready"), 1)
            for k, (l, r) in enumerate(((XCHI, kh), (XCHI, kl), (XCLO, kh))):
                last = pe.matmul(bS1[:, :], l[:, q1], r[:, :], start=k == 0, stop=k == 2)
            last.then_inc(s("s1_ready"), 1)

        def pe_transpose_probs(pe, b, hp):
            n = b * PAIRS + hp
            pe.wait_ge(s("norm_done"), n + 1)
            p = SP[hp % 2]
            for h, ready, done in ((0, "ta_ready", "pta_done"), (1, "tb_ready", "ptb_done")):
                at_least(pe, s(done), n)
                for k, c in enumerate((h * T, 2 * T + h * N, 2 * T + h * N + T)):
                    last = pe.transpose(bT[h][:, k * T:(k + 1) * T], p[:, c:c + T], ident[:, :])
                last.then_inc(s(ready), 1)

        def pe_values(pe, b, hp):
            n = b * PAIRS + hp
            if hp % 2 == 0:
                pe.wait_ge(s("v_done"), b * (PAIRS // 2) + hp // 2 + 1)
            pe.wait_ge(s("pta_done"), n + 1)
            pe.wait_ge(s("ptb_done"), n + 1)
            at_least(pe, s("ot_done"), n)
            for k in range(QB):
                for h in range(2):
                    v = VB[:, k, (2 * hp + h) * DH:(2 * hp + h + 1) * DH]
                    probs = PT[h][:, 0:N] if k == 0 else PT[h][:, N:N + T]
                    last = pe.matmul(bO[h * DH:(h + 1) * DH, k * T:N], v, probs, start=k == 0, stop=k == 1,
                                     skip_group_check=True)
            last.then_inc(s("ot_ready"), 1)

        def pe_uniform(pe, b):
            at_least(pe, s("tail_done"), b)
            pe.wait_ge(s("cbar_done"), b + 1)
            pe.matmul(bA[:, N:N + D], CBARB[:, :], WVO[:, :], start=True, stop=True, skip_group_check=True)

        def pe_project(pe, b, hp):
            n = b * PAIRS + hp
            pe.wait_ge(s("ot_done"), n + 1)
            for q in range(QB):
                last = pe.matmul(bA[:, q * D:(q + 1) * D], OT[:, q * T:(q + 1) * T], WOS[:, hp, :], start=False,
                                 stop=hp == PAIRS - 1, skip_group_check=True)
            if hp == PAIRS - 1:
                last.then_inc(s("acc_ready"), 1)

        def pe_operands(pe, b):
            pe.wait_ge(s("xn_ready"), b + 1)
            pe.wait_ge(s("c_loaded"), 16 * (b + 1))
            at_least(pe, s("klo_done"), b * PAIRS)
            for k in range(QB):
                pe.transpose(bK[:, k * T:(k + 1) * T], CS[:, k, :], ident[:, :])
            for k in range(QB):
                last = pe.transpose(bK[:, N + k * T:N + (k + 1) * T], XN[:, k * T:(k + 1) * T], ident[:, :])
            last.then_inc(s("xct_ready"), 1)

        def pe_attention(pe, b, first, final):
            pe_proj(pe, b, 0)
            if not first:
                pe_values(pe, b - 1, PAIRS - 2)
            for hp in range(PAIRS):
                pe_scores(pe, b, hp)
                if hp < PAIRS - 1:
                    pe_proj(pe, b, hp + 1)
                elif not final:
                    pe_operands(pe, b + 1)
                if hp >= 2:
                    pe_values(pe, b, hp - 2)
                elif hp == 1 and not first:
                    pe_values(pe, b - 1, PAIRS - 1)
                if hp >= 1:
                    pe_transpose_probs(pe, b, hp - 1)
                elif not first:
                    pe_transpose_probs(pe, b - 1, PAIRS - 1)
                if hp == 2:
                    pe_uniform(pe, b)
                if hp >= 2:
                    pe_project(pe, b, hp - 2)
                elif not first:
                    pe_project(pe, b - 1, PAIRS - 2 + hp)

        def act_k_hi(act, b, hp):
            n = b * PAIRS + hp
            act.wait_ge(s("kp_ready"), n + 1)
            act.activation(KHI[hp % 2][:, :], bK[:, :], ACT.Copy).then_inc(s("khi_done"), 1)

        def act_v(act, b, hp):
            act.wait_ge(s("v_ready"), b * (PAIRS // 2) + hp // 2 + 1)
            act.activation(VB[:, :, hp * 128:hp * 128 + 256], bV[:, :].rearrange("p (q c) -> p q c", q=QB),
                           ACT.Copy).then_inc(s("v_done"), 1)

        def act_out(act, b, hp):
            act.wait_ge(s("ot_ready"), b * PAIRS + hp + 1)
            act.activation(OT[:, :], bO[:, 0:N], ACT.Copy).then_inc(s("ot_done"), 1)

        BLOCKS = ((0, T, 0), (T, T, 1), (2 * T, N, 2), (2 * T + N, N, 3))

        def act_operands(act, b):
            act.wait_ge(s("xct_ready"), b + 1)
            act.activation(XCHI[:, :], bK[:, :], ACT.Copy).then_inc(s("xchi_done"), 1)

        def act_attention(act, b, first, final):
            act_k_hi(act, b, 0)
            act_v(act, b, 0)
            if not first:
                act_out(act, b - 1, PAIRS - 2)
            for hp in range(PAIRS):
                n = b * PAIRS + hp
                k = hp % 2
                for c, w, i in BLOCKS:
                    if i == 2:
                        if hp < PAIRS - 1:
                            act_k_hi(act, b, hp + 1)
                        elif not final:
                            act_operands(act, b + 1)
                    if i == 3 and hp % 2 == 1 and hp < PAIRS - 1:
                        act_v(act, b, hp + 1)
                    act.wait_ge(s("neg_done"), 4 * n + i + 1)
                    act.activation(SP[k][:, c:c + w], SP[k][:, c:c + w], ACT.Exp, bias=NEGM[k][:, i:i + 1],
                                   scale=-1.0, accum_out=RSUM[k][:, i:i + 1]).then_inc(s("exp_done"), 1)
                if hp >= 2:
                    act_out(act, b, hp - 2)
                elif hp == 1 and not first:
                    act_out(act, b - 1, PAIRS - 1)

        def dve_k_lo(dve, b, hp):
            n = b * PAIRS + hp
            dve.wait_ge(s("khi_done"), n + 1)
            dve.tensor_tensor(KLO[hp % 2][:, :], bK[:, :], KHI[hp % 2][:, :].bitcast(f32), ALU.subtract
                              ).then_inc(s("klo_done"), 1)

        def dve_probs(dve, b, hp):
            n = b * PAIRS + hp
            for h, ready, done in ((0, "ta_ready", "pta_done"), (1, "tb_ready", "ptb_done")):
                dve.wait_ge(s(ready), n + 1)
                dve.tensor_copy(PT[h][:, :], bT[h][:, 0:3 * T]).then_inc(s(done), 1)

        def dve_bias(dve, b):
            x3 = X[:, ds(b * N, N)].rearrange("p (q d) -> p q d", q=QB)
            dve.tensor_tensor(x3, x3, TGBO[:, :].unsqueeze(1).to_broadcast([128, QB, D]), ALU.add
                              ).then_inc(s("tail_chain"), 1)

        def dve_tail(dve, b):
            c = s("tail_chain")
            base = b * 4 + 2
            dve.wait_ge(s("acc_ready"), b + 1)
            dve.wait_ge(c, base + 1)
            for q in range(QB):
                xq = X[:, ds(b * N + q * D, D)]
                i = dve.scalar_tensor_tensor(out=xq, in0=bA[:, q * D:(q + 1) * D], scalar=GCOL[:, q:q + 1], in1=xq,
                                             op0=ALU.mult, op1=ALU.add)
            i.then_inc(c, 1)
            dve.wait_ge(c, base + 2)
            for q in range(QB):
                xq = X[:, ds(b * N + q * D, D)]
                i = dve.scalar_tensor_tensor(out=xq, in0=bA[:, N:N + D], scalar=FCOL[:, q:q + 1], in1=xq,
                                             op0=ALU.mult, op1=ALU.add)
            i.then_inc(s("tail_done"), 1)

        def dve_flags(dve, b):
            c = s("tail_chain")
            at_least(dve, s("tail_done"), b)
            dve.wait_ge(s("neg_kept"), b + 1)
            dve.tensor_scalar(FCOL[:, :], NKEEP[:, :], BIG / 10, GATE[:, 0:1], ALU.is_ge, ALU.mult).then_inc(c, 1)
            dve.wait_ge(c, b * 4 + 1)
            dve.tensor_scalar(GCOL[:, :], FCOL[:, :], -1.0, GATE[:, 0:1], ALU.mult, ALU.add).then_inc(c, 1)

        def dve_normalise(dve, b):
            at_least(dve, s("xct_ready"), b)
            for q in range(QB):
                i = dve.tensor_scalar(XN[:, q * D:(q + 1) * D], X[:, ds(b * N + q * D, D)],
                                      MV[:, ds(b * QB + q, 1), 0:1].rearrange("p a c -> p (a c)"),
                                      RSTD[:, ds(b * QB + q, 1)], ALU.subtract, ALU.mult)
            i.then_inc(s("xn_ready"), 1)

        def dve_operands(dve, b):
            dve.wait_ge(s("xchi_done"), b + 1)
            at_least(dve, s("cbar_done"), b)
            dve.reduce_sum(CBAR[:, :], bK[:, 0:N], AX.X).then_inc(s("cbar_sum"), 1)
            dve.tensor_tensor(XCLO[:, :], bK[:, :], XCHI[:, :].bitcast(f32), ALU.subtract).then_inc(s("xclo_done"), 1)

        def dve_attention(dve, b, first, final):
            at_least(dve, s("neg_done"), 4 * b * PAIRS)
            for lo, n, k in ((0, T, 0), (T, N, 0)):
                i = dve.scalar_tensor_tensor(out=MB[:, lo:lo + n], in0=MASK[:, ds(b * N, n)], scalar=-BIG,
                                             in1=TRI[:, lo:lo + n], op0=ALU.mult, op1=ALU.add)
            i.then_inc(s("mb_ready"), 1)
            dve_k_lo(dve, b, 0)
            for hp in range(PAIRS):
                n = b * PAIRS + hp
                k = hp % 2
                waits_alone(dve, s("ident_ready"), (s("tb_ready"), n - 1), (s("mb_ready"), b + 1), (s("s0_ready"), n + 1))
                for c, w, i in BLOCKS:
                    if i == 2:
                        waits_alone(dve, s("ident_ready"), (s("s1_ready"), n + 1))
                    bank, bc = (bS0, c) if i < 2 else (bS1, c - 2 * T)
                    m = MB[:, 0:T] if i < 2 else MB[:, T:3 * T]
                    dve.tensor_tensor_reduce(out=SP[k][:, c:c + w], in0=bank[:, bc:bc + w], in1=m, scale=-1.0, scalar=HUGE,
                                             op0=ALU.add, op1=ALU.min, accum_out=NEGM[k][:, i:i + 1]
                                             ).then_inc(s("neg_done"), 1)
                if hp == 2 and not first:
                    dve_tail(dve, b - 1)
                if hp < PAIRS - 1:
                    dve_k_lo(dve, b, hp + 1)
                elif not final:
                    dve_operands(dve, b + 1)
                if hp == 0:
                    dve.wait_ge(s("neg_done"), 4 * n + 4)
                    dve.tensor_copy(NKEEP[:, :], NEGM[0][:, 0:4:2]).then_inc(s("neg_kept"), 1)
                if hp == 1:
                    if not first:
                        dve_bias(dve, b - 1)
                    dve.wait_ge(s("cbar_sum"), b + 1)
                    dve.tensor_scalar(CBARB[:, :], ZERO[:, 0:128], 1.0, CBAR[:, 0:1], ALU.mult, ALU.add
                                      ).then_inc(s("cbar_done"), 1)
                if hp == 2:
                    dve_flags(dve, b)
                dve.wait_ge(s("exp_done"), 4 * (n + 1))
                dve.reciprocal(RCP[k][:, :], RSUM[k][:, :]).then_inc(s("recip_done"), 1)
                if hp >= 1:
                    dve_probs(dve, b, hp - 1)
                elif not first:
                    dve_probs(dve, b - 1, PAIRS - 1)
                if hp == 3 and not first:
                    dve_stats(dve, X, (b - 1) * QB, QB, CHUNKS + b - 1, (s("tail_done"), b))
                if hp == PAIRS - 2 and not final:
                    dve_normalise(dve, b + 1)

        def pool_attention(pool, b, first):
            for hp in range(PAIRS):
                n = b * PAIRS + hp
                k = hp % 2
                waits_alone(pool, s("ident_ready"), (s("recip_done"), n + 1))
                for c, w, i in BLOCKS:
                    last = pool.tensor_scalar(SP[k][:, c:c + w], SP[k][:, c:c + w], RCP[k][:, i:i + 1], 1.0,
                                              ALU.mult, ALU.mult)
                last.then_inc(s("norm_done"), 1)
                w1e = ds(b * 2 * H, 2 * H)
                if hp == 4 and not first:
                    pool_rstd(pool, (b - 1) * QB, QB, CHUNKS + b - 1)
                if hp == 2:
                    pool.wait_ge(s("w1raw_loaded"), 16 * (b + 1))
                    pool.tensor_copy(W1HI[0][:, w1e], W1RAW[:, :]).then_inc(s("w1hi_split"), 1)
                if hp == 5:
                    pool.wait_ge(s("w1hi_split"), b + 1)
                    pool.tensor_tensor(W1LO[0][:, w1e], W1RAW[:, :], W1HI[0][:, w1e].bitcast(f32), ALU.subtract
                                       ).then_inc(s("w1lo_split"), 1)

        G_START = 0
        G_ATT = G_START + CHUNKS
        G_MIX = G_ATT + B
        TURNS = B // U
        G_SELF = G_MIX + CHUNKS
        G_CROSS = G_SELF + TURNS
        G_FF = G_CROSS + TURNS
        G_DEC = G_FF + TURNS
        G_END = G_DEC + TURNS

        def dve_stats(dve, src, tile, n, g, written=None):
            cols = lambda t: src[:, ds((tile + t) * D, D)]
            waits_alone(dve, s("ident_ready"), (s("aggr_done"), ONE + g), *([written] if written else []))
            for t in range(n):
                l = dve.bn_stats(STAT[:, t * 6:(t + 1) * 6], cols(t))
            l.then_inc(s("stat_done"), 1)
            waits_alone(dve, s("ident_ready"), (s("stat_done"), ONE + g + 1), (s("mv_done"), ONE + g))
            for t in range(n):
                l = dve.bn_aggr(AGGR[:, t, :], STAT[:, t * 6:(t + 1) * 6])
            l.then_inc(s("aggr_done"), 1)
            waits_alone(dve, s("ident_ready"), (s("aggr_done"), ONE + g + 1))
            dve.tensor_tensor(MV[:, ds(tile, n), :], AGGR[:, 0:n, :], EPS2[:, 0:n, :], ALU.add).then_inc(s("mv_done"), 1)

        def pool_rstd(pool, tile, n, g):
            waits_alone(pool, s("ident_ready"), (s("mv_done"), ONE + g + 1))
            pool.tensor_tensor(RSTD[:, ds(tile, n)], MV[:, ds(tile, n), 1:2].rearrange("p t c -> p (t c)"), HALF[:, 0:n],
                               ALU.pow).then_inc(s("rstd_ready"), 1)

        for m in range(2):
            for name in ("n_ready xt_ready xthi_done xtlo_done lt_ready lt_done lg_ready lg_done route exp_ready "
                         "w_ready wsl_done wt_ready wt_done b2_ready up_a up_g sil_done h_done y_ready acc_chain "
                         "chunk_done").split():
                s(f"m{m}_{name}")
        ROUTE = 18
        DIFF_STEP = 12
        LAST = E - 1

        def dve_next_normalised(dve, m, c, groups):
            dve.wait_ge(s("rstd_ready"), groups)
            at_least(dve, s(f"m{m}_xt_ready"), c)
            for t in range(CH):
                tile = c * CH + t
                l = dve.tensor_scalar(XNS[:, t * D:(t + 1) * D], X[:, ds(tile * D, D)],
                                      MV[:, ds(tile, 1), 0:1].rearrange("p a c -> p (a c)"),
                                      RSTD[:, ds(tile, 1)], ALU.subtract, ALU.mult)
            l.then_inc(s(f"m{m}_n_ready"), 1)

        def pe_next_transposed(pe, m, c):
            pe.wait_ge(s(f"m{m}_n_ready"), c + 1)
            at_least(pe, s(f"m{m}_lg_done"), c)
            if m == 0:
                at_least(pe, s(f"m{m}_wt_done"), c)
            for t in range(CH):
                l = pe.transpose(P[6][:, t * T:(t + 1) * T], XNS[:, t * D:(t + 1) * D], ident[:, :])
            l.then_inc(s(f"m{m}_xt_ready"), 1)

        def act_next_hi(act, m, c):
            act.wait_ge(s(f"m{m}_xt_ready"), c + 1)
            act.activation(XTHI[:, ds(c * W, W)], P[6][:, :], ACT.Copy).then_inc(s(f"m{m}_xthi_done"), 1)

        def dve_next_lo(dve, m, c):
            cols = ds(c * W, W)
            dve.wait_ge(s(f"m{m}_xthi_done"), c + 1)
            dve.tensor_tensor(XTLO[:, cols], P[6][:, :], XTHI[:, cols].bitcast(f32), ALU.subtract
                              ).then_inc(s(f"m{m}_xtlo_done"), 1)

        def pe_next_logits(pe, m, c):
            wr = slice(m * 128, (m + 1) * 128)
            cols = ds(c * W, W)
            pe.wait_ge(s(f"m{m}_xtlo_done"), c + 1)
            at_least(pe, s(f"m{m}_lt_done"), c)
            if m == 0 and not (isinstance(c, int) and c == 0):
                pe.wait_ge(s(f"m{m}_acc_chain"), ONE + (c - 1) * (E + 1) + 1)
            for n, (l_, r_) in enumerate(((WRHI, XTHI), (WRHI, XTLO), (WRLO, XTHI))):
                l = pe.matmul(P[7][:, :], l_[:, wr], r_[:, cols], start=n == 0, stop=n == 2)
            l.then_inc(s(f"m{m}_lt_ready"), 1)

        def act_next_logits(act, m, c):
            act.wait_ge(s(f"m{m}_lt_ready"), c + 1)
            at_least(act, s(f"m{m}_lg_ready"), c)
            act.activation(LTS[:, :], P[7][:, :], ACT.Copy).then_inc(s(f"m{m}_lt_done"), 1)

        def pe_next_logits_back(pe, m, c):
            pe.wait_ge(s(f"m{m}_lt_done"), c + 1)
            for t in range(CH):
                l = pe.transpose(P[6][:, t * T:(t + 1) * T], LTS[:, t * T:(t + 1) * T], ident[:, :])
            l.then_inc(s(f"m{m}_lg_ready"), 1)

        def dve_next_route(dve, m, c, part):
            chain = s(f"m{m}_route")
            full = [128, CH, E]
            step = [c * ROUTE + (0, 6, DIFF_STEP)[part]]

            def then(i):
                i.then_inc(chain, 1)
                step[0] = step[0] + 1
                dve.wait_ge(chain, step[0])

            def over(v):
                return v[:, :].unsqueeze(2).to_broadcast(full)

            lg, first, second = LG[:, :, :], RT[0][:, :, :], RT[1][:, :, :]
            if part == 0:
                dve.wait_ge(s(f"m{m}_lg_ready"), c + 1)
                src = P[6][:, :].rearrange("p (t c) -> p t c", c=128)[:, :, 0:E]
                bias = BRB[:, :] if m == 0 else ZERO[:, 0:E]
                dve.tensor_tensor(lg, src, bias.unsqueeze(1).to_broadcast(full), ALU.add).then_inc(s(f"m{m}_lg_done"), 1)
                dve.wait_ge(s(f"m{m}_lg_done"), c + 1)
                then(dve.tensor_reduce(RV[0][:, :], lg, AX.X, ALU.max))
                then(dve.tensor_tensor(first, lg, over(RV[0]), ALU.is_equal))
                then(dve.tensor_tensor(first, first, RANK[:, :, :], ALU.mult))
                then(dve.tensor_reduce(RV[1][:, :], first, AX.X, ALU.max))
                then(dve.tensor_tensor(first, first, over(RV[1]), ALU.is_equal))
                then(dve.scalar_tensor_tensor(out=second, in0=first, scalar=-BIG, in1=lg, op0=ALU.mult, op1=ALU.add))
            elif part == 1:
                then(dve.tensor_reduce(RV[2][:, :], second, AX.X, ALU.max))
                then(dve.tensor_tensor(second, second, over(RV[2]), ALU.is_equal))
                then(dve.tensor_tensor(second, second, RANK[:, :, :], ALU.mult))
                then(dve.tensor_reduce(RV[1][:, :], second, AX.X, ALU.max))
                then(dve.tensor_tensor(RV[3][:, :], RV[2][:, :], RV[0][:, :], ALU.subtract))
                then(dve.tensor_tensor(second, second, over(RV[1]), ALU.is_equal))
            else:
                dve.wait_ge(s(f"m{m}_exp_ready"), c + 1)
                then(dve.tensor_scalar(RV[5][:, :], RV[4][:, :], 1.0, None, ALU.add))
                then(dve.reciprocal(RV[5][:, :], RV[5][:, :]))
                then(dve.tensor_tensor(RV[4][:, :], RV[4][:, :], RV[5][:, :], ALU.mult))
                then(dve.tensor_tensor(first, first, over(RV[5]), ALU.mult))
                then(dve.tensor_tensor(second, second, over(RV[4]), ALU.mult))
                then(dve.tensor_tensor(WGT[:, :, :], first, second, ALU.add))

        def pool_second_weight(pool, m, c):
            pool.wait_ge(s(f"m{m}_route"), c * ROUTE + DIFF_STEP - 1)
            pool.tensor_tensor(RV[4][:, :], EULER[:, :], RV[3][:, :], ALU.pow).then_inc(s(f"m{m}_exp_ready"), 1)

        def dve_chunk(dve, m, c, first, final):
            q = lambda name: s(f"m{m}_{name}")
            combs = E + 1 - m
            steps = c * E
            nxt = c + 1
            for e in range(E):
                if e == 2 and not final:
                    dve_next_lo(dve, m, nxt)
                for j in range(2):
                    n = 2 * (steps + e) + j + 1
                    dve.wait_ge(q("sil_done"), n)
                    dve.wait_ge(q("up_g"), n)
                    if m == 0:
                        l = dve.scalar_tensor_tensor(out=HT[e % 2][:, j, :], in0=P[2 * j + 1][:, :],
                                                     scalar=COLS[:, e * 4 + 2 + j:e * 4 + 3 + j], in1=SIL[j][:, :],
                                                     op0=ALU.add, op1=ALU.mult)
                    else:
                        l = dve.tensor_tensor(HT[e % 2][:, j, :], P[2 * j + 1][:, :], SIL[j][:, :], ALU.mult)
                    l.then_inc(q("h_done"), 1)
                if e == 0:
                    if not first:
                        dve_combine(dve, m, c - 1, LAST)
                        dve_update(dve, m, c - 1)
                    dve.wait_ge(q("route"), (c + 1) * ROUTE)
                    dve.wait_ge(q("acc_chain"), ONE + c * combs)
                    dve.tensor_copy(WSL[:, :], WGT[:, :, :].rearrange("p t e -> p (t e)")).then_inc(q("wsl_done"), 1)
                    dve.wait_ge(q("wsl_done"), c + 1)
                    if not first and m == 0:
                        dve_stats(dve, X, (c - 1) * CH, CH, G_MIX + c - 1, (q("chunk_done"), ONE + c))
                if e == 1 and m == 0:
                    dve.wait_ge(q("b2_ready"), c + 1)
                    dve.wait_ge(q("chunk_done"), ONE + c)
                    dve.tensor_copy(ACC[:, :], P[7][:, :]).then_inc(q("acc_chain"), 1)
                if e >= 1:
                    dve_combine(dve, m, c, e - 1)
                if not final:
                    if e == 1:
                        dve_next_normalised(dve, m, nxt, G_MIX if m == 0 else G_END)
                    if e in (4, 5, 6):
                        dve_next_route(dve, m, nxt, e - 4)

        def dve_combine(dve, m, c, e):
            q = lambda name: s(f"m{m}_{name}")
            combs = E + 1 - m
            dve.wait_ge(q("y_ready"), c * E + e + 1)
            dve.wait_ge(q("acc_chain"), ONE + c * combs + e + (combs - E))
            if m == 1 and e == 0:
                dve.wait_ge(q("chunk_done"), ONE + c)
            y = P[4 + e % 2]
            for t in range(CH):
                tok = slice(t * D, (t + 1) * D)
                w = WSL[:, t * E + e:t * E + e + 1]
                if m == 1 and e == 0:
                    l = dve.tensor_scalar(ACC[:, tok], y[:, tok], w, None, ALU.mult)
                else:
                    l = dve.scalar_tensor_tensor(out=ACC[:, tok], in0=y[:, tok], scalar=w, in1=ACC[:, tok],
                                                 op0=ALU.mult, op1=ALU.add)
            l.then_inc(q("acc_chain"), 1)

        def dve_update(dve, m, c):
            dve.wait_ge(s(f"m{m}_acc_chain"), ONE + (c + 1) * (E + 1 - m))
            xc = X[:, ds(c * W, W)]
            dve.scalar_tensor_tensor(out=xc, in0=ACC[:, :], scalar=GATE[:, 2 + m:3 + m], in1=xc,
                                     op0=ALU.mult, op1=ALU.add).then_inc(s(f"m{m}_chunk_done"), 1)

        def dve_mixture(dve, m):
            dve_next_normalised(dve, m, 0, G_ATT + 2 if m == 0 else G_DEC + 1)
            dve_next_lo(dve, m, 0)
            for part in range(3):
                dve_next_route(dve, m, 0, part)
            dve_chunk(dve, m, 0, True, False)
            with dve.Fori(1, CHUNKS - 1) as c:
                dve_chunk(dve, m, c, False, False)
            dve_chunk(dve, m, CHUNKS - 1, False, True)
            dve_combine(dve, m, CHUNKS - 1, LAST)
            dve_update(dve, m, CHUNKS - 1)
            if m == 0:
                dve_stats(dve, X, (CHUNKS - 1) * CH, CH, G_MIX + CHUNKS - 1, (s("m0_chunk_done"), ONE + CHUNKS))

        def pe_up(pe, m, c, e):
            for j in range(2):
                pe.wait_ge(s(f"m{m}_h_done"), H0 + 2 * (c * E + e - 1) + j + 1)
                for bank, col, ready in ((P[2 * j], j, "up_a"), (P[2 * j + 1], 2 + j, "up_g")):
                    wc = slice(e * 2 * H + col * 128, e * 2 * H + (col + 1) * 128)
                    for n, (l_, r_) in enumerate(((W1HI[m], XTHI), (W1HI[m], XTLO), (W1LO[m], XTHI))):
                        l = pe.matmul(bank[:, :], l_[:, wc], r_[:, ds(c * W, W)], start=n == 0, stop=n == 2)
                    l.then_inc(s(f"m{m}_{ready}"), 1)

        def pe_down(pe, m, c, e):
            combs = E + 1 - m
            pe.wait_ge(s(f"m{m}_h_done"), H0 + 2 * (c * E + e) + 2)
            if e >= 2:
                pe.wait_ge(s(f"m{m}_acc_chain"), ONE + c * combs + combs - E + e - 1)
            elif not (isinstance(c, int) and c == 0):
                pe.wait_ge(s(f"m{m}_acc_chain"), ONE + c * combs + e - 1)
            for t in range(CH):
                for j in range(2):
                    l = pe.matmul(P[4 + e % 2][:, t * D:(t + 1) * D], HT[e % 2][:, j, t * T:(t + 1) * T],
                                  W2S[m][:, (2 * e + j) * D:(2 * e + j + 1) * D], start=j == 0, stop=j == 1)
            l.then_inc(s(f"m{m}_y_ready"), 1)

        def pe_chunk(pe, m, c, first, final):
            q = lambda name: s(f"m{m}_{name}")
            nxt = c + 1
            for e in range(E):
                pe_up(pe, m, c, e)
                if e == 0 and not first:
                    pe_down(pe, m, c - 1, LAST)
                if e == 0 and m == 0:
                    pe.wait_ge(q("wsl_done"), c + 1)
                    pe.wait_ge(q("lg_done"), c + 1)
                    for t in range(CH):
                        l = pe.transpose(P[6][0:E, t * T:(t + 1) * T], WSL[:, t * E:(t + 1) * E], ident[:, :])
                    l.then_inc(q("wt_ready"), 1)
                if e == 1 and m == 0:
                    pe.wait_ge(q("wt_done"), c + 1)
                    for t in range(CH):
                        l = pe.matmul(P[7][:, t * D:(t + 1) * D], WTS[:, t * T:(t + 1) * T], B2S[:, :], start=True, stop=True)
                    l.then_inc(q("b2_ready"), 1)
                if e >= 1:
                    pe_down(pe, m, c, e - 1)
                if not final:
                    if e == 1:
                        pe_next_transposed(pe, m, nxt)
                    if e == 2:
                        pe_next_logits(pe, m, nxt)
                    if e == 3:
                        pe_next_logits_back(pe, m, nxt)

        def pe_mixture(pe, m):
            pe_next_transposed(pe, m, 0)
            pe_next_logits(pe, m, 0)
            pe_next_logits_back(pe, m, 0)
            pe_chunk(pe, m, 0, True, False)
            with pe.Fori(1, CHUNKS - 1) as c:
                pe_chunk(pe, m, c, False, False)
            pe_chunk(pe, m, CHUNKS - 1, False, True)
            pe_down(pe, m, CHUNKS - 1, LAST)
            pe.wait_ge(s(f"m{m}_chunk_done"), ONE + CHUNKS)

        def act_chunk(act, m, c, first, final):
            q = lambda name: s(f"m{m}_{name}")
            for e in range(E):
                if e == 1 and m == 0:
                    act.wait_ge(q("wt_ready"), c + 1)
                    at_least(act, q("b2_ready"), c)
                    act.activation(WTS[:, :], P[6][0:E, :], ACT.Copy).then_inc(q("wt_done"), 1)
                if e == 2 and not final:
                    act_next_hi(act, m, c + 1)
                if e == 3 and not final:
                    act_next_logits(act, m, c + 1)
                for j in range(2):
                    n = 2 * (c * E + e) + j
                    act.wait_ge(q("up_a"), n + 1)
                    act.wait_ge(q("h_done"), H0 + n - 1)
                    bias = COLS[:, e * 4 + j:e * 4 + j + 1] if m == 0 else 0.0
                    act.activation(SIL[j][:, :], P[2 * j][:, :], ACT.Silu, bias=bias).then_inc(q("sil_done"), 1)

        def act_mixture(act, m):
            act_next_hi(act, m, 0)
            act_next_logits(act, m, 0)
            act_chunk(act, m, 0, True, False)
            with act.Fori(1, CHUNKS - 1) as c:
                act_chunk(act, m, c, False, False)
            act_chunk(act, m, CHUNKS - 1, False, True)

        for name in ("d_loaded dy_ready dyt_ready dyt_done ds_ready dneg_done dexp_done dt_ready dpt_done dav_ready "
                     "dres_done dchain dcnt dh_ready dh_done dff_ready dfin").split():
            s(name)
        def decoder_loads(sp):
            with sp.Fori(0, TURNS) as i:
                sp.wait_ge(s("dres_done"), ONE + (TURNS + i) * U)
                sp.dma_start(CU[:, :, :, :].rearrange("p u q d -> p (u q) d"), ctxt[:, ds(i * U * QB, U * QB), :]
                             ).then_inc(s("d_loaded"), 16)

        def final_store(sp):
            for c in range(CHUNKS):
                sp.wait_ge(s("m1_chunk_done"), ONE + c + 1)
                sp.dma_start(outt[:, c * CH:(c + 1) * CH, :], X[:, c * W:(c + 1) * W].rearrange("p (t d) -> p t d", d=D)
                             ).then_inc(s("out_stored"), 16)
            sp.wait_ge(s("out_stored"), 16 * CHUNKS)

        SC = float(D) ** -0.5

        def dve_apply(dve, src, i, gamma, beta, groups):
            c = s("dchain")
            dve.wait_ge(s("rstd_ready"), groups)
            for t in range(U * QB):
                tile = i * U * QB + t
                l = dve.tensor_scalar(YS[:, t * D:(t + 1) * D], src[:, ds(tile * D, D)],
                                      MV[:, ds(tile, 1), 0:1].rearrange("p a c -> p (a c)"),
                                      RSTD[:, ds(tile, 1)], ALU.subtract, ALU.mult)
                if gamma is None and t % QB == QB - 1:
                    l.then_inc(s("dy_ready"), 1)
            if gamma is not None:
                l.then_inc(c, 1)
                for u in range(U):
                    y = YS[:, u * N:(u + 1) * N].rearrange("p (q d) -> p q d", d=D)
                    if u == 0:
                        dve_linked(dve, i)
                    l = dve.tensor_tensor(y, y, BC[:, gamma, :].unsqueeze(1).to_broadcast([128, QB, D]), ALU.mult)
                l.then_inc(c, 1)
                dve_linked(dve, i)
                for u in range(U):
                    y = YS[:, u * N:(u + 1) * N].rearrange("p (q d) -> p q d", d=D)
                    dve.tensor_tensor(y, y, BC[:, beta, :].unsqueeze(1).to_broadcast([128, QB, D]), ALU.add
                                      ).then_inc(s("dy_ready"), 1)

        LINK = [0, 0, 0]

        def dve_linked(dve, i):
            LINK[1] += 1
            dve.wait_ge(s("dchain"), LINK[0] + i * LINK[2] + LINK[1])

        def dve_decoder(dve):
            for stage in range(2):
                cross = stage == 1
                LINK[1], LINK[2] = 0, (3 if cross else 1)
                keys = N if cross else T
                base = stage * B
                with dve.Fori(0, TURNS) as i:
                    n0 = base + i * U
                    dve.wait_ge(s("dav_ready"), ONE + n0)
                    if cross:
                        dve_apply(dve, YR, i, 1, 2, G_SELF + i + 1)
                    else:
                        dve_apply(dve, X, i, None, None, G_MIX + (i + 1) * (U * QB // CH))
                    for u in range(U):
                        waits_alone(dve, s("ident_ready"), (s("ds_ready"), n0 + u + 1))
                        for q in range(QB):
                            lo, n = (q * N, N) if cross else ((0, T) if q == 0 else (T, N))
                            m = ZERO[:, :] if cross else TRI[:, lo:lo + n]
                            k = u * QB + q
                            dve.tensor_tensor_reduce(out=UP[:, u * 512 + lo:u * 512 + lo + n], in0=P[u][:, lo:lo + n],
                                                     in1=m, scale=-SC, scalar=HUGE, op0=ALU.add, op1=ALU.min,
                                                     accum_out=UNEG[:, k:k + 1]).then_inc(s("dneg_done"), 1)
                    for u in range(U):
                        w = 512 if cross else 3 * T
                        dve.wait_ge(s("dt_ready"), n0 + u + 1)
                        dve.tensor_copy(UPT[:, u * 512:u * 512 + w], P[4 + u][:, 0:w]).then_inc(s("dpt_done"), 1)
                    dve.wait_ge(s("dexp_done"), 2 * (n0 + U))
                    dve.reciprocal(URCP[:, :], USUM[:, :]).then_inc(s("dchain"), 1)
                    dve_linked(dve, i)
                    for u in range(U):
                        dve.wait_ge(s("dav_ready"), ONE + n0 + u + 1)
                        for q in range(QB):
                            k = u * QB + q
                            tile = i * U * QB + k
                            l = dve.scalar_tensor_tensor(out=YR[:, ds(tile * D, D)], in0=P[u][:, q * D:(q + 1) * D],
                                                         scalar=URCP[:, k:k + 1], in1=YS[:, k * D:(k + 1) * D],
                                                         op0=ALU.mult, op1=ALU.add)
                        l.then_inc(s("dres_done"), 1)
                    dve_stats(dve, YR, i * U * QB, U * QB, (G_CROSS if cross else G_SELF) + i, (s("dres_done"), ONE + n0 + U))
                    assert LINK[1] == LINK[2], LINK
                LINK[0] += TURNS * LINK[2]
            LINK[1], LINK[2] = 0, 3
            with dve.Fori(0, TURNS) as i:
                dve.wait_ge(s("dfin"), ONE + i * U)
                dve_apply(dve, YR, i, 3, 4, G_CROSS + i + 1)
                dve.wait_ge(s("dy_ready"), 2 * B + (i + 1) * U)
                for u in range(U):
                    y = YS[:, u * N:(u + 1) * N].rearrange("p (q d) -> p q d", d=D)
                    dve.wait_ge(s("dyt_ready"), 2 * B + i * U + u + 1)
                    l = dve.tensor_tensor(y, y, BC[:, 7, :].unsqueeze(1).to_broadcast([128, QB, D]), ALU.add)
                l.then_inc(s("dchain"), 1)
                dve_linked(dve, i)
                for u in range(U):
                    dve.wait_ge(s("dff_ready"), ONE + i * U + u + 1)
                    dve.tensor_tensor(YR[:, ds((i * U + u) * N, N)], P[4 + u][:, 0:N], YS[:, u * N:(u + 1) * N], ALU.add
                                      ).then_inc(s("dfin"), 1)
                dve_stats(dve, YR, i * U * QB, U * QB, G_FF + i, (s("dfin"), ONE + (i + 1) * U))
                assert LINK[1] == LINK[2], LINK
            fc = s("dcnt")
            dve.tensor_scalar(BC[:, 5, :], BC[:, 5, :], GATE[:, 1:2], None, ALU.mult)
            dve.tensor_scalar(BC[:, 6, :], BC[:, 6, :], GATE[:, 1:2], None, ALU.mult).then_inc(fc, 1)
            dve.wait_ge(fc, 1)
            with dve.Fori(0, TURNS) as i:
                dve.wait_ge(s("rstd_ready"), G_FF + i + 1)
                for t in range(U * QB):
                    tile = i * U * QB + t
                    l = dve.tensor_scalar(YS[:, t * D:(t + 1) * D], YR[:, ds(tile * D, D)],
                                          MV[:, ds(tile, 1), 0:1].rearrange("p a c -> p (a c)"),
                                          RSTD[:, ds(tile, 1)], ALU.subtract, ALU.mult)
                l.then_inc(fc, 1)
                dve.wait_ge(fc, i * 4 + 2)
                full = [128, U * QB, D]
                y = YS[:, :].rearrange("p (t d) -> p t d", d=D)
                xs = X[:, ds(i * U * N, U * N)]
                dve.tensor_tensor(y, y, BC[:, 5, :].unsqueeze(1).to_broadcast(full), ALU.mult).then_inc(fc, 1)
                dve.wait_ge(fc, i * 4 + 3)
                dve.tensor_tensor(y, y, BC[:, 6, :].unsqueeze(1).to_broadcast(full), ALU.add).then_inc(fc, 1)
                dve.wait_ge(fc, i * 4 + 4)
                dve.tensor_tensor(xs, xs, YS[:, :], ALU.add).then_inc(fc, 1)
                dve_stats(dve, X, i * U * QB, U * QB, G_DEC + i, (fc, i * 4 + 5))

        def pe_decoder(pe):
            for stage in range(2):
                cross = stage == 1
                base = stage * B
                with pe.Fori(0, TURNS) as i:
                    n0 = base + i * U
                    if cross:
                        pe.wait_ge(s("d_loaded"), 16 * (i + 1))
                    pe.wait_ge(s("dres_done"), ONE + n0)
                    for u in range(U):
                        pe.wait_ge(s("dy_ready"), n0 + u + 1)
                        for k in range(QB):
                            l = pe.transpose(P[u][:, k * T:(k + 1) * T], YS[:, u * N + k * D:u * N + (k + 1) * D], ident[:, :])
                        if cross:
                            for k in range(QB):
                                l = pe.transpose(P[u][:, N + k * T:N + (k + 1) * T], CU[:, u, k, :], ident[:, :])
                        l.then_inc(s("dyt_ready"), 1)
                    for u in range(U):
                        pe.wait_ge(s("dyt_done"), n0 + u + 1)
                        yt = YT[:, u * 512:(u + 1) * 512]
                        for q in range(QB):
                            lo, n = (q * N, N) if cross else ((0, T) if q == 0 else (T, N))
                            keys = yt[:, N:2 * N] if cross else yt[:, 0:n]
                            l = pe.matmul(P[u][:, lo:lo + n], yt[:, q * T:(q + 1) * T], keys, start=True, stop=True)
                        l.then_inc(s("ds_ready"), 1)
                    for u in range(U):
                        pe.wait_ge(s("dexp_done"), 2 * (n0 + u + 1))
                        blocks = 4 if cross else 3
                        for k in range(blocks):
                            l = pe.transpose(P[4 + u][:, k * T:(k + 1) * T], UP[:, u * 512 + k * T:u * 512 + (k + 1) * T],
                                             ident[:, :])
                        l.then_inc(s("dt_ready"), 1)
                    for u in range(U):
                        pe.wait_ge(s("dpt_done"), n0 + u + 1)
                        for q in range(QB):
                            ks = range(QB) if cross else range(q + 1)
                            for k in ks:
                                blk = 2 * q + k if cross else q + k
                                v = CU[:, u, k, :] if cross else YS[:, u * N + k * D:u * N + (k + 1) * D]
                                l = pe.matmul(P[u][:, q * D:(q + 1) * D],
                                              UPT[:, u * 512 + blk * T:u * 512 + (blk + 1) * T], v,
                                              start=k == 0, stop=k == ks[-1])
                        l.then_inc(s("dav_ready"), 1)
            hc = DFF // 128
            with pe.Fori(0, TURNS) as i:
                pe.wait_ge(s("dres_done"), ONE + 2 * B)
                pe.wait_ge(s("dfin"), ONE + i * U)
                for u in range(U):
                    pe.wait_ge(s("dy_ready"), 2 * B + i * U + u + 1)
                    for k in range(QB):
                        l = pe.transpose(P[u][:, k * T:(k + 1) * T], YS[:, u * N + k * D:u * N + (k + 1) * D], ident[:, :])
                    l.then_inc(s("dyt_ready"), 1)
                pe.wait_ge(s("dyt_done"), 2 * B + (i + 1) * U)
                for k in range(2):
                    for m in range(hc):
                        g = k * hc + m
                        if g >= 4:
                            pe.wait_ge(s("dh_done"), i * 2 * hc + g - 3)
                        l = pe.matmul(P[g % 4][:, :], L1W1[:, m * 128:(m + 1) * 128], YT[:, k * W:(k + 1) * W],
                                      start=True, stop=True)
                        l.then_inc(s("dh_ready"), 1)
                for u in range(U):
                    half = u // 2
                    pe.wait_ge(s("dh_done"), i * 2 * hc + (half + 1) * hc)
                    for k in range(QB):
                        t = (u % 2) * QB + k
                        for m in range(hc):
                            c = (half * hc + m) * W + t * T
                            src = HL[:, c:c + T] if half == 0 else UP_HL(c)
                            l = pe.matmul(P[4 + u][:, k * D:(k + 1) * D], src, L1W2[:, m, :],
                                          start=m == 0, stop=m == hc - 1)
                    l.then_inc(s("dff_ready"), 1)

        def UP_HL(c):
            return UP[:, c - 4 * W:c - 4 * W + T]

        def act_decoder(act):
            for stage in range(2):
                cross = stage == 1
                base = stage * B
                with act.Fori(0, TURNS) as i:
                    n0 = base + i * U
                    w = 512 if cross else N
                    for u in range(U):
                        act.wait_ge(s("dyt_ready"), n0 + u + 1)
                        act.activation(YT[:, u * 512:u * 512 + w], P[u][:, 0:w], ACT.Copy).then_inc(s("dyt_done"), 1)
                    for u in range(U):
                        for q in range(QB):
                            k = u * QB + q
                            lo, n = (q * N, N) if cross else ((0, T) if q == 0 else (T, N))
                            act.wait_ge(s("dneg_done"), 2 * n0 + k + 1)
                            p = UP[:, u * 512 + lo:u * 512 + lo + n]
                            act.activation(p, p, ACT.Exp, bias=UNEG[:, k:k + 1], scale=-1.0,
                                           accum_out=USUM[:, k:k + 1]).then_inc(s("dexp_done"), 1)
            hc = DFF // 128
            with act.Fori(0, TURNS) as i:
                for u in range(U):
                    act.wait_ge(s("dyt_ready"), 2 * B + i * U + u + 1)
                    act.activation(YT[:, u * N:(u + 1) * N], P[u][:, 0:N], ACT.Copy).then_inc(s("dyt_done"), 1)
                for g in range(2 * hc):
                    act.wait_ge(s("dh_ready"), i * 2 * hc + g + 1)
                    if g == 0:
                        act.wait_ge(s("dff_ready"), ONE + i * U)
                    dst = HL[:, g * W:(g + 1) * W] if g < hc else UP[:, (g - hc) * W:(g - hc + 1) * W]
                    act.activation(dst, P[g % 4][:, :], ACT.Relu, bias=COLS[:, 32 + g % hc:33 + g % hc]
                                   ).then_inc(s("dh_done"), 1)

        def split1_loads(sp):
            for e in range(E):
                sp.wait_ge(s("w1lo_split"), E) if e == 0 else sp.wait_ge(s("w1lo_split1"), e)
                sp.dma_start(W1RAW[:, 0:H], m1_wg[e]).then_inc(s("w1raw_loaded1"), 16)
                sp.dma_start(W1RAW[:, H:2 * H], m1_wu[e]).then_inc(s("w1raw_loaded1"), 16)

        def pool_split1(pool, e):
            w1e = slice(e * 2 * H, (e + 1) * 2 * H)
            pool.wait_ge(s("w1raw_loaded1"), 32 * (e + 1))
            pool.tensor_copy(W1HI[1][:, w1e], W1RAW[:, :]).then_inc(s("w1hi_split1"), 1)
            pool.wait_ge(s("w1hi_split1"), e + 1)
            pool.tensor_tensor(W1LO[1][:, w1e], W1RAW[:, :], W1HI[1][:, w1e].bitcast(f32), ALU.subtract
                               ).then_inc(s("w1lo_split1"), 1)

        @block.sync
        def _(sp):
            for c in range(CHUNKS):
                sp.dma_start(X[:, c * W:(c + 1) * W].rearrange("p (t d) -> p t d", d=D),
                             xt[:, c * CH:(c + 1) * CH, :]).then_inc(s("x_loaded"), 16)
            for k, w in enumerate((Wq, Wk, Wv)):
                sp.dma_start(RAW[:, k * INNER:(k + 1) * INNER], w).then_inc(s("proj_loaded"), 16)
            sp.dma_start(WOS[:, :, :], Wo.rearrange("(c p) d -> p c d", p=128)).then_inc(s("wo_loaded"), 16)
            sp.dma_start(L1W1[:, :], w1).then_inc(s("l1w_loaded"), 16)
            sp.dma_start(L1W2[:, :, :], w2.rearrange("(c p) d -> p c d", p=128)).then_inc(s("l1w_loaded"), 16)
            sp.dma_start(W2S[0][:, :].rearrange("p (g d) -> p g d", d=D),
                         m0_W2.rearrange("e (j p) d -> p (e j) d", p=128)).then_inc(s("w2_loaded"), 16)
            sp.dma_start(W2S[1][:, :].rearrange("p (g d) -> p g d", d=D),
                         m1_wd.rearrange("e (j p) d -> p (e j) d", p=128)).then_inc(s("w2_loaded"), 16)

            def attention_loads(b):
                at_least(sp, s("xct_ready"), b)
                sp.dma_start(CS[:, :, :], ctxt[:, ds(b * QB, QB), :]).then_inc(s("c_loaded"), 16)
                at_least(sp, s("w1lo_split"), b)
                sp.dma_start(W1RAW[:, :], m0_W1.rearrange("e d h -> d e h")[:, ds(b, 1), :].rearrange("d e h -> d (e h)")
                             ).then_inc(s("w1raw_loaded"), 16)

            attention_loads(0)
            with sp.Fori(1, B) as b:
                attention_loads(b)
            split1_loads(sp)
            decoder_loads(sp)
            final_store(sp)

        @block.gpsimd
        def _(pool):
            pool.memset(ident[:, :], 0.0).then_inc(s("pool_const"), 1)
            pool.memset(TRI[:, :], 0.0).then_inc(s("pool_const"), 1)
            pool.memset(ROWS[:, :], 0.0).then_inc(s("rows_zero"), 1)
            pool.memset(WRF[:, :], 0.0).then_inc(s("wrf_zero"), 1)
            pool.memset(HALF[:, :], -0.5)
            pool.memset(EULER[:, :], math.e)
            pool.memset(EPS2[:, :, 0:1], 0.0)
            pool.memset(EPS2[:, :, 1:2], EPS)
            pool.memset(ZERO[:, :], 0.0)
            for e in range(E):
                l = pool.memset(RANK[:, :, e:e + 1], float(E - e))
            l.then_inc(s("pool_const"), 1)
            pool.wait_ge(s("pool_const"), 2)
            pool.affine_select(out=ident[:, :], in_=ident[:, :], compare_op=ALU.not_equal, fill=1.0, base=0,
                               pattern=[[-1, 128]], channel_multiplier=1).then_inc(s("ident_ready"), 1)
            pool.affine_select(out=TRI[:, 0:T], in_=TRI[:, 0:T], compare_op=ALU.is_ge, fill=-BIG, base=0,
                               pattern=[[-1, T]], channel_multiplier=1)
            pool.affine_select(out=TRI[:, T:3 * T], in_=TRI[:, T:3 * T], compare_op=ALU.is_ge, fill=-BIG, base=T,
                               pattern=[[-1, N]], channel_multiplier=1).then_inc(s("ident_ready"), 1)
            with pool.Fori(0, CHUNKS) as c:
                pool_rstd(pool, c * CH, CH, G_START + c)
            pool_attention(pool, 0, True)
            with pool.Fori(1, B) as b:
                pool_attention(pool, b, False)
            pool_rstd(pool, (B - 1) * QB, QB, G_ATT + B - 1)
            pool_second_weight(pool, 0, 0)
            pool.wait_ge(s("acc_ready"), B)
            for c in range(CHUNKS):
                if c >= 1:
                    pool_rstd(pool, (c - 1) * CH, CH, G_MIX + c - 1)
                if c < CHUNKS - 1:
                    pool_second_weight(pool, 0, c + 1)
                for e in range(c * E // CHUNKS, (c + 1) * E // CHUNKS):
                    pool_split1(pool, e)
            pool_rstd(pool, (CHUNKS - 1) * CH, CH, G_MIX + CHUNKS - 1)
            for g in (G_SELF, G_CROSS, G_FF, G_DEC):
                for i in range(TURNS):
                    pool_rstd(pool, i * U * QB, U * QB, g + i)
            for c in range(CHUNKS):
                pool_second_weight(pool, 1, c)

        @block.scalar
        def _(act):
            act_loads(act)
            act.wait_ge(s("gates_loaded"), 32)
            act.activation(GATE[:, :], GATE[:, :], ACT.Tanh).then_inc(s("gate_ready"), 1)
            for g in (0, 2, 4):
                act.wait_ge(s("wt_ready"), g + 1)
                act.activation(WT[:, g * 512:(g + 1) * 512], P[g][:, :], ACT.Copy).then_inc(s("wt_act"), 1)
            act.activation(WVHI[:, :], RAW[:, 2 * INNER:3 * INNER], ACT.Copy).then_inc(s("wv_act"), 1)
            for k in range(4):
                act.wait_ge(s("g_ready"), k + 1)
                dst = GHI[:, :].rearrange("p (h d) -> p h d", d=D)[:, 8 * (k // 2) + k % 2:8 * (k // 2) + 8:2, :]
                act.activation(dst, P[k][:, :].rearrange("p (h d) -> p h d", d=D), ACT.Copy, scale=DH ** -0.5
                               ).then_inc(s("ghi_done"), 1)
            act.wait_ge(s("cols_done"), 2)
            act.activation(WRHI[:, :], WRF[:, :], ACT.Copy).then_inc(s("wr_act"), 1)
            act_operands(act, 0)
            act_attention(act, 0, True, False)
            with act.Fori(1, B - 1) as b:
                act_attention(act, b, False, False)
            act_attention(act, B - 1, False, True)
            act_out(act, B - 1, PAIRS - 2)
            act_out(act, B - 1, PAIRS - 1)
            act_mixture(act, 0)
            act_decoder(act)
            act_mixture(act, 1)

        @block.vector
        def _(dve):
            open_counts(dve)
            dve.wait_ge(s("x_loaded"), 16 * CHUNKS)
            dve.wait_ge(s("pool_const"), 3)
            dve.wait_ge(s("ident_ready"), 2)
            with dve.Fori(0, CHUNKS) as c:
                dve_stats(dve, X, c * CH, CH, G_START + c)
            for g in (1, 3, 5):
                dve.wait_ge(s("wt_ready"), g + 1)
                dve.tensor_copy(WT[:, g * 512:(g + 1) * 512], P[g][:, :]).then_inc(s("wt_dve"), 1)
            dve.wait_ge(s("wv_act"), 1)
            dve.tensor_tensor(WVLO[:, :], RAW[:, 2 * INNER:3 * INNER], WVHI[:, :].bitcast(f32), ALU.subtract
                              ).then_inc(s("wv_dve"), 1)
            for k in range(4):
                dve.wait_ge(s("ghi_done"), k + 1)
                sel = (slice(None), slice(8 * (k // 2) + k % 2, 8 * (k // 2) + 8, 2), slice(None))
                dve.scalar_tensor_tensor(out=GLO[:, :].rearrange("p (h d) -> p h d", d=D)[sel],
                                         in0=P[k][:, :].rearrange("p (h d) -> p h d", d=D), scalar=DH ** -0.5,
                                         in1=GHI[:, :].bitcast(f32).rearrange("p (h d) -> p h d", d=D)[sel],
                                         op0=ALU.mult, op1=ALU.subtract).then_inc(s("glo_done"), 1)
            dve.wait_ge(s("wvo_ready"), 1)
            dve.tensor_scalar(WVO[:, :], P[4][:, 0:D], 1.0 / N, None, ALU.mult).then_inc(s("wvo_done"), 1)
            dve.wait_ge(s("cols_ready"), 1)
            dve.tensor_copy(COLS[:, :], P[6][:, 0:128]).then_inc(s("cols_done"), 1)
            dve.wait_ge(s("cols_done"), 1)
            dve.wait_ge(s("wr_loaded"), 16)
            dve.tensor_copy(WRF[:, 128:128 + E], COLS[:, 64:64 + E]).then_inc(s("cols_done"), 1)
            dve.wait_ge(s("wr_act"), 1)
            dve.tensor_tensor(WRLO[:, :], WRF[:, :], WRHI[:, :].bitcast(f32), ALU.subtract).then_inc(s("wr_split"), 1)
            dve.wait_ge(s("bcast_loaded"), BCASTS)
            dve.wait_ge(s("gate_ready"), 1)
            dve.tensor_scalar(TGBO[:, :], BC[:, 0, :], GATE[:, 0:1], None, ALU.mult).then_inc(s("wr_split"), 1)
            dve.wait_ge(s("wr_split"), 2)
            dve.wait_ge(s("mask_loaded"), 16)
            dve.wait_ge(s("rstd_ready"), G_ATT)
            dve_normalise(dve, 0)
            dve_operands(dve, 0)
            dve_attention(dve, 0, True, False)
            with dve.Fori(1, B - 1) as b:
                dve_attention(dve, b, False, False)
            dve_attention(dve, B - 1, False, True)
            dve_probs(dve, B - 1, PAIRS - 1)
            dve_bias(dve, B - 1)
            dve_tail(dve, B - 1)
            dve_stats(dve, X, (B - 1) * QB, QB, G_ATT + B - 1, (s("tail_done"), B))
            dve_mixture(dve, 0)
            dve_decoder(dve)
            dve_mixture(dve, 1)

        @block.tensor
        def _(pe):
            pe.wait_ge(s("ident_ready"), 1)
            pe.wait_ge(s("proj_loaded"), 48)
            for g in range(6):
                for k in range(4):
                    c = g * 512 + k * 128
                    l = pe.transpose(P[g][:, k * 128:(k + 1) * 128], RAW[:, c:c + 128], ident[:, :])
                l.then_inc(s("wt_ready"), 1)
            pe.wait_ge(s("rows_loaded"), 48)
            pe.transpose(P[6][:, 0:128], ROWS[:, :], ident[:, :]).then_inc(s("cols_ready"), 1)
            pe.wait_ge(s("wt_act"), 3)
            pe.wait_ge(s("wt_dve"), 3)
            for k in range(4):
                r = (k % 2) * DH
                for j in range(4):
                    c = (4 * (k // 2) + j) * 128
                    l = pe.matmul(P[k][:, j * D:(j + 1) * D], WT[r:r + DH, INNER + c:INNER + c + 128],
                                  WT[r:r + DH, c:c + 128], start=True, stop=True)
                l.then_inc(s("g_ready"), 1)
            pe.wait_ge(s("wo_loaded"), 16)
            for c in range(PAIRS):
                l = pe.matmul(P[4][:, 0:D], WT[:, 2 * INNER + c * 128:2 * INNER + (c + 1) * 128], WOS[:, c, :],
                              start=c == 0, stop=c == PAIRS - 1)
            l.then_inc(s("wvo_ready"), 1)
            pe.wait_ge(s("glo_done"), 4)
            pe.wait_ge(s("wv_dve"), 1)
            pe.wait_ge(s("wvo_done"), 1)
            pe.wait_ge(s("cols_done"), 1)
            pe_operands(pe, 0)
            pe_attention(pe, 0, True, False)
            with pe.Fori(1, B - 1) as b:
                pe_attention(pe, b, False, False)
            pe_attention(pe, B - 1, False, True)
            pe_values(pe, B - 1, PAIRS - 2)
            pe_transpose_probs(pe, B - 1, PAIRS - 1)
            pe_project(pe, B - 1, PAIRS - 2)
            pe_values(pe, B - 1, PAIRS - 1)
            pe_project(pe, B - 1, PAIRS - 1)
            pe.wait_ge(s("tail_done"), B)
            pe.wait_ge(s("wr_split"), 2)
            pe.wait_ge(s("w1lo_split"), E)
            pe.wait_ge(s("w2_loaded"), 32)
            pe.wait_ge(s("bcast_loaded"), BCASTS)
            pe_mixture(pe, 0)
            pe.wait_ge(s("l1w_loaded"), 32)
            pe_decoder(pe)
            pe.wait_ge(s("dfin"), ONE + B)
            pe.wait_ge(s("w1lo_split1"), E)
            pe_mixture(pe, 1)


_ARGS = ['x', 'ctx_1024', 'mask_BxS2_bf0', 'g_xattn', 'g_ffn', 'L0_xattn_Wq', 'L0_xattn_Wk', 'L0_xattn_Wv',
         'L0_xattn_Wo', 'L0_xattn_bo', 'L0_ffn_W1', 'L0_ffn_b1', 'L0_ffn_W2', 'L0_ffn_b2', 'L0_ffn_Wr', 'L0_ffn_br',
         'L1_xattn_w1', 'L1_xattn_b1', 'L1_xattn_w2', 'L1_xattn_b2', 'L1_xattn_g1', 'L1_xattn_beta1', 'L1_xattn_g2',
         'L1_xattn_beta2', 'L1_xattn_g3', 'L1_xattn_beta3', 'L1_ffn_gate_w', 'L1_ffn_w_gate', 'L1_ffn_w_up',
         'L1_ffn_w_down']


def kernel(**inputs):
    import numpy as np
    import concourse.bacc as bacc
    from concourse import mybir as mb
    from concourse.bass_utils import run_bass_kernel_spmd

    nc = bacc.Bacc("TRN2", target_bir_lowering=False, num_devices=1)
    arrays, args = {}, []
    for name in _ARGS:
        a = np.ascontiguousarray(inputs[name])
        arrays[f"in_{name}"] = a
        args.append(nc.dram_tensor(f"in_{name}", a.shape, mb.dt.from_np(a.dtype), kind="ExternalInput").ap())
    out = nc.dram_tensor("out_x", (B, N, D), f32, kind="ExternalOutput").ap()
    build(nc, *args, out)
    r = run_bass_kernel_spmd(nc, [arrays], core_ids=[0])
    return r.results[0]["out_x"]
```

```python
import math

import concourse.bass as bass
from concourse import mybir
from contextlib import ExitStack

f32 = mybir.dt.float32
f32r = mybir.dt.float32r
u8 = mybir.dt.uint8
ALU = mybir.AluOpType
ACT = mybir.ActivationFunctionType
AX = mybir.AxisListType

B, N, D = 8, 256, 128
HEADS, DH = 16, 64
PAIRS = HEADS // 2
INNER = HEADS * DH
E, H = 8, 256
DFF = 512
T = 128
QB = N // T
TILES = B * QB
CH = 4
CHUNKS = TILES // CH
W = CH * T
U = 2
UNITS = B // U
ONE = 1
H0 = 2
EPS = 1e-5
BIG = 1e30
HUGE = 3e38


def ds(start, size):
    return bass.ds(start, size)


def at_least(eng, sem, value):
    if isinstance(value, int) and value <= 0:
        return
    eng.wait_ge(sem, value)


def waits_alone(eng, const, *waits):
    held = [(sem, value if isinstance(value, int) else eng.to_reg(value)) for sem, value in waits]
    eng.wait_ge(const, 1)
    for sem, value in held:
        at_least(eng, sem, value)


def build(nc, x, ctx_in, mask, g_xattn, g_ffn, Wq, Wk, Wv, Wo, bo, m0_W1, m0_b1, m0_W2, m0_b2, m0_Wr, m0_br,
          w1, b1, w2, b2, g1, beta1, g2, beta2, g3, beta3, m1_gate, m1_wg, m1_wu, m1_wd, out):
    stack = ExitStack()
    with stack:
        def sb(name, shape, dt=f32):
            return stack.enter_context(nc.sbuf_tensor(name, shape, dt))

        def sem(name):
            return stack.enter_context(nc.semaphore(name))

        P = [stack.enter_context(nc.psum_tensor(f"bank{i}", [128, 512], f32)) for i in range(8)]

        X = sb("X", [128, TILES * D])
        MV = sb("MV", [128, TILES, 2])
        RSTD = sb("RSTD", [128, TILES])
        HALF = sb("HALF", [128, 8])
        EULER = sb("EULER", [128, CH])
        EPS2 = sb("EPS2", [128, 8, 2])
        STAT = sb("STAT", [128, 8 * 6])
        AGGR = sb("AGGR", [128, 8, 2])
        ident = sb("ident", [128, 128])
        TRI = sb("TRI", [128, 3 * T])
        ZERO = sb("ZERO", [128, N])
        GATE = sb("GATE", [128, 4])
        BC = sb("BC", [128, 8, D])
        ROWS = sb("ROWS", [128, 128])
        COLS = sb("COLS", [128, 128])
        RAW = sb("RAW", [128, 3 * INNER])
        WT = sb("WT", [128, 3 * INNER])
        SPLITS = sb("SPLITS", [128, 9216], f32r)
        GHI = SPLITS[:, 0:2048]
        GLO = SPLITS[:, 2048:4096]
        WVHI = SPLITS[:, 4096:5120]
        WVLO = SPLITS[:, 5120:6144]
        WOS = sb("WOS", [128, PAIRS, D])
        WVO = sb("WVO", [128, D])
        MASK = sb("MASK", [128, B * N], u8)
        MB = sb("MB", [128, 3 * T])
        XN = sb("XN", [128, N])
        CS = sb("CS", [128, QB, D])
        XCHI = SPLITS[:, 6144:6656]
        XCLO = SPLITS[:, 6656:7168]
        CBAR = sb("CBAR", [128, 1])
        CBARB = sb("CBARB", [128, 128])
        KHI = [SPLITS[:, 7168 + 512 * i:7680 + 512 * i] for i in range(2)]
        KLO = [SPLITS[:, 8192 + 512 * i:8704 + 512 * i] for i in range(2)]
        ARENA = sb("ARENA", [128, 6144])
        VB = ARENA[:, 0:2048].rearrange("p (q c) -> p q c", q=QB)
        SP = [ARENA[:, 2048 + 768 * i:2816 + 768 * i] for i in range(2)]
        NEGM = [sb(f"NEGM{i}", [128, 4]) for i in range(2)]
        RSUM = [sb(f"RSUM{i}", [128, 4]) for i in range(2)]
        RCP = [sb(f"RCP{i}", [128, 4]) for i in range(2)]
        PT = [ARENA[:, 3584 + 384 * i:3968 + 384 * i] for i in range(2)]
        OT = ARENA[:, 4352:4608]
        TGBO = sb("TGBO", [128, D])
        NKEEP = sb("NKEEP", [128, 2])
        FCOL = sb("FCOL", [128, 2])
        GCOL = sb("GCOL", [128, 2])
        XTHI = sb("XTHI", [128, TILES * T], f32r)
        XTLO = sb("XTLO", [128, TILES * T], f32r)
        W1RAW = sb("W1RAW", [128, 2 * H])
        W1HI = [sb("W1HI", [128, E * 2 * H], f32r), SPLITS[:, 0:E * 2 * H]]
        W1LO = [sb("W1LO", [128, E * 2 * H], f32r), SPLITS[:, E * 2 * H:2 * E * 2 * H]]
        W2S = [sb(f"W2S{m}", [128, E * 2 * D]) for m in range(2)]
        B2S = sb("B2S", [E, D])
        WRF = sb("WRF", [128, 2 * 128])
        WRHI = sb("WRHI", [128, 2 * 128], f32r)
        WRLO = sb("WRLO", [128, 2 * 128], f32r)
        BRB = sb("BRB", [128, E])
        HT = [ARENA[:, 1024 * k:1024 * (k + 1)].rearrange("p (j t) -> p j t", j=2) for k in range(2)]
        SIL = [ARENA[:, 2048 + W * j:2048 + W * (j + 1)] for j in range(2)]
        ACC = ARENA[:, 3072:3584]
        XNS = RAW[:, 2048:2048 + W]
        LTS = RAW[:, 2048 + W:2048 + 2 * W]
        LG = sb("LG", [128, CH, E])
        RANK = sb("RANK", [128, CH, E])
        RT = [sb(f"RT{k}", [128, CH, E]) for k in range(2)]
        RV = [sb(f"RV{k}", [128, CH]) for k in range(6)]
        WGT = sb("WGT", [128, CH, E])
        WSL = sb("WSL", [128, CH * E])
        WTS = sb("WTS", [E, W])
        L1W1 = sb("L1W1", [128, DFF])
        L1W2 = sb("L1W2", [128, DFF // 128, D])
        UP = ARENA[:, 0:2048]
        YS = ARENA[:, 2048:3072]
        CU = ARENA[:, 3072:4096]
        YR = ARENA[:, 4096:6144]
        UNEG = sb("UNEG", [128, 2 * U * QB])
        USUM = sb("USUM", [128, 2 * U * QB])
        URCP = sb("URCP", [128, 2 * U * QB])
        YT = RAW[:, 0:2048]
        UPT = WT[:, 0:2048]
        COL_B1, COL_GB = 32, 36

        block = stack.enter_context(nc.Block())
        S = {}

        def s(name):
            if name not in S:
                S[name] = sem(name)
            return S[name]

        TICK = sb("TICK", [128, 32])
        COUNTED = ["stat_done", "aggr_done", "mv_done"]
        COUNTED += [f"m{m}_{name}" for m in range(2) for name in ("chunk_done", "acc_chain")]

        def open_counts(eng):
            for k, name in enumerate(COUNTED):
                eng.memset(TICK[:, k:k + 1], 0.0).then_inc(s(name), ONE)
            for m in range(2):
                eng.memset(TICK[:, 16 + m:17 + m], 0.0).then_inc(s(f"m{m}_h_done"), H0)

        for name in ("x_loaded x0_loaded proj_loaded wv_loaded wo_loaded rows_loaded bcast_loaded mask_loaded gates_loaded wr_loaded "
                     "w2_loaded l1w_loaded out_stored pool_const ident_ready rows_zero wrf_zero "
                     "stat_done aggr_done mv_done rstd_ready gate_ready cbar_sum "
                     "wt_ready wt_act wt_dve cols_ready cols_done g_ready ghi_done glo_done wvo_ready wvo_done wr_split wr_act wv_act wv_dve "
                     "xn_ready c_loaded xct_ready xchi_done xclo_done mb_ready cbar_done "
                     "neg_kept kp_ready khi_done klo_done v_ready v_done s0_ready s1_ready neg_done exp_done recip_done norm_done "
                     "ta_ready tb_ready pta_done ptb_done ot_ready ot_done acc_ready tail_chain tail_done "
                     "w1raw_loaded w1hi_split w1lo_split w1raw_loaded1 w1hi_split1 w1lo_split1").split():
            s(name)

        xt = x.rearrange("b (q p) d -> p (b q) d", p=T)
        outt = out.rearrange("b (q p) d -> p (b q) d", p=T)
        ctxt = ctx_in.rearrange("b (q p) d -> p (b q) d", p=T)

        def row(v):
            return v.rearrange("(a n) -> a n", a=1)

        def act_loads(act):
            act.dma_start(GATE[:, 0:2], row(g_xattn).partition_broadcast(128)).then_inc(s("gates_loaded"), 16)
            act.dma_start(GATE[:, 2:4], row(g_ffn).partition_broadcast(128)).then_inc(s("gates_loaded"), 16)
            for c in range(CHUNKS):
                act.dma_start(X[:, c * W:(c + 1) * W].rearrange("p (t d) -> p t d", d=D),
                              xt[:, c * CH:(c + 1) * CH, :]).then_inc(s("x_loaded" if c else "x0_loaded"), 16)
            act.dma_start(MASK[:, :], mask.rearrange("(a b) n -> a (b n)", a=1).partition_broadcast(128)
                          ).then_inc(s("mask_loaded"), 16)

        def small_loads(sp):
            sp.wait_ge(s("rows_zero"), 1)
            sp.dma_start(ROWS[0:32, :], m0_b1.rearrange("e (c p) -> (e c) p", p=128)).then_inc(s("rows_loaded"), 16)
            sp.dma_start(ROWS[32:36, :], b1.rearrange("(c p) -> c p", p=128)).then_inc(s("rows_loaded"), 16)
            for k, v in enumerate((g1, beta1, g2, beta2)):
                sp.dma_start(ROWS[COL_GB + k:COL_GB + k + 1, :], row(v)).then_inc(s("rows_loaded"), 16)
            sp.dma_start(ROWS[64:72, :], m1_gate).then_inc(s("rows_loaded"), 16)
            sp.wait_ge(s("wrf_zero"), 1)
            sp.dma_start(WRF[:, 0:E], m0_Wr).then_inc(s("wr_loaded"), 16)
            for k, v in enumerate((bo, g1, beta1, g2, beta2, g3, beta3, b2)):
                sp.dma_start(BC[:, k, :], row(v).partition_broadcast(128)).then_inc(s("bcast_loaded"), 16)
            sp.dma_start(BRB[:, :], row(m0_br).partition_broadcast(128)).then_inc(s("bcast_loaded"), 16)
            sp.dma_start(B2S[:, :], m0_b2).then_inc(s("bcast_loaded"), 16)

        BCASTS = 10 * 16

        bK, bV, bS0, bS1, bO, bA = P[0], P[1], P[2], P[3], P[6], P[7]
        bT = (P[4], P[5])

        def pe_proj(pe, b, hp):
            n = b * PAIRS + hp
            if hp == 0:
                pe.wait_ge(s("xclo_done"), b + 1)
            at_least(pe, s("klo_done"), n)
            for h in range(2):
                g = ds((2 * hp + h) * D, D)
                for k, (l, r) in enumerate(((GHI, XCHI), (GHI, XCLO), (GLO, XCHI))):
                    last = pe.matmul(bK[:, h * N:(h + 1) * N], l[:, g], r[:, 0:N], start=k == 0, stop=k == 2)
            last.then_inc(s("kp_ready"), 1)
            if hp % 2 == 0:
                at_least(pe, s("v_done"), b * (PAIRS // 2) + hp // 2)
                cols = ds(hp * 128, 256)
                for q in range(QB):
                    t = ds(q * T, T)
                    for k, (l, r) in enumerate(((XCHI, WVHI), (XCHI, WVLO), (XCLO, WVHI))):
                        last = pe.matmul(bV[:, q * 256:(q + 1) * 256], l[:, t], r[:, cols], start=k == 0, stop=k == 2)
                last.then_inc(s("v_ready"), 1)

        def pe_scores(pe, b, hp):
            n = b * PAIRS + hp
            pe.wait_ge(s("klo_done"), n + 1)
            at_least(pe, s("neg_done"), 4 * n)
            kh, kl = KHI[hp % 2], KLO[hp % 2]

            def first_keys(t):
                return t[:, :].rearrange("p (h k) -> p h k", h=2)[:, :, 0:T]

            q0, q1 = ds(N, T), ds(N + T, T)
            o0 = bS0[:, 0:2 * T].rearrange("p (h k) -> p h k", h=2)
            for k, (l, r) in enumerate(((XCHI, kh), (XCHI, kl), (XCLO, kh))):
                last = pe.matmul(o0, l[:, q0], first_keys(r), start=k == 0, stop=k == 2)
            last.then_inc(s("s0_ready"), 1)
            for k, (l, r) in enumerate(((XCHI, kh), (XCHI, kl), (XCLO, kh))):
                last = pe.matmul(bS1[:, :], l[:, q1], r[:, :], start=k == 0, stop=k == 2)
            last.then_inc(s("s1_ready"), 1)

        def pe_transpose_probs(pe, b, hp):
            n = b * PAIRS + hp
            pe.wait_ge(s("norm_done"), n + 1)
            p = SP[hp % 2]
            for h, ready, done in ((0, "ta_ready", "pta_done"), (1, "tb_ready", "ptb_done")):
                at_least(pe, s(done), n)
                for k, c in enumerate((h * T, 2 * T + h * N, 2 * T + h * N + T)):
                    last = pe.transpose(bT[h][:, k * T:(k + 1) * T], p[:, c:c + T], ident[:, :])
                last.then_inc(s(ready), 1)

        def pe_values(pe, b, hp):
            n = b * PAIRS + hp
            if hp % 2 == 0:
                pe.wait_ge(s("v_done"), b * (PAIRS // 2) + hp // 2 + 1)
            pe.wait_ge(s("pta_done"), n + 1)
            pe.wait_ge(s("ptb_done"), n + 1)
            at_least(pe, s("ot_done"), n)
            for k in range(QB):
                for h in range(2):
                    v = VB[:, k, (2 * hp + h) * DH:(2 * hp + h + 1) * DH]
                    probs = PT[h][:, 0:N] if k == 0 else PT[h][:, N:N + T]
                    last = pe.matmul(bO[h * DH:(h + 1) * DH, k * T:N], v, probs, start=k == 0, stop=k == 1,
                                     skip_group_check=True)
            last.then_inc(s("ot_ready"), 1)

        def pe_uniform(pe, b):
            at_least(pe, s("tail_done"), b)
            pe.wait_ge(s("cbar_done"), b + 1)
            pe.matmul(bA[:, N:N + D], CBARB[:, :], WVO[:, :], start=True, stop=True, skip_group_check=True)

        def pe_project(pe, b, hp):
            n = b * PAIRS + hp
            pe.wait_ge(s("ot_done"), n + 1)
            for q in range(QB):
                last = pe.matmul(bA[:, q * D:(q + 1) * D], OT[:, q * T:(q + 1) * T], WOS[:, hp, :], start=False,
                                 stop=hp == PAIRS - 1, skip_group_check=True)
            if hp == PAIRS - 1:
                last.then_inc(s("acc_ready"), 1)

        def pe_operands(pe, b):
            pe.wait_ge(s("xn_ready"), b + 1)
            pe.wait_ge(s("c_loaded"), 16 * (b + 1))
            at_least(pe, s("klo_done"), b * PAIRS)
            for k in range(QB):
                pe.transpose(bK[:, k * T:(k + 1) * T], CS[:, k, :], ident[:, :])
            for k in range(QB):
                last = pe.transpose(bK[:, N + k * T:N + (k + 1) * T], XN[:, k * T:(k + 1) * T], ident[:, :])
            last.then_inc(s("xct_ready"), 1)

        def pe_attention(pe, b, first, final):
            pe_proj(pe, b, 0)
            if not first:
                pe_values(pe, b - 1, PAIRS - 2)
            for hp in range(PAIRS):
                pe_scores(pe, b, hp)
                if hp < PAIRS - 1:
                    pe_proj(pe, b, hp + 1)
                elif not final:
                    pe_operands(pe, b + 1)
                if hp >= 2:
                    pe_values(pe, b, hp - 2)
                elif hp == 1 and not first:
                    pe_values(pe, b - 1, PAIRS - 1)
                if hp >= 1:
                    pe_transpose_probs(pe, b, hp - 1)
                elif not first:
                    pe_transpose_probs(pe, b - 1, PAIRS - 1)
                if hp == 2:
                    pe_uniform(pe, b)
                if hp >= 2:
                    pe_project(pe, b, hp - 2)
                elif not first:
                    pe_project(pe, b - 1, PAIRS - 2 + hp)

        def act_k_hi(act, b, hp):
            n = b * PAIRS + hp
            act.wait_ge(s("kp_ready"), n + 1)
            act.activation(KHI[hp % 2][:, :], bK[:, :], ACT.Copy).then_inc(s("khi_done"), 1)

        def act_v(act, b, hp):
            act.wait_ge(s("v_ready"), b * (PAIRS // 2) + hp // 2 + 1)
            act.activation(VB[:, :, hp * 128:hp * 128 + 256], bV[:, :].rearrange("p (q c) -> p q c", q=QB),
                           ACT.Copy).then_inc(s("v_done"), 1)

        def act_out(act, b, hp):
            act.wait_ge(s("ot_ready"), b * PAIRS + hp + 1)
            act.activation(OT[:, :], bO[:, 0:N], ACT.Copy).then_inc(s("ot_done"), 1)

        BLOCKS = ((0, T, 0), (T, T, 1), (2 * T, N, 2), (2 * T + N, N, 3))

        def act_operands(act, b):
            act.wait_ge(s("xct_ready"), b + 1)
            act.activation(XCHI[:, :], bK[:, :], ACT.Copy).then_inc(s("xchi_done"), 1)

        def act_attention(act, b, first, final):
            act_k_hi(act, b, 0)
            act_v(act, b, 0)
            if not first:
                act_out(act, b - 1, PAIRS - 2)
            for hp in range(PAIRS):
                n = b * PAIRS + hp
                k = hp % 2
                for c, w, i in BLOCKS:
                    if i == 2:
                        if hp < PAIRS - 1:
                            act_k_hi(act, b, hp + 1)
                        elif not final:
                            act_operands(act, b + 1)
                    if i == 2 + hp % 2 and hp >= 2:
                        act_out(act, b, hp - 2)
                    elif i == 3 and hp == 1 and not first:
                        act_out(act, b - 1, PAIRS - 1)
                    if i == 3 and hp % 2 == 1 and hp < PAIRS - 1:
                        act_v(act, b, hp + 1)
                    act.wait_ge(s("neg_done"), 4 * n + i + 1)
                    act.activation(SP[k][:, c:c + w], SP[k][:, c:c + w], ACT.Exp, bias=NEGM[k][:, i:i + 1],
                                   scale=-1.0, accum_out=RSUM[k][:, i:i + 1]).then_inc(s("exp_done"), 1)

        def dve_k_lo(dve, b, hp):
            n = b * PAIRS + hp
            dve.wait_ge(s("khi_done"), n + 1)
            dve.tensor_tensor(KLO[hp % 2][:, :], bK[:, :], KHI[hp % 2][:, :].bitcast(f32), ALU.subtract
                              ).then_inc(s("klo_done"), 1)

        def dve_probs(dve, b, hp):
            n = b * PAIRS + hp
            for h, ready, done in ((0, "ta_ready", "pta_done"), (1, "tb_ready", "ptb_done")):
                dve.wait_ge(s(ready), n + 1)
                dve.tensor_copy(PT[h][:, :], bT[h][:, 0:3 * T]).then_inc(s(done), 1)

        def dve_bias(dve, b):
            x3 = X[:, ds(b * N, N)].rearrange("p (q d) -> p q d", q=QB)
            dve.tensor_tensor(x3, x3, TGBO[:, :].unsqueeze(1).to_broadcast([128, QB, D]), ALU.add
                              ).then_inc(s("tail_chain"), 1)

        def dve_tail(dve, b):
            c = s("tail_chain")
            base = b * 4 + 2
            dve.wait_ge(s("acc_ready"), b + 1)
            dve.wait_ge(c, base + 1)
            for q in range(QB):
                xq = X[:, ds(b * N + q * D, D)]
                i = dve.scalar_tensor_tensor(out=xq, in0=bA[:, q * D:(q + 1) * D], scalar=GCOL[:, q:q + 1], in1=xq,
                                             op0=ALU.mult, op1=ALU.add)
            i.then_inc(c, 1)
            dve.wait_ge(c, base + 2)
            for q in range(QB):
                xq = X[:, ds(b * N + q * D, D)]
                i = dve.scalar_tensor_tensor(out=xq, in0=bA[:, N:N + D], scalar=FCOL[:, q:q + 1], in1=xq,
                                             op0=ALU.mult, op1=ALU.add)
            i.then_inc(s("tail_done"), 1)

        def dve_flags(dve, b):
            c = s("tail_chain")
            at_least(dve, s("tail_done"), b)
            dve.wait_ge(s("neg_kept"), b + 1)
            dve.tensor_scalar(FCOL[:, :], NKEEP[:, :], BIG / 10, GATE[:, 0:1], ALU.is_ge, ALU.mult).then_inc(c, 1)
            dve.wait_ge(c, b * 4 + 1)
            dve.tensor_scalar(GCOL[:, :], FCOL[:, :], -1.0, GATE[:, 0:1], ALU.mult, ALU.add).then_inc(c, 1)

        def dve_normalise(dve, b):
            at_least(dve, s("xct_ready"), b)
            for q in range(QB):
                i = dve.tensor_scalar(XN[:, q * D:(q + 1) * D], X[:, ds(b * N + q * D, D)],
                                      MV[:, ds(b * QB + q, 1), 0:1].rearrange("p a c -> p (a c)"),
                                      RSTD[:, ds(b * QB + q, 1)], ALU.subtract, ALU.mult)
            i.then_inc(s("xn_ready"), 1)

        def dve_operands(dve, b):
            dve.wait_ge(s("xchi_done"), b + 1)
            at_least(dve, s("cbar_done"), b)
            dve.reduce_sum(CBAR[:, :], bK[:, 0:N], AX.X).then_inc(s("cbar_sum"), 1)
            dve.tensor_tensor(XCLO[:, :], bK[:, :], XCHI[:, :].bitcast(f32), ALU.subtract).then_inc(s("xclo_done"), 1)

        def dve_attention(dve, b, first, final):
            at_least(dve, s("neg_done"), 4 * b * PAIRS)
            for lo, n, k in ((0, T, 0), (T, N, 0)):
                i = dve.scalar_tensor_tensor(out=MB[:, lo:lo + n], in0=MASK[:, ds(b * N, n)], scalar=-BIG,
                                             in1=TRI[:, lo:lo + n], op0=ALU.mult, op1=ALU.add)
            i.then_inc(s("mb_ready"), 1)
            dve_k_lo(dve, b, 0)
            for hp in range(PAIRS):
                n = b * PAIRS + hp
                k = hp % 2
                waits_alone(dve, s("ident_ready"), (s("tb_ready"), n - 1), (s("mb_ready"), b + 1), (s("s0_ready"), n + 1))
                for c, w, i in BLOCKS:
                    if i == 2:
                        waits_alone(dve, s("ident_ready"), (s("s1_ready"), n + 1))
                    bank, bc = (bS0, c) if i < 2 else (bS1, c - 2 * T)
                    m = MB[:, 0:T] if i < 2 else MB[:, T:3 * T]
                    dve.tensor_tensor_reduce(out=SP[k][:, c:c + w], in0=bank[:, bc:bc + w], in1=m, scale=-1.0, scalar=HUGE,
                                             op0=ALU.add, op1=ALU.min, accum_out=NEGM[k][:, i:i + 1]
                                             ).then_inc(s("neg_done"), 1)
                if hp == 2 and not first:
                    dve_tail(dve, b - 1)
                if hp < PAIRS - 1:
                    dve_k_lo(dve, b, hp + 1)
                elif not final:
                    dve_operands(dve, b + 1)
                if hp == 0:
                    dve.wait_ge(s("neg_done"), 4 * n + 4)
                    dve.tensor_copy(NKEEP[:, :], NEGM[0][:, 0:4:2]).then_inc(s("neg_kept"), 1)
                if hp == 1:
                    if not first:
                        dve_bias(dve, b - 1)
                    dve.wait_ge(s("cbar_sum"), b + 1)
                    dve.tensor_scalar(CBARB[:, :], ZERO[:, 0:128], 1.0, CBAR[:, 0:1], ALU.mult, ALU.add
                                      ).then_inc(s("cbar_done"), 1)
                if hp == 2:
                    dve_flags(dve, b)
                dve.wait_ge(s("exp_done"), 4 * (n + 1))
                dve.reciprocal(RCP[k][:, :], RSUM[k][:, :]).then_inc(s("recip_done"), 1)
                if hp >= 1:
                    dve_probs(dve, b, hp - 1)
                elif not first:
                    dve_probs(dve, b - 1, PAIRS - 1)
                if 3 <= hp < 6 and not first:
                    dve_stats(dve, X, (b - 1) * QB, QB, CHUNKS + b - 1, (s("tail_done"), b), (hp - 3,))
                if first and 3 <= hp < 2 + CHUNKS:
                    dve_stats(dve, X, (hp - 2) * CH, CH, G_START + hp - 2)
                if hp == PAIRS - 2 and not final:
                    dve_normalise(dve, b + 1)

        def pool_attention(pool, b, first):
            for hp in range(PAIRS):
                n = b * PAIRS + hp
                k = hp % 2
                waits_alone(pool, s("ident_ready"), (s("recip_done"), n + 1))
                for c, w, i in BLOCKS:
                    last = pool.tensor_scalar(SP[k][:, c:c + w], SP[k][:, c:c + w], RCP[k][:, i:i + 1], 1.0,
                                              ALU.mult, ALU.mult)
                last.then_inc(s("norm_done"), 1)
                w1e = ds(b * 2 * H, 2 * H)
                if first and 4 <= hp < 3 + CHUNKS:
                    pool_rstd(pool, (hp - 3) * CH, CH, G_START + hp - 3)
                if hp == 6 and not first:
                    pool_rstd(pool, (b - 1) * QB, QB, CHUNKS + b - 1)
                if hp == 2:
                    pool.wait_ge(s("w1raw_loaded"), 16 * (b + 1))
                    pool.tensor_copy(W1HI[0][:, w1e], W1RAW[:, :]).then_inc(s("w1hi_split"), 1)
                if hp == 5:
                    pool.wait_ge(s("w1hi_split"), b + 1)
                    pool.tensor_tensor(W1LO[0][:, w1e], W1RAW[:, :], W1HI[0][:, w1e].bitcast(f32), ALU.subtract
                                       ).then_inc(s("w1lo_split"), 1)

        G_START = 0
        G_ATT = G_START + CHUNKS
        G_MIX = G_ATT + B
        G_SELF = G_MIX + CHUNKS
        G_CROSS = G_SELF + UNITS
        G_FF = [G_CROSS + UNITS + k for k in (0, 1, 3, 4)]
        G_DEC = [G_CROSS + UNITS + k for k in (2, 5, 6, 7)]
        G_END = G_CROSS + 3 * UNITS

        def dve_stats(dve, src, tile, n, g, written=None, parts=(0, 1, 2)):
            if 0 in parts:
                waits_alone(dve, s("ident_ready"), (s("aggr_done"), ONE + g), *([written] if written else []))
                for t in range(n):
                    l = dve.bn_stats(STAT[:, t * 6:(t + 1) * 6], src[:, ds((tile + t) * D, D)])
                l.then_inc(s("stat_done"), 1)
            if 1 in parts:
                waits_alone(dve, s("ident_ready"), (s("stat_done"), ONE + g + 1), (s("mv_done"), ONE + g))
                for t in range(n):
                    l = dve.bn_aggr(AGGR[:, t, :], STAT[:, t * 6:(t + 1) * 6])
                l.then_inc(s("aggr_done"), 1)
            if 2 in parts:
                waits_alone(dve, s("ident_ready"), (s("aggr_done"), ONE + g + 1))
                dve.tensor_tensor(MV[:, ds(tile, n), :], AGGR[:, 0:n, :], EPS2[:, 0:n, :], ALU.add
                                  ).then_inc(s("mv_done"), 1)

        def pool_rstd(pool, tile, n, g):
            waits_alone(pool, s("ident_ready"), (s("mv_done"), ONE + g + 1))
            pool.tensor_tensor(RSTD[:, ds(tile, n)], MV[:, ds(tile, n), 1:2].rearrange("p t c -> p (t c)"), HALF[:, 0:n],
                               ALU.pow).then_inc(s("rstd_ready"), 1)

        for m in range(2):
            for name in ("n_ready xt_ready xthi_done xtlo_done lt_ready lt_done lg_ready lg_done route exp_ready "
                         "w_ready wsl_done wt_ready wt_done b2_ready up_a up_g sil_done h_done y_ready acc_chain "
                         "chunk_done").split():
                s(f"m{m}_{name}")
        ROUTE = 18
        DIFF_STEP = 12
        LAST = E - 1

        def next_banks(m, c):
            if isinstance(c, int) and c == 0:
                return (P[4], P[5]) if m else (P[0], P[1])
            return P[6], P[7]

        def lag(m, c):
            return 2 if m == 1 and isinstance(c, int) and c == 0 else 0

        def dve_next_normalised(dve, m, c, groups):
            dve.wait_ge(s("rstd_ready"), groups)
            at_least(dve, s(f"m{m}_xt_ready"), c)
            for t in range(CH):
                tile = c * CH + t
                l = dve.tensor_scalar(XNS[:, t * D:(t + 1) * D], X[:, ds(tile * D, D)],
                                      MV[:, ds(tile, 1), 0:1].rearrange("p a c -> p (a c)"),
                                      RSTD[:, ds(tile, 1)], ALU.subtract, ALU.mult)
            l.then_inc(s(f"m{m}_n_ready"), 1)

        def pe_next_transposed(pe, m, c):
            pe.wait_ge(s(f"m{m}_n_ready"), c + 1)
            at_least(pe, s(f"m{m}_lg_done"), c)
            if m == 0:
                at_least(pe, s(f"m{m}_wt_done"), c)
            for t in range(CH):
                l = pe.transpose(next_banks(m, c)[0][:, t * T:(t + 1) * T], XNS[:, t * D:(t + 1) * D], ident[:, :])
            l.then_inc(s(f"m{m}_xt_ready"), 1)

        def act_next_hi(act, m, c):
            act.wait_ge(s(f"m{m}_xt_ready"), c + 1)
            act.activation(XTHI[:, ds(c * W, W)], next_banks(m, c)[0][:, :], ACT.Copy).then_inc(s(f"m{m}_xthi_done"), 1)

        def dve_next_lo(dve, m, c):
            cols = ds(c * W, W)
            dve.wait_ge(s(f"m{m}_xthi_done"), c + 1)
            dve.tensor_tensor(XTLO[:, cols], next_banks(m, c)[0][:, :], XTHI[:, cols].bitcast(f32), ALU.subtract
                              ).then_inc(s(f"m{m}_xtlo_done"), 1)

        def pe_next_logits(pe, m, c):
            wr = slice(m * 128, (m + 1) * 128)
            cols = ds(c * W, W)
            pe.wait_ge(s(f"m{m}_xtlo_done"), c + 1)
            at_least(pe, s(f"m{m}_lt_done"), c)
            if m == 0 and not (isinstance(c, int) and c == 0):
                pe.wait_ge(s(f"m{m}_acc_chain"), ONE + (c - 1) * (E + 1) + 1)
            for n, (l_, r_) in enumerate(((WRHI, XTHI), (WRHI, XTLO), (WRLO, XTHI))):
                l = pe.matmul(next_banks(m, c)[1][:, :], l_[:, wr], r_[:, cols], start=n == 0, stop=n == 2)
            l.then_inc(s(f"m{m}_lt_ready"), 1)

        def act_next_logits(act, m, c):
            act.wait_ge(s(f"m{m}_lt_ready"), c + 1)
            at_least(act, s(f"m{m}_lg_ready"), c)
            act.activation(LTS[:, :], next_banks(m, c)[1][:, :], ACT.Copy).then_inc(s(f"m{m}_lt_done"), 1)

        def pe_next_logits_back(pe, m, c):
            pe.wait_ge(s(f"m{m}_lt_done"), c + 1)
            for t in range(CH):
                l = pe.transpose(next_banks(m, c)[0][:, t * T:(t + 1) * T], LTS[:, t * T:(t + 1) * T], ident[:, :])
            l.then_inc(s(f"m{m}_lg_ready"), 1)

        def dve_next_route(dve, m, c, part):
            chain = s(f"m{m}_route")
            full = [128, CH, E]
            step = [c * ROUTE + (0, 6, DIFF_STEP)[part]]

            def then(i):
                i.then_inc(chain, 1)
                step[0] = step[0] + 1
                dve.wait_ge(chain, step[0])

            def over(v):
                return v[:, :].unsqueeze(2).to_broadcast(full)

            lg, first, second = LG[:, :, :], RT[0][:, :, :], RT[1][:, :, :]
            if part == 0:
                dve.wait_ge(s(f"m{m}_lg_ready"), c + 1)
                src = next_banks(m, c)[0][:, :].rearrange("p (t c) -> p t c", c=128)[:, :, 0:E]
                bias = BRB[:, :] if m == 0 else ZERO[:, 0:E]
                dve.tensor_tensor(lg, src, bias.unsqueeze(1).to_broadcast(full), ALU.add).then_inc(s(f"m{m}_lg_done"), 1)
                dve.wait_ge(s(f"m{m}_lg_done"), c + 1)
                then(dve.tensor_reduce(RV[0][:, :], lg, AX.X, ALU.max))
                then(dve.tensor_tensor(first, lg, over(RV[0]), ALU.is_equal))
                then(dve.tensor_tensor(first, first, RANK[:, :, :], ALU.mult))
                then(dve.tensor_reduce(RV[1][:, :], first, AX.X, ALU.max))
                then(dve.tensor_tensor(first, first, over(RV[1]), ALU.is_equal))
                then(dve.scalar_tensor_tensor(out=second, in0=first, scalar=-BIG, in1=lg, op0=ALU.mult, op1=ALU.add))
            elif part == 1:
                then(dve.tensor_reduce(RV[2][:, :], second, AX.X, ALU.max))
                then(dve.tensor_tensor(second, second, over(RV[2]), ALU.is_equal))
                then(dve.tensor_tensor(second, second, RANK[:, :, :], ALU.mult))
                then(dve.tensor_reduce(RV[1][:, :], second, AX.X, ALU.max))
                then(dve.tensor_tensor(RV[3][:, :], RV[2][:, :], RV[0][:, :], ALU.subtract))
                then(dve.tensor_tensor(second, second, over(RV[1]), ALU.is_equal))
            else:
                dve.wait_ge(s(f"m{m}_exp_ready"), c + 1)
                then(dve.tensor_scalar(RV[5][:, :], RV[4][:, :], 1.0, None, ALU.add))
                then(dve.reciprocal(RV[5][:, :], RV[5][:, :]))
                then(dve.tensor_tensor(RV[4][:, :], RV[4][:, :], RV[5][:, :], ALU.mult))
                then(dve.tensor_tensor(first, first, over(RV[5]), ALU.mult))
                then(dve.tensor_tensor(second, second, over(RV[4]), ALU.mult))
                then(dve.tensor_tensor(WGT[:, :, :], first, second, ALU.add))

        def pool_second_weight(pool, m, c):
            pool.wait_ge(s(f"m{m}_route"), c * ROUTE + DIFF_STEP - 1)
            pool.tensor_tensor(RV[4][:, :], EULER[:, :], RV[3][:, :], ALU.pow).then_inc(s(f"m{m}_exp_ready"), 1)

        def dve_chunk(dve, m, c, first, final):
            q = lambda name: s(f"m{m}_{name}")
            combs = E + 1 - m
            steps = c * E
            nxt, z = c + 1, lag(m, c)
            for e in range(E):
                if e == 3 + z and not final:
                    dve_next_lo(dve, m, nxt)
                for j in range(2):
                    n = 2 * (steps + e) + j + 1
                    dve.wait_ge(q("sil_done"), n)
                    dve.wait_ge(q("up_g"), n)
                    if m == 0:
                        l = dve.scalar_tensor_tensor(out=HT[e % 2][:, j, :], in0=P[2 * j + 1][:, :],
                                                     scalar=COLS[:, e * 4 + 2 + j:e * 4 + 3 + j], in1=SIL[j][:, :],
                                                     op0=ALU.add, op1=ALU.mult)
                    else:
                        l = dve.tensor_tensor(HT[e % 2][:, j, :], P[2 * j + 1][:, :], SIL[j][:, :], ALU.mult)
                    l.then_inc(q("h_done"), 1)
                if e == 0:
                    if first and m == 1:
                        dve_next_route(dve, m, 0, 0)
                        dve_next_route(dve, m, 0, 1)
                        dve_final_normalised(dve, 1)
                        dve_next_route(dve, m, 0, 2)
                    if not first:
                        dve_combine(dve, m, c - 1, LAST)
                        dve_update(dve, m, c - 1)
                    dve.wait_ge(q("route"), (c + 1) * ROUTE)
                    dve.wait_ge(q("acc_chain"), ONE + c * combs)
                    dve.tensor_copy(WSL[:, :], WGT[:, :, :].rearrange("p t e -> p (t e)")).then_inc(q("wsl_done"), 1)
                    dve.wait_ge(q("wsl_done"), c + 1)
                    if not first and m == 0:
                        dve_stats(dve, X, (c - 1) * CH, CH, G_MIX + c - 1, (q("chunk_done"), ONE + c))
                if e == 1 and m == 0:
                    dve.wait_ge(q("b2_ready"), c + 1)
                    dve.wait_ge(q("chunk_done"), ONE + c)
                    dve.tensor_copy(ACC[:, :], P[7][:, :]).then_inc(q("acc_chain"), 1)
                if e >= 1:
                    dve_combine(dve, m, c, e - 1)
                if first and m == 1:
                    if e == 1:
                        dve_unit_stats(dve, LAST_UNIT)
                    if e in (2, 4, 6):
                        dve_final_stats(dve, e // 2)
                    if e in (2, 5):
                        dve_final_normalised(dve, 2 if e == 2 else 3)
                if not final:
                    if e == 1 + z:
                        dve_next_normalised(dve, m, nxt, G_MIX if m == 0 else G_DEC[1] + 1 if first else G_END)
                    for part in range(3):
                        if e == min(5 + part + z, LAST):
                            dve_next_route(dve, m, nxt, part)

        def dve_combine(dve, m, c, e):
            q = lambda name: s(f"m{m}_{name}")
            combs = E + 1 - m
            dve.wait_ge(q("y_ready"), c * E + e + 1)
            dve.wait_ge(q("acc_chain"), ONE + c * combs + e + (combs - E))
            if m == 1 and e == 0:
                dve.wait_ge(q("chunk_done"), ONE + c)
            y = P[4 + e % 2]
            for t in range(CH):
                tok = slice(t * D, (t + 1) * D)
                w = WSL[:, t * E + e:t * E + e + 1]
                if m == 1 and e == 0:
                    l = dve.tensor_scalar(ACC[:, tok], y[:, tok], w, None, ALU.mult)
                else:
                    l = dve.scalar_tensor_tensor(out=ACC[:, tok], in0=y[:, tok], scalar=w, in1=ACC[:, tok],
                                                 op0=ALU.mult, op1=ALU.add)
            l.then_inc(q("acc_chain"), 1)

        def dve_update(dve, m, c):
            dve.wait_ge(s(f"m{m}_acc_chain"), ONE + (c + 1) * (E + 1 - m))
            xc = X[:, ds(c * W, W)]
            dve.scalar_tensor_tensor(out=xc, in0=ACC[:, :], scalar=GATE[:, 2 + m:3 + m], in1=xc,
                                     op0=ALU.mult, op1=ALU.add).then_inc(s(f"m{m}_chunk_done"), 1)

        def dve_mixture(dve, m):
            dve_chunk(dve, m, 0, True, False)
            with dve.Fori(1, CHUNKS - 1) as c:
                dve_chunk(dve, m, c, False, False)
            dve_chunk(dve, m, CHUNKS - 1, False, True)
            if m == 0:
                dve.wait_ge(s("m0_h_done"), H0 + 2 * E * CHUNKS)
                dve_unit_normalised(dve, 0)
            dve_combine(dve, m, CHUNKS - 1, LAST)
            dve_update(dve, m, CHUNKS - 1)
            if m == 0:
                dve_stats(dve, X, (CHUNKS - 1) * CH, CH, G_MIX + CHUNKS - 1, (s("m0_chunk_done"), ONE + CHUNKS))

        def pe_up(pe, m, c, e):
            for j in range(2):
                pe.wait_ge(s(f"m{m}_h_done"), H0 + 2 * (c * E + e - 1) + j + 1)
                for bank, col, ready in ((P[2 * j], j, "up_a"), (P[2 * j + 1], 2 + j, "up_g")):
                    wc = slice(e * 2 * H + col * 128, e * 2 * H + (col + 1) * 128)
                    for n, (l_, r_) in enumerate(((W1HI[m], XTHI), (W1HI[m], XTLO), (W1LO[m], XTHI))):
                        l = pe.matmul(bank[:, :], l_[:, wc], r_[:, ds(c * W, W)], start=n == 0, stop=n == 2)
                    l.then_inc(s(f"m{m}_{ready}"), 1)

        def pe_down(pe, m, c, e):
            combs = E + 1 - m
            pe.wait_ge(s(f"m{m}_h_done"), H0 + 2 * (c * E + e) + 2)
            if m == 1 and e == 0 and isinstance(c, int) and c == 0:
                pe.wait_ge(s("m1_lg_done"), 1)
            if e >= 2:
                pe.wait_ge(s(f"m{m}_acc_chain"), ONE + c * combs + combs - E + e - 1)
            elif not (isinstance(c, int) and c == 0):
                pe.wait_ge(s(f"m{m}_acc_chain"), ONE + c * combs + e - 1)
            for t in range(CH):
                for j in range(2):
                    l = pe.matmul(P[4 + e % 2][:, t * D:(t + 1) * D], HT[e % 2][:, j, t * T:(t + 1) * T],
                                  W2S[m][:, (2 * e + j) * D:(2 * e + j + 1) * D], start=j == 0, stop=j == 1)
            l.then_inc(s(f"m{m}_y_ready"), 1)

        def pe_chunk(pe, m, c, first, final):
            q = lambda name: s(f"m{m}_{name}")
            nxt, z = c + 1, lag(m, c)
            for e in range(E):
                pe_up(pe, m, c, e)
                if e == 0 and m == 0:
                    pe.wait_ge(q("route"), (c + 1) * ROUTE)
                    pe.wait_ge(q("lg_done"), c + 1)
                    for t in range(CH):
                        l = pe.transpose(P[6][0:E, t * T:(t + 1) * T], WGT[:, t, :], ident[:, :])
                    l.then_inc(q("wt_ready"), 1)
                if e == 0 and not first:
                    pe_down(pe, m, c - 1, LAST)
                if e == 1 and m == 0:
                    pe.wait_ge(q("wt_done"), c + 1)
                    for t in range(CH):
                        l = pe.matmul(P[7][:, t * D:(t + 1) * D], WTS[:, t * T:(t + 1) * T], B2S[:, :], start=True, stop=True)
                    l.then_inc(q("b2_ready"), 1)
                if e == 2 + z and not final:
                    pe_next_transposed(pe, m, nxt)
                if e >= 1:
                    pe_down(pe, m, c, e - 1)
                if e == 3 + z and not final:
                    pe_next_logits(pe, m, nxt)
                if e == 4 + z and not final:
                    pe_next_logits_back(pe, m, nxt)

        def pe_mixture(pe, m):
            if m == 0:
                pe.wait_ge(s("m0_lg_done"), 1)
            pe_chunk(pe, m, 0, True, False)
            with pe.Fori(1, CHUNKS - 1) as c:
                pe_chunk(pe, m, c, False, False)
            pe_chunk(pe, m, CHUNKS - 1, False, True)
            pe_down(pe, m, CHUNKS - 1, LAST)

        def act_chunk(act, m, c, first, final):
            q = lambda name: s(f"m{m}_{name}")
            z = lag(m, c)
            for e in range(E):
                if e == 1 and m == 0:
                    act.wait_ge(q("wt_ready"), c + 1)
                    at_least(act, q("b2_ready"), c)
                    act.activation(WTS[:, :], P[6][0:E, :], ACT.Copy).then_inc(q("wt_done"), 1)
                if e == 3 + z and not final:
                    act_next_hi(act, m, c + 1)
                if e == 4 + z and not final:
                    act_next_logits(act, m, c + 1)
                for j in range(2):
                    n = 2 * (c * E + e) + j
                    act.wait_ge(q("up_a"), n + 1)
                    act.wait_ge(q("h_done"), H0 + n - 1)
                    bias = COLS[:, e * 4 + j:e * 4 + j + 1] if m == 0 else 0.0
                    act.activation(SIL[j][:, :], P[2 * j][:, :], ACT.Silu, bias=bias).then_inc(q("sil_done"), 1)

        def act_mixture(act, m):
            act_chunk(act, m, 0, True, False)
            with act.Fori(1, CHUNKS - 1) as c:
                act_chunk(act, m, c, False, False)
            act_chunk(act, m, CHUNKS - 1, False, True)

        for name in ("d_loaded0 d_loaded1 d_loaded2 d_loaded3 dy_ready dyt_ready dyt_done dgb_done ds_ready dneg_done dexp_done drcp_done dt_ready0 dt_ready1 dpt_done0 dpt_done1 "
                     "dav_ready dres_done dconst dfin_ready dh_ready dh_done dfin_chain").split():
            s(name)
        LAST_UNIT = 3 * UNITS - 1
        SC = float(D) ** -0.5
        GAMMA = {1: COL_GB, 2: COL_GB + 2}
        hc = DFF // 128

        def s_bank(n, v):
            return P[2 * (n % 2) + v]

        def t_bank(n, v):
            return P[4 + 2 * (n % 2) + v]

        def buf(a, n, width):
            return a[:, (n % 2) * width:(n % 2 + 1) * width]

        def hidden(n, m):
            return buf(UPT if m < 2 else UP, n, U * 512)[:, (m % 2) * W:(m % 2 + 1) * W]

        def context(k):
            return (CU if k < 2 else WT[:, 2048:3072])[:, (k % 2) * U * N:(k % 2 + 1) * U * N]

        def decoder_loads(sp):
            sp.wait_ge(s("m0_chunk_done"), ONE + CHUNKS)
            for k in range(UNITS):
                sp.dma_start(context(k).rearrange("p (t d) -> p t d", d=D),
                             ctxt[:, k * U * QB:(k + 1) * U * QB, :]).then_inc(s(f"d_loaded{k}"), 16)

        def final_store(sp):
            for c in range(CHUNKS):
                sp.wait_ge(s("m1_chunk_done"), ONE + c + 1)
                sp.dma_start(outt[:, c * CH:(c + 1) * CH, :], X[:, c * W:(c + 1) * W].rearrange("p (t d) -> p t d", d=D)
                             ).then_inc(s("out_stored"), 16)
            sp.wait_ge(s("out_stored"), 16 * CHUNKS)

        def blocks_of(stage):
            return ((0, N), (N, N)) if stage == 1 else ((0, T), (T, N))

        def dve_unit_normalised(dve, n):
            stage, k = n // UNITS, n % UNITS
            src, group = ((X, G_MIX), (YR, G_SELF), (YR, G_CROSS))[stage]
            dve.wait_ge(s("rstd_ready"), group + k + 1)
            at_least(dve, s("dres_done"), n - 1)
            for t in range(U * QB):
                tile = k * U * QB + t
                l = dve.tensor_scalar(buf(YS, n, U * N)[:, t * D:(t + 1) * D], src[:, tile * D:(tile + 1) * D],
                                      MV[:, tile, 0:1], RSTD[:, tile:tile + 1], ALU.subtract, ALU.mult)
                if t % QB == QB - 1:
                    l.then_inc(s("dy_ready"), 1)

        def pool_unit_affine(pool, n):
            stage = n // UNITS
            done = 2 * (n - UNITS)
            y = buf(YS, n, U * N).rearrange("p (t d) -> p t d", d=D)
            full = [128, U * QB, D]
            pool.wait_ge(s("dyt_ready"), U * (n + 1))
            pool.tensor_tensor(y, y, BC[:, 2 * stage - 1, :].unsqueeze(1).to_broadcast(full), ALU.mult
                              ).then_inc(s("dgb_done"), 1)
            pool.wait_ge(s("dgb_done"), done + 1)
            pool.tensor_tensor(y, y, BC[:, 2 * stage, :].unsqueeze(1).to_broadcast(full), ALU.add
                              ).then_inc(s("dgb_done"), 1)

        def dve_unit_max(dve, n):
            stage = n // UNITS
            up = buf(UP, n, U * 512)
            for v in range(U):
                dve.wait_ge(s("ds_ready"), U * n + v + 1)
                for q, (lo, w) in enumerate(blocks_of(stage)):
                    m = ZERO[:, :] if stage == 1 else TRI[:, lo:lo + w]
                    k = (n % 2) * U * QB + v * QB + q
                    dve.tensor_tensor_reduce(out=up[:, v * 512 + lo:v * 512 + lo + w], in0=s_bank(n, v)[:, lo:lo + w],
                                             in1=m, scale=-SC, scalar=HUGE, op0=ALU.add, op1=ALU.min,
                                             accum_out=UNEG[:, k:k + 1]).then_inc(s("dneg_done"), 1)

        def unit_probs(eng, copy, n, v):
            w = 512 if n >= UNITS else 3 * T
            eng.wait_ge(s(f"dt_ready{v}"), n + 1)
            copy(buf(UPT, n, U * 512)[:, v * 512:v * 512 + w], t_bank(n, v)[:, 0:w]).then_inc(s(f"dpt_done{v}"), 1)

        def dve_unit_residual(dve, n):
            k = n % UNITS
            c = (n % 2) * U * QB
            dve.wait_ge(s("dexp_done"), U * QB * (n + 1))
            dve.reciprocal(URCP[:, c:c + U * QB], USUM[:, c:c + U * QB]).then_inc(s("drcp_done"), 1)
            dve.wait_ge(s("drcp_done"), n + 1)
            at_least(dve, s("dgb_done"), 2 * (n - UNITS + 1))
            for v in range(U):
                dve.wait_ge(s("dav_ready"), U * n + v + 1)
                for q in range(QB):
                    t = v * QB + q
                    tok = slice((k * U * QB + t) * D, (k * U * QB + t + 1) * D)
                    l = dve.scalar_tensor_tensor(out=YR[:, tok], in0=s_bank(n, v)[:, q * D:(q + 1) * D],
                                                 scalar=URCP[:, c + t:c + t + 1], in1=buf(YS, n, U * N)[:, t * D:(t + 1) * D],
                                                 op0=ALU.mult, op1=ALU.add)
            l.then_inc(s("dres_done"), 1)

        def dve_unit_fed(dve, n):
            k = n % UNITS
            dve.wait_ge(s("dav_ready"), U * 2 * UNITS + n - 2 * UNITS + 1)
            dve.wait_ge(s("dgb_done"), 2 * (n - UNITS + 1))
            dve.tensor_tensor(YR[:, k * W:(k + 1) * W], t_bank(n, 0)[:, :], buf(YS, n, U * N), ALU.add
                              ).then_inc(s("dres_done"), 1)

        def dve_unit_stats(dve, n):
            stage, k = n // UNITS, n % UNITS
            dve_stats(dve, YR, k * U * QB, U * QB, (G_SELF + k, G_CROSS + k, G_FF[k])[stage], (s("dres_done"), n + 1))

        def dve_final_normalised(dve, k):
            dve.wait_ge(s("rstd_ready"), G_FF[k] + 1)
            for t in range(k * U * QB, (k + 1) * U * QB):
                l = dve.tensor_scalar(YR[:, t * D:(t + 1) * D], YR[:, t * D:(t + 1) * D], MV[:, t, 0:1], RSTD[:, t:t + 1],
                                      ALU.subtract, ALU.mult)
            l.then_inc(s("dfin_ready"), 1)

        def pool_final(pool, k):
            fc = s("dfin_chain")
            full = [128, U * QB, D]
            y = YR[:, k * W:(k + 1) * W]
            y3 = y.rearrange("p (t d) -> p t d", d=D)
            xs = X[:, k * W:(k + 1) * W]
            pool.wait_ge(s("dconst"), 1)
            pool.wait_ge(s("dfin_ready"), k + 1)
            pool.tensor_tensor(y3, y3, BC[:, 5, :].unsqueeze(1).to_broadcast(full), ALU.mult).then_inc(fc, 1)
            pool.wait_ge(fc, 3 * k + 1)
            pool.tensor_tensor(y3, y3, BC[:, 6, :].unsqueeze(1).to_broadcast(full), ALU.add).then_inc(fc, 1)
            pool.wait_ge(fc, 3 * k + 2)
            pool.tensor_tensor(xs, xs, y, ALU.add).then_inc(fc, 1)

        def dve_final_stats(dve, k):
            dve_stats(dve, X, k * U * QB, U * QB, G_DEC[k], (s("dfin_chain"), 3 * k + 3))

        def dve_decoder(dve):
            dve.tensor_scalar(BC[:, 5, :], BC[:, 5, :], GATE[:, 1:2], None, ALU.mult)
            dve.tensor_scalar(BC[:, 6, :], BC[:, 6, :], GATE[:, 1:2], None, ALU.mult)
            dve.tensor_tensor(BC[:, 4, :], BC[:, 4, :], BC[:, 7, :], ALU.add).then_inc(s("dconst"), 1)
            dve.wait_ge(s("dconst"), 1)
            for n in range(LAST_UNIT + 1):
                if n < 2 * UNITS:
                    dve_unit_max(dve, n)
                if 1 <= n <= 2 * UNITS:
                    dve_unit_residual(dve, n - 1)
                if n == LAST_UNIT:
                    dve_final_stats(dve, 0)
                    dve_unit_stats(dve, n - 1)
                    dve_next_normalised(dve, 1, 0, G_DEC[0] + 1)
                else:
                    dve_unit_normalised(dve, n + 1)
                if n < 2 * UNITS:
                    unit_probs(dve, dve.tensor_copy, n, 1)
                if 1 <= n < LAST_UNIT:
                    dve_unit_stats(dve, n - 1)
                if n == 2 * UNITS + 2:
                    dve_final_normalised(dve, 0)
                if n >= 2 * UNITS:
                    dve_unit_fed(dve, n)
            dve_next_lo(dve, 1, 0)

        def pe_unit_transposed(pe, n):
            stage = n // UNITS
            at_least(pe, s("dres_done"), n - 1)
            if stage == 1:
                pe.wait_ge(s(f"d_loaded{n % UNITS}"), 16)
            for v in range(U):
                pe.wait_ge(s("dy_ready"), U * n + v + 1)
                for k in range(QB):
                    c = v * N + k * D
                    l = pe.transpose(s_bank(n, v)[:, k * T:(k + 1) * T], buf(YS, n, U * N)[:, c:c + D], ident[:, :])
                if stage == 1:
                    for k in range(QB):
                        c = v * N + k * D
                        l = pe.transpose(s_bank(n, v)[:, N + k * T:N + (k + 1) * T], context(n % UNITS)[:, c:c + D],
                                         ident[:, :])
                l.then_inc(s("dyt_ready"), 1)

        def pe_unit_scores(pe, n):
            stage = n // UNITS
            for v in range(U):
                pe.wait_ge(s("dyt_done"), U * n + v + 1)
                yt = buf(YT, n, U * 512)[:, v * 512:(v + 1) * 512]
                for q, (lo, w) in enumerate(blocks_of(stage)):
                    keys = yt[:, N:2 * N] if stage == 1 else yt[:, 0:w]
                    l = pe.matmul(s_bank(n, v)[:, lo:lo + w], yt[:, q * T:(q + 1) * T], keys, start=True, stop=True)
                l.then_inc(s("ds_ready"), 1)

        def pe_unit_probs(pe, n):
            stage = n // UNITS
            up = buf(UP, n, U * 512)
            for v in range(U):
                pe.wait_ge(s("dexp_done"), U * QB * n + (v + 1) * QB)
                at_least(pe, s(f"dpt_done{v}"), n - 1)
                for k in range(4 if stage == 1 else 3):
                    c = v * 512 + k * T
                    l = pe.transpose(t_bank(n, v)[:, k * T:(k + 1) * T], up[:, c:c + T], ident[:, :])
                l.then_inc(s(f"dt_ready{v}"), 1)

        def pe_unit_values(pe, n):
            stage = n // UNITS
            values = context(n % UNITS) if stage == 1 else buf(YS, n, U * N)
            for v in range(U):
                pe.wait_ge(s(f"dpt_done{v}"), n + 1)
                for q in range(QB):
                    last = QB - 1 if stage == 1 else q
                    for k in range(last + 1):
                        c = v * 512 + (2 * q + k if stage == 1 else q + k) * T
                        l = pe.matmul(s_bank(n, v)[:, q * D:(q + 1) * D], buf(UPT, n, U * 512)[:, c:c + T],
                                      values[:, v * N + k * D:v * N + (k + 1) * D], start=k == 0, stop=k == last)
                l.then_inc(s("dav_ready"), 1)

        def pe_unit_hidden(pe, n):
            k = n - 2 * UNITS
            pe.wait_ge(s("dyt_done"), U * (n + 1))
            for m, bank in enumerate((t_bank(n, 0), t_bank(n, 1), s_bank(n, 0), s_bank(n, 1))):
                if m < 2 and k < 2:
                    pe.wait_ge(s(f"dpt_done{m}"), n - 1)
                pe.matmul(bank[:, :], L1W1[:, m * 128:(m + 1) * 128], buf(YT, n, U * 512)[:, 0:W], start=True, stop=True
                          ).then_inc(s("dh_ready"), 1)

        def pe_unit_down(pe, n):
            k = n - 2 * UNITS
            pe.wait_ge(s("dh_done"), hc * (k + 1))
            for t in range(CH):
                for m in range(hc):
                    l = pe.matmul(t_bank(n, 0)[:, t * D:(t + 1) * D], hidden(n, m)[:, t * T:(t + 1) * T], L1W2[:, m, :],
                                  start=m == 0, stop=m == hc - 1)
            l.then_inc(s("dav_ready"), 1)

        def pe_decoder(pe):
            pe_unit_transposed(pe, 0)
            pe_unit_scores(pe, 0)
            pe.wait_ge(s("m0_chunk_done"), ONE + CHUNKS)
            for n in range(LAST_UNIT + 1):
                if n < 2 * UNITS:
                    pe_unit_probs(pe, n)
                if n < LAST_UNIT:
                    pe_unit_transposed(pe, n + 1)
                if n >= 2 * UNITS:
                    pe_unit_down(pe, n)
                if n + 1 < 2 * UNITS:
                    pe_unit_scores(pe, n + 1)
                elif n < LAST_UNIT:
                    pe_unit_hidden(pe, n + 1)
                if n < 2 * UNITS:
                    pe_unit_values(pe, n)
            pe.wait_ge(s("dres_done"), LAST_UNIT)
            pe_next_transposed(pe, 1, 0)
            pe_next_logits(pe, 1, 0)
            pe_next_logits_back(pe, 1, 0)

        def act_unit_transposed(act, n):
            stage = n // UNITS
            for v in range(U):
                act.wait_ge(s("dyt_ready"), U * n + v + 1)
                width = N if stage == 2 else 512
                yt = buf(YT, n, U * 512)[:, v * width:(v + 1) * width]
                if stage == 0:
                    l = act.activation(yt[:, 0:N], s_bank(n, v)[:, 0:N], ACT.Copy)
                else:
                    g = GAMMA[stage]
                    l = act.activation(yt[:, 0:N], s_bank(n, v)[:, 0:N], ACT.Identity, bias=COLS[:, g + 1:g + 2],
                                       scale=COLS[:, g:g + 1])
                if stage == 1:
                    l = act.activation(yt[:, N:2 * N], s_bank(n, v)[:, N:2 * N], ACT.Copy)
                l.then_inc(s("dyt_done"), 1)

        def act_unit_exp(act, n):
            stage = n // UNITS
            up = buf(UP, n, U * 512)
            for v in range(U):
                for q, (lo, w) in enumerate(blocks_of(stage)):
                    k = (n % 2) * U * QB + v * QB + q
                    act.wait_ge(s("dneg_done"), U * QB * n + v * QB + q + 1)
                    p = up[:, v * 512 + lo:v * 512 + lo + w]
                    act.activation(p, p, ACT.Exp, bias=UNEG[:, k:k + 1], scale=-1.0, accum_out=USUM[:, k:k + 1]
                                   ).then_inc(s("dexp_done"), 1)

        def act_unit_relu(act, n):
            k = n - 2 * UNITS
            for m in range(hc):
                bank = (t_bank(n, 0), t_bank(n, 1), s_bank(n, 0), s_bank(n, 1))[m]
                act.wait_ge(s("dh_ready"), hc * k + m + 1)
                act.activation(hidden(n, m), bank[:, :], ACT.Relu, bias=COLS[:, COL_B1 + m:COL_B1 + m + 1]
                               ).then_inc(s("dh_done"), 1)

        def act_decoder(act):
            act_unit_transposed(act, 0)
            for n in range(LAST_UNIT + 1):
                if n < 2 * UNITS:
                    act_unit_exp(act, n)
                    unit_probs(act, lambda o, i: act.activation(o, i, ACT.Copy), n, 0)
                    act_unit_transposed(act, n + 1)
                else:
                    act_unit_relu(act, n)
                    if n < LAST_UNIT:
                        act_unit_transposed(act, n + 1)
            act_next_hi(act, 1, 0)
            act_next_logits(act, 1, 0)
            act.wait_ge(s("dres_done"), LAST_UNIT + 1)

        def split1_loads(sp):
            for e in range(E):
                sp.wait_ge(s("w1lo_split"), E) if e == 0 else sp.wait_ge(s("w1lo_split1"), e)
                sp.dma_start(W1RAW[:, 0:H], m1_wg[e]).then_inc(s("w1raw_loaded1"), 16)
                sp.dma_start(W1RAW[:, H:2 * H], m1_wu[e]).then_inc(s("w1raw_loaded1"), 16)

        def pool_split1(pool, e):
            w1e = slice(e * 2 * H, (e + 1) * 2 * H)
            pool.wait_ge(s("w1raw_loaded1"), 32 * (e + 1))
            pool.tensor_copy(W1HI[1][:, w1e], W1RAW[:, :]).then_inc(s("w1hi_split1"), 1)
            pool.wait_ge(s("w1hi_split1"), e + 1)
            pool.tensor_tensor(W1LO[1][:, w1e], W1RAW[:, :], W1HI[1][:, w1e].bitcast(f32), ALU.subtract
                               ).then_inc(s("w1lo_split1"), 1)

        @block.sync
        def _(sp):
            for k, w in enumerate((Wq, Wk, Wv)):
                sp.dma_start(RAW[:, k * INNER:(k + 1) * INNER], w).then_inc(s("proj_loaded" if k < 2 else "wv_loaded"), 16)
            sp.dma_start(WOS[:, :, :], Wo.rearrange("(c p) d -> p c d", p=128)).then_inc(s("wo_loaded"), 16)

            def attention_loads(b):
                at_least(sp, s("xct_ready"), b)
                sp.dma_start(CS[:, :, :], ctxt[:, ds(b * QB, QB), :]).then_inc(s("c_loaded"), 16)
                at_least(sp, s("w1lo_split"), b)
                sp.dma_start(W1RAW[:, :], m0_W1.rearrange("e d h -> d e h")[:, ds(b, 1), :].rearrange("d e h -> d (e h)")
                             ).then_inc(s("w1raw_loaded"), 16)

            attention_loads(0)
            small_loads(sp)
            sp.dma_start(L1W1[:, :], w1).then_inc(s("l1w_loaded"), 16)
            sp.dma_start(L1W2[:, :, :], w2.rearrange("(c p) d -> p c d", p=128)).then_inc(s("l1w_loaded"), 16)
            sp.dma_start(W2S[0][:, :].rearrange("p (g d) -> p g d", d=D),
                         m0_W2.rearrange("e (j p) d -> p (e j) d", p=128)).then_inc(s("w2_loaded"), 16)
            sp.dma_start(W2S[1][:, :].rearrange("p (g d) -> p g d", d=D),
                         m1_wd.rearrange("e (j p) d -> p (e j) d", p=128)).then_inc(s("w2_loaded"), 16)
            with sp.Fori(1, B) as b:
                attention_loads(b)
            split1_loads(sp)
            decoder_loads(sp)
            final_store(sp)

        @block.gpsimd
        def _(pool):
            pool.memset(ident[:, :], 0.0).then_inc(s("pool_const"), 1)
            pool.memset(TRI[:, :], 0.0).then_inc(s("pool_const"), 1)
            pool.memset(ROWS[:, :], 0.0).then_inc(s("rows_zero"), 1)
            pool.memset(WRF[:, :], 0.0).then_inc(s("wrf_zero"), 1)
            pool.memset(HALF[:, :], -0.5)
            pool.memset(EULER[:, :], math.e)
            pool.memset(EPS2[:, :, 0:1], 0.0)
            pool.memset(EPS2[:, :, 1:2], EPS)
            pool.memset(ZERO[:, :], 0.0)
            for e in range(E):
                l = pool.memset(RANK[:, :, e:e + 1], float(E - e))
            l.then_inc(s("pool_const"), 1)
            pool.wait_ge(s("pool_const"), 2)
            pool.affine_select(out=ident[:, :], in_=ident[:, :], compare_op=ALU.not_equal, fill=1.0, base=0,
                               pattern=[[-1, 128]], channel_multiplier=1).then_inc(s("ident_ready"), 1)
            pool.affine_select(out=TRI[:, 0:T], in_=TRI[:, 0:T], compare_op=ALU.is_ge, fill=-BIG, base=0,
                               pattern=[[-1, T]], channel_multiplier=1)
            pool.affine_select(out=TRI[:, T:3 * T], in_=TRI[:, T:3 * T], compare_op=ALU.is_ge, fill=-BIG, base=T,
                               pattern=[[-1, N]], channel_multiplier=1).then_inc(s("ident_ready"), 1)
            pool_rstd(pool, 0, CH, G_START)
            pool_attention(pool, 0, True)
            with pool.Fori(1, B) as b:
                pool_attention(pool, b, False)
            pool_second_weight(pool, 0, 0)
            pool_rstd(pool, (B - 1) * QB, QB, G_ATT + B - 1)
            pool.wait_ge(s("acc_ready"), B)
            for c in range(CHUNKS):
                if c >= 1:
                    pool_rstd(pool, (c - 1) * CH, CH, G_MIX + c - 1)
                if c < CHUNKS - 1:
                    pool_second_weight(pool, 0, c + 1)
                for e in range(c * E // CHUNKS, (c + 1) * E // CHUNKS):
                    pool_split1(pool, e)
            pool_rstd(pool, (CHUNKS - 1) * CH, CH, G_MIX + CHUNKS - 1)
            for n in range(1, LAST_UNIT):
                k = (n - 1) % UNITS
                pool_rstd(pool, k * U * QB, U * QB, (G_SELF + k, G_CROSS + k, G_FF[k])[(n - 1) // UNITS])
                if n + 1 >= UNITS:
                    pool_unit_affine(pool, n + 1)
            pool_final(pool, 0)
            pool_rstd(pool, 0, U * QB, G_DEC[0])
            pool_rstd(pool, 2 * U * QB, U * QB, G_FF[2])
            pool_second_weight(pool, 1, 0)
            pool_final(pool, 1)
            pool_rstd(pool, 3 * U * QB, U * QB, G_FF[3])
            pool_rstd(pool, U * QB, U * QB, G_DEC[1])
            for k in (2, 3):
                pool_final(pool, k)
                pool_rstd(pool, k * U * QB, U * QB, G_DEC[k])
            for c in range(1, CHUNKS):
                pool_second_weight(pool, 1, c)

        @block.scalar
        def _(act):
            act_loads(act)
            act.wait_ge(s("gates_loaded"), 32)
            act.activation(GATE[:, :], GATE[:, :], ACT.Tanh).then_inc(s("gate_ready"), 1)
            for g in (0, 2, 4):
                act.wait_ge(s("wt_ready"), g + 1)
                act.activation(WT[:, g * 512:(g + 1) * 512], P[g][:, :], ACT.Copy).then_inc(s("wt_act"), 1)
            act.activation(WVHI[:, :], RAW[:, 2 * INNER:3 * INNER], ACT.Copy).then_inc(s("wv_act"), 1)
            for k in range(4):
                act.wait_ge(s("g_ready"), k + 1)
                dst = GHI[:, :].rearrange("p (h d) -> p h d", d=D)[:, 8 * (k // 2) + k % 2:8 * (k // 2) + 8:2, :]
                act.activation(dst, P[k][:, :].rearrange("p (h d) -> p h d", d=D), ACT.Copy, scale=DH ** -0.5
                               ).then_inc(s("ghi_done"), 1)
            act_operands(act, 0)
            act.wait_ge(s("cols_done"), 2)
            act.activation(WRHI[:, :], WRF[:, :], ACT.Copy).then_inc(s("wr_act"), 1)
            act_attention(act, 0, True, False)
            with act.Fori(1, B - 1) as b:
                act_attention(act, b, False, False)
            act_attention(act, B - 1, False, True)
            act_out(act, B - 1, PAIRS - 2)
            act_next_hi(act, 0, 0)
            act_next_logits(act, 0, 0)
            act_out(act, B - 1, PAIRS - 1)
            act_mixture(act, 0)
            act_decoder(act)
            act_mixture(act, 1)

        @block.vector
        def _(dve):
            open_counts(dve)
            dve.wait_ge(s("pool_const"), 3)
            dve.wait_ge(s("ident_ready"), 2)
            dve.wait_ge(s("x0_loaded"), 16)
            dve_stats(dve, X, 0, CH, G_START)
            for g in (1, 3, 5):
                dve.wait_ge(s("wt_ready"), g + 1)
                dve.tensor_copy(WT[:, g * 512:(g + 1) * 512], P[g][:, :]).then_inc(s("wt_dve"), 1)
            dve.wait_ge(s("wv_act"), 1)
            dve.tensor_tensor(WVLO[:, :], RAW[:, 2 * INNER:3 * INNER], WVHI[:, :].bitcast(f32), ALU.subtract
                              ).then_inc(s("wv_dve"), 1)
            dve.wait_ge(s("rstd_ready"), G_START + 1)
            dve_normalise(dve, 0)
            for k in range(4):
                dve.wait_ge(s("ghi_done"), k + 1)
                sel = (slice(None), slice(8 * (k // 2) + k % 2, 8 * (k // 2) + 8, 2), slice(None))
                dve.scalar_tensor_tensor(out=GLO[:, :].rearrange("p (h d) -> p h d", d=D)[sel],
                                         in0=P[k][:, :].rearrange("p (h d) -> p h d", d=D), scalar=DH ** -0.5,
                                         in1=GHI[:, :].bitcast(f32).rearrange("p (h d) -> p h d", d=D)[sel],
                                         op0=ALU.mult, op1=ALU.subtract).then_inc(s("glo_done"), 1)
            dve_operands(dve, 0)
            dve.wait_ge(s("wvo_ready"), 1)
            dve.tensor_scalar(WVO[:, :], P[4][:, 0:D], 1.0 / N, None, ALU.mult).then_inc(s("wvo_done"), 1)
            dve.wait_ge(s("cols_ready"), 1)
            dve.tensor_copy(COLS[:, :], P[6][:, 0:128]).then_inc(s("cols_done"), 1)
            dve.wait_ge(s("cols_done"), 1)
            dve.wait_ge(s("wr_loaded"), 16)
            dve.tensor_copy(WRF[:, 128:128 + E], COLS[:, 64:64 + E]).then_inc(s("cols_done"), 1)
            dve.wait_ge(s("wr_act"), 1)
            dve.tensor_tensor(WRLO[:, :], WRF[:, :], WRHI[:, :].bitcast(f32), ALU.subtract).then_inc(s("wr_split"), 1)
            dve.wait_ge(s("bcast_loaded"), BCASTS)
            dve.wait_ge(s("gate_ready"), 1)
            dve.tensor_scalar(TGBO[:, :], BC[:, 0, :], GATE[:, 0:1], None, ALU.mult).then_inc(s("wr_split"), 1)
            dve.wait_ge(s("wr_split"), 2)
            dve.wait_ge(s("mask_loaded"), 16)
            dve.wait_ge(s("x_loaded"), 16 * (CHUNKS - 1))
            dve_attention(dve, 0, True, False)
            dve.wait_ge(s("rstd_ready"), G_ATT)
            with dve.Fori(1, B - 1) as b:
                dve_attention(dve, b, False, False)
            dve_attention(dve, B - 1, False, True)
            dve_next_normalised(dve, 0, 0, G_ATT + 2)
            dve_probs(dve, B - 1, PAIRS - 1)
            dve_next_lo(dve, 0, 0)
            dve_bias(dve, B - 1)
            dve_next_route(dve, 0, 0, 0)
            dve_next_route(dve, 0, 0, 1)
            dve_tail(dve, B - 1)
            dve_next_route(dve, 0, 0, 2)
            dve_stats(dve, X, (B - 1) * QB, QB, G_ATT + B - 1, (s("tail_done"), B))
            dve_mixture(dve, 0)
            dve_decoder(dve)
            dve_mixture(dve, 1)

        @block.tensor
        def _(pe):
            pe.wait_ge(s("ident_ready"), 1)
            pe.wait_ge(s("proj_loaded"), 32)
            for g in range(6):
                if g == 4:
                    pe.wait_ge(s("wv_loaded"), 16)
                for k in range(4):
                    c = g * 512 + k * 128
                    l = pe.transpose(P[g][:, k * 128:(k + 1) * 128], RAW[:, c:c + 128], ident[:, :])
                l.then_inc(s("wt_ready"), 1)
            pe.wait_ge(s("wt_act"), 2)
            pe.wait_ge(s("wt_dve"), 2)
            for k in range(4):
                r = (k % 2) * DH
                for j in range(4):
                    c = (4 * (k // 2) + j) * 128
                    l = pe.matmul(P[k][:, j * D:(j + 1) * D], WT[r:r + DH, INNER + c:INNER + c + 128],
                                  WT[r:r + DH, c:c + 128], start=True, stop=True)
                l.then_inc(s("g_ready"), 1)
            pe.wait_ge(s("glo_done"), 1)
            pe_operands(pe, 0)
            pe.wait_ge(s("rows_loaded"), 7 * 16)
            pe.transpose(P[6][:, 0:128], ROWS[:, :], ident[:, :]).then_inc(s("cols_ready"), 1)
            pe.wait_ge(s("wo_loaded"), 16)
            pe.wait_ge(s("wt_act"), 3)
            pe.wait_ge(s("wt_dve"), 3)
            for c in range(PAIRS):
                l = pe.matmul(P[4][:, 0:D], WT[:, 2 * INNER + c * 128:2 * INNER + (c + 1) * 128], WOS[:, c, :],
                              start=c == 0, stop=c == PAIRS - 1)
            l.then_inc(s("wvo_ready"), 1)
            pe.wait_ge(s("glo_done"), 4)
            pe.wait_ge(s("wv_dve"), 1)
            pe.wait_ge(s("wvo_done"), 1)
            pe.wait_ge(s("cols_done"), 1)
            pe_attention(pe, 0, True, False)
            with pe.Fori(1, B - 1) as b:
                pe_attention(pe, b, False, False)
            pe_attention(pe, B - 1, False, True)
            pe_values(pe, B - 1, PAIRS - 2)
            pe.wait_ge(s("wr_split"), 2)
            pe_next_transposed(pe, 0, 0)
            pe_transpose_probs(pe, B - 1, PAIRS - 1)
            pe_project(pe, B - 1, PAIRS - 2)
            pe_next_logits(pe, 0, 0)
            pe_values(pe, B - 1, PAIRS - 1)
            pe_next_logits_back(pe, 0, 0)
            pe_project(pe, B - 1, PAIRS - 1)
            pe.wait_ge(s("w1lo_split"), E)
            pe.wait_ge(s("w2_loaded"), 32)
            pe.wait_ge(s("bcast_loaded"), BCASTS)
            pe_mixture(pe, 0)
            pe.wait_ge(s("l1w_loaded"), 32)
            pe_decoder(pe)
            pe.wait_ge(s("w1lo_split1"), E)
            pe_mixture(pe, 1)


_ARGS = ['x', 'ctx_1024', 'mask_BxS2_bf0', 'g_xattn', 'g_ffn', 'L0_xattn_Wq', 'L0_xattn_Wk', 'L0_xattn_Wv',
         'L0_xattn_Wo', 'L0_xattn_bo', 'L0_ffn_W1', 'L0_ffn_b1', 'L0_ffn_W2', 'L0_ffn_b2', 'L0_ffn_Wr', 'L0_ffn_br',
         'L1_xattn_w1', 'L1_xattn_b1', 'L1_xattn_w2', 'L1_xattn_b2', 'L1_xattn_g1', 'L1_xattn_beta1', 'L1_xattn_g2',
         'L1_xattn_beta2', 'L1_xattn_g3', 'L1_xattn_beta3', 'L1_ffn_gate_w', 'L1_ffn_w_gate', 'L1_ffn_w_up',
         'L1_ffn_w_down']


def kernel(**inputs):
    import numpy as np
    import concourse.bacc as bacc
    from concourse import mybir as mb
    from concourse.bass_utils import run_bass_kernel_spmd

    nc = bacc.Bacc("TRN2", target_bir_lowering=False, num_devices=1)
    arrays, args = {}, []
    for name in _ARGS:
        a = np.ascontiguousarray(inputs[name])
        arrays[f"in_{name}"] = a
        args.append(nc.dram_tensor(f"in_{name}", a.shape, mb.dt.from_np(a.dtype), kind="ExternalInput").ap())
    out = nc.dram_tensor("out_x", (B, N, D), f32, kind="ExternalOutput").ap()
    build(nc, *args, out)
    r = run_bass_kernel_spmd(nc, [arrays], core_ids=[0])
    return r.results[0]["out_x"]
```
